# Optimizing a Trainium2 kernel written in Bass

```python
import numpy as np
import jax
import jax.numpy as jnp

def _softmax(x, axis=-1):
    return jax.nn.softmax(x, axis=axis)

def _gelu(x):
    return jax.nn.gelu(x, approximate=True)

def _silu(x):
    return jax.nn.silu(x)

def _sigmoid(x):
    return jax.nn.sigmoid(x)

def _layernorm(x, axis=-1, eps=1e-05):
    m = jnp.mean(x, axis=axis, keepdims=True)
    v = jnp.var(x, axis=axis, keepdims=True)
    return (x - m) / jnp.sqrt(v + eps)

def _scatter_add(tgt, idx, src, axis=0):
    return tgt.at[idx].add(src)

def _segment_sum(src, seg, n):
    return jax.ops.segment_sum(src, seg, n)
kernel_name = 'mk_recurrent_d2_jaxref_r8_12aa4e'

def setup_inputs(seed: int=0):
    np.random.seed(seed)
    _w = jnp.asarray

    def _L0_attn_setup():
        import jax, jax.numpy as jnp
        import numpy as np
        D_MODEL = 128
        Q_HEADS = 16
        KV_HEADS = 4
        HEAD_DIM = D_MODEL // Q_HEADS
        KV_DIM = HEAD_DIM * KV_HEADS
        GROUPS = Q_HEADS // KV_HEADS
        LN_EPS = 1e-05
        NEG_INF = -10000000000.0
        key = jax.random.key(seed)
        ks = jax.random.split(key, 6)
        b, n = (2, 256)

        def xavier(k, fan_in, fan_out):
            limit = np.sqrt(6.0 / (fan_in + fan_out)).astype(np.float32)
            return jax.random.uniform(k, (fan_in, fan_out), jnp.float32, -limit, limit)
        return {'x': jax.random.normal(ks[0], (b, n, D_MODEL), jnp.float32), 'Wq': xavier(ks[1], D_MODEL, D_MODEL), 'bq': jnp.zeros((D_MODEL,), jnp.float32), 'Wk': xavier(ks[2], D_MODEL, KV_DIM), 'bk': jnp.zeros((KV_DIM,), jnp.float32), 'Wv': xavier(ks[3], D_MODEL, KV_DIM), 'bv': jnp.zeros((KV_DIM,), jnp.float32), 'ln_g': jnp.ones((D_MODEL,), jnp.float32), 'ln_b': jnp.zeros((D_MODEL,), jnp.float32), 'Wo': xavier(ks[4], D_MODEL, D_MODEL), 'bo': jnp.zeros((D_MODEL,), jnp.float32)}
    _L0_attn_in = _L0_attn_setup()

    def _L0_ffn_setup():
        import jax, jax.numpy as jnp
        import numpy as np
        B, S, D, E, H, K = (4, 256, 128, 8, 64, 2)
        key = jax.random.key(seed)
        ks = jax.random.split(key, 11)
        sc = 0.02
        return {'x': jax.random.normal(ks[0], (B, S, D), dtype=jnp.float32), 'gate_W': jax.random.normal(ks[1], (D, E), dtype=jnp.float32) * sc, 'W1': jax.random.normal(ks[2], (E, D, H), dtype=jnp.float32) * sc, 'b1': jnp.zeros((E, H), dtype=jnp.float32), 'W2': jax.random.normal(ks[3], (E, H, D), dtype=jnp.float32) * sc, 'b2': jnp.zeros((E, D), dtype=jnp.float32), 'Ws1': jax.random.normal(ks[4], (D, H), dtype=jnp.float32) * sc, 'bs1': jnp.zeros((H,), dtype=jnp.float32), 'Ws2': jax.random.normal(ks[5], (H, D), dtype=jnp.float32) * sc, 'bs2': jnp.zeros((D,), dtype=jnp.float32), 'route_scale': jnp.ones((), dtype=jnp.float32)}
    _L0_ffn_in = _L0_ffn_setup()

    def _L1_attn_setup():
        import jax, jax.numpy as jnp
        import numpy as np
        E = 128
        H = 16
        D = E // H
        B = 2
        S = 256
        YAT_EPS = 0.1
        key = jax.random.key(seed)
        ks = jax.random.split(key, 5)
        w_scale = (6.0 / (E + E)) ** 0.5

        def xavier(k):
            return jax.random.uniform(k, (E, E), jnp.float32, -w_scale, w_scale)
        return {'x': jax.random.normal(ks[0], (B, S, E), jnp.float32), 'Wq': xavier(ks[1]), 'bq': jnp.zeros((E,), jnp.float32), 'Wk': xavier(ks[2]), 'bk': jnp.zeros((E,), jnp.float32), 'Wv': xavier(ks[3]), 'bv': jnp.zeros((E,), jnp.float32), 'Wo': xavier(ks[4]), 'bo': jnp.zeros((E,), jnp.float32)}
    _L1_attn_in = _L1_attn_setup()

    def _L1_ffn_setup():
        import jax, jax.numpy as jnp
        import numpy as np
        B, S, D = (1, 256, 128)
        E, K, F = (64, 8, 96)
        SF = 96
        C = 64
        ROUTED_SCALE = 1.0

        def _moe_forward(x, router_w, w_gate, w_up, w_down, ws_gate_up, ws_down):
            T = x.shape[0]
            logits = x.astype(jnp.float32) @ router_w.T
            probs = jax.nn.softmax(logits, axis=-1)
            topk_w, topk_ids = jax.lax.top_k(probs, K)
            topk_w = topk_w / jnp.sum(topk_w, axis=-1, keepdims=True)
            topk_w = topk_w.astype(x.dtype)
            N = T * K
            flat_e = topk_ids.reshape(-1)
            flat_w = topk_w.reshape(-1)
            tok = jnp.arange(N) // K
            onehot = flat_e[:, None] == jnp.arange(E)[None, :]
            pos = jnp.cumsum(onehot, axis=0)[jnp.arange(N), flat_e] - 1
            valid = pos < C
            idx = jnp.where(valid, flat_e * C + pos, E * C)
            x_buf = jnp.zeros((E * C + 1, x.shape[1]), x.dtype).at[idx].set(x[tok])
            xb = x_buf[:E * C].reshape(E, C, -1)
            g = jnp.einsum('ecd,edf->ecf', xb, w_gate)
            u = jnp.einsum('ecd,edf->ecf', xb, w_up)
            h = jax.nn.silu(g) * u
            y = jnp.einsum('ecf,efd->ecd', h, w_down).reshape(E * C, -1)
            safe = jnp.where(valid, idx, 0)
            contrib = y[safe] * (flat_w * valid.astype(flat_w.dtype))[:, None]
            routed = jax.ops.segment_sum(contrib, tok, num_segments=T)
            routed = routed * ROUTED_SCALE
            gu = x @ ws_gate_up
            sg, su = (gu[:, :SF], gu[:, SF:])
            shared = jax.nn.silu(sg) * su @ ws_down
            return routed + shared
        key = jax.random.key(seed)
        ks = jax.random.split(key, 7)
        w = 0.02
        return {'hidden_states': jax.random.normal(ks[0], (B, S, D), jnp.float32), 'router_w': jax.random.normal(ks[1], (E, D), jnp.float32) * w, 'w_gate': jax.random.normal(ks[2], (E, D, F), jnp.float32) * w, 'w_up': jax.random.normal(ks[3], (E, D, F), jnp.float32) * w, 'w_down': jax.random.normal(ks[4], (E, F, D), jnp.float32) * w, 'ws_gate_up': jax.random.normal(ks[5], (D, 2 * SF), jnp.float32) * w, 'ws_down': jax.random.normal(ks[6], (SF, D), jnp.float32) * w}
    _L1_ffn_in = _L1_ffn_setup()
    _d = {'L0_attn_x': _L0_attn_in['x'], 'L0_attn_Wq': _L0_attn_in['Wq'], 'L0_attn_bq': _L0_attn_in['bq'], 'L0_attn_Wk': _L0_attn_in['Wk'], 'L0_attn_bk': _L0_attn_in['bk'], 'L0_attn_Wv': _L0_attn_in['Wv'], 'L0_attn_bv': _L0_attn_in['bv'], 'L0_attn_ln_g': _L0_attn_in['ln_g'], 'L0_attn_ln_b': _L0_attn_in['ln_b'], 'L0_attn_Wo': _L0_attn_in['Wo'], 'L0_attn_bo': _L0_attn_in['bo'], 'L0_ffn_gate_W': _L0_ffn_in['gate_W'], 'L0_ffn_W1': _L0_ffn_in['W1'], 'L0_ffn_b1': _L0_ffn_in['b1'], 'L0_ffn_W2': _L0_ffn_in['W2'], 'L0_ffn_b2': _L0_ffn_in['b2'], 'L0_ffn_Ws1': _L0_ffn_in['Ws1'], 'L0_ffn_bs1': _L0_ffn_in['bs1'], 'L0_ffn_Ws2': _L0_ffn_in['Ws2'], 'L0_ffn_bs2': _L0_ffn_in['bs2'], 'L0_ffn_route_scale': _L0_ffn_in['route_scale'], 'L1_attn_Wq': _L1_attn_in['Wq'], 'L1_attn_bq': _L1_attn_in['bq'], 'L1_attn_Wk': _L1_attn_in['Wk'], 'L1_attn_bk': _L1_attn_in['bk'], 'L1_attn_Wv': _L1_attn_in['Wv'], 'L1_attn_bv': _L1_attn_in['bv'], 'L1_attn_Wo': _L1_attn_in['Wo'], 'L1_attn_bo': _L1_attn_in['bo'], 'L1_ffn_router_w': _L1_ffn_in['router_w'], 'L1_ffn_w_gate': _L1_ffn_in['w_gate'], 'L1_ffn_w_up': _L1_ffn_in['w_up'], 'L1_ffn_w_down': _L1_ffn_in['w_down'], 'L1_ffn_ws_gate_up': _L1_ffn_in['ws_gate_up'], 'L1_ffn_ws_down': _L1_ffn_in['ws_down']}
    _x0 = _d['L0_attn_x']
    _d['L0_attn_x'] = jax.random.normal(jax.random.fold_in(jax.random.key(seed), 1), (1, 2048, 128), dtype=_x0.dtype)
    del _x0
    return _d

def reference(L0_attn_x, L0_attn_Wq, L0_attn_bq, L0_attn_Wk, L0_attn_bk, L0_attn_Wv, L0_attn_bv, L0_attn_ln_g, L0_attn_ln_b, L0_attn_Wo, L0_attn_bo, L0_ffn_gate_W, L0_ffn_W1, L0_ffn_b1, L0_ffn_W2, L0_ffn_b2, L0_ffn_Ws1, L0_ffn_bs1, L0_ffn_Ws2, L0_ffn_bs2, L0_ffn_route_scale, L1_attn_Wq, L1_attn_bq, L1_attn_Wk, L1_attn_bk, L1_attn_Wv, L1_attn_bv, L1_attn_Wo, L1_attn_bo, L1_ffn_router_w, L1_ffn_w_gate, L1_ffn_w_up, L1_ffn_w_down, L1_ffn_ws_gate_up, L1_ffn_ws_down):

    def _L0_attn_ref(x, Wq, bq, Wk, bk, Wv, bv, ln_g, ln_b, Wo, bo):
        import jax, jax.numpy as jnp
        import numpy as np
        D_MODEL = 128
        Q_HEADS = 16
        KV_HEADS = 4
        HEAD_DIM = D_MODEL // Q_HEADS
        KV_DIM = HEAD_DIM * KV_HEADS
        GROUPS = Q_HEADS // KV_HEADS
        LN_EPS = 1e-05
        NEG_INF = -10000000000.0
        b, n, _ = x.shape
        q = x @ Wq + bq
        k = x @ Wk + bk
        v = x @ Wv + bv
        q = q.reshape(b, n, GROUPS, KV_HEADS, HEAD_DIM)
        q = jnp.transpose(q, (0, 2, 3, 1, 4))
        k = k.reshape(b, n, KV_HEADS, HEAD_DIM)
        v = v.reshape(b, n, KV_HEADS, HEAD_DIM)
        scale = jnp.asarray(HEAD_DIM ** 0.5, q.dtype)
        q = q / scale
        attn_logits = jnp.einsum('bghnd,bmhd->bghnm', q, k)
        causal = jnp.tril(jnp.ones((n, n), dtype=bool))
        attn_logits = jnp.where(causal[None, None, None, :, :], attn_logits, NEG_INF)
        attn = jax.nn.softmax(attn_logits, axis=-1)
        out = jnp.einsum('bghnm,bmhd->bghnd', attn, v)
        out = jnp.transpose(out, (0, 3, 1, 2, 4)).reshape(b, n, D_MODEL)
        mu = jnp.mean(out, axis=-1, keepdims=True)
        var = jnp.var(out, axis=-1, keepdims=True)
        out = (out - mu) * jax.lax.rsqrt(var + LN_EPS) * ln_g + ln_b
        out = out @ Wo + bo
        return out

    def _L0_ffn_ref(x, gate_W, W1, b1, W2, b2, Ws1, bs1, Ws2, bs2, route_scale):
        import jax, jax.numpy as jnp
        import numpy as np
        B, S, D, E, H, K = (4, 256, 128, 8, 64, 2)
        scores = jax.nn.sigmoid(x @ gate_W) * route_scale
        topk_scores, topk_idx = jax.lax.top_k(scores, K)
        topk_w = topk_scores / topk_scores.sum(-1, keepdims=True)
        onehot = jax.nn.one_hot(topk_idx, E, dtype=x.dtype)
        gate_full = jnp.einsum('bsk,bske->bse', topk_w, onehot)
        h = jax.nn.gelu(jnp.einsum('bsd,edh->bseh', x, W1) + b1, approximate=False)
        y = jnp.einsum('bseh,ehd->bsed', h, W2) + b2
        expert_out = jnp.einsum('bse,bsed->bsd', gate_full, y)
        shared = jax.nn.gelu(x @ Ws1 + bs1, approximate=False) @ Ws2 + bs2
        return expert_out + shared

    def _L1_attn_ref(x, Wq, bq, Wk, bk, Wv, bv, Wo, bo):
        import jax, jax.numpy as jnp
        import numpy as np
        E = 128
        H = 16
        D = E // H
        B = 2
        S = 256
        YAT_EPS = 0.1
        b, s, _ = x.shape
        Q = x @ Wq + bq
        K = x @ Wk + bk
        V = x @ Wv + bv
        Q = Q.reshape(b, s, H, D).transpose(0, 2, 1, 3)
        K = K.reshape(b, s, H, D).transpose(0, 2, 1, 3)
        V = V.reshape(b, s, H, D).transpose(0, 2, 1, 3)
        Qn = Q / (jnp.linalg.norm(Q, axis=-1, keepdims=True) + 1e-08)
        Kn = K / (jnp.linalg.norm(K, axis=-1, keepdims=True) + 1e-08)
        dot = jnp.einsum('bhqd,bhkd->bhqk', Qn, Kn)
        scores = (1.0 + dot) ** 2 / (YAT_EPS + (1.0 - dot))
        attn = scores / (jnp.sum(scores, axis=-1, keepdims=True) + 1e-06)
        out = jnp.einsum('bhqk,bhkd->bhqd', attn, V)
        out = out.transpose(0, 2, 1, 3).reshape(b, s, E)
        return out @ Wo + bo

    def _L1_ffn_ref(hidden_states, router_w, w_gate, w_up, w_down, ws_gate_up, ws_down):
        import jax, jax.numpy as jnp
        import numpy as np
        B, S, D = (1, 256, 128)
        E, K, F = (64, 8, 96)
        SF = 96
        C = 64
        ROUTED_SCALE = 1.0

        def _moe_forward(x, router_w, w_gate, w_up, w_down, ws_gate_up, ws_down):
            T = x.shape[0]
            logits = x.astype(jnp.float32) @ router_w.T
            probs = jax.nn.softmax(logits, axis=-1)
            topk_w, topk_ids = jax.lax.top_k(probs, K)
            topk_w = topk_w / jnp.sum(topk_w, axis=-1, keepdims=True)
            topk_w = topk_w.astype(x.dtype)
            N = T * K
            flat_e = topk_ids.reshape(-1)
            flat_w = topk_w.reshape(-1)
            tok = jnp.arange(N) // K
            onehot = flat_e[:, None] == jnp.arange(E)[None, :]
            pos = jnp.cumsum(onehot, axis=0)[jnp.arange(N), flat_e] - 1
            valid = pos < C
            idx = jnp.where(valid, flat_e * C + pos, E * C)
            x_buf = jnp.zeros((E * C + 1, x.shape[1]), x.dtype).at[idx].set(x[tok])
            xb = x_buf[:E * C].reshape(E, C, -1)
            g = jnp.einsum('ecd,edf->ecf', xb, w_gate)
            u = jnp.einsum('ecd,edf->ecf', xb, w_up)
            h = jax.nn.silu(g) * u
            y = jnp.einsum('ecf,efd->ecd', h, w_down).reshape(E * C, -1)
            safe = jnp.where(valid, idx, 0)
            contrib = y[safe] * (flat_w * valid.astype(flat_w.dtype))[:, None]
            routed = jax.ops.segment_sum(contrib, tok, num_segments=T)
            routed = routed * ROUTED_SCALE
            gu = x @ ws_gate_up
            sg, su = (gu[:, :SF], gu[:, SF:])
            shared = jax.nn.silu(sg) * su @ ws_down
            return routed + shared
        b, s, d = hidden_states.shape
        x = hidden_states.reshape(-1, d)
        out = _moe_forward(x, router_w, w_gate, w_up, w_down, ws_gate_up, ws_down)
        return out.reshape(b, s, d)
    x = L0_attn_x
    xn = _layernorm(x, axis=-1)
    s = _L0_attn_ref(xn, L0_attn_Wq, L0_attn_bq, L0_attn_Wk, L0_attn_bk, L0_attn_Wv, L0_attn_bv, L0_attn_ln_g, L0_attn_ln_b, L0_attn_Wo, L0_attn_bo)
    g = _silu(_L0_ffn_ref(xn, L0_ffn_gate_W, L0_ffn_W1, L0_ffn_b1, L0_ffn_W2, L0_ffn_b2, L0_ffn_Ws1, L0_ffn_bs1, L0_ffn_Ws2, L0_ffn_bs2, L0_ffn_route_scale))
    x = x + s * g
    xn = _layernorm(x, axis=-1)
    s = _L1_attn_ref(xn, L1_attn_Wq, L1_attn_bq, L1_attn_Wk, L1_attn_bk, L1_attn_Wv, L1_attn_bv, L1_attn_Wo, L1_attn_bo)
    g = _silu(_L1_ffn_ref(xn, L1_ffn_router_w, L1_ffn_w_gate, L1_ffn_w_up, L1_ffn_w_down, L1_ffn_ws_gate_up, L1_ffn_ws_down))
    x = x + s * g
    return x

_drawn_inputs = setup_inputs


def setup_inputs(seed=0):
    import zlib

    import numpy as np

    out = dict(_drawn_inputs(seed))
    spreads = {'L0_attn_bq': (0.0, 0.8),
     'L0_attn_bk': (0.0, 2.0),
     'L0_attn_bv': (0.0, 0.1),
     'L0_attn_ln_g': (1.0, 0.6),
     'L0_attn_ln_b': (0.0, 0.8),
     'L0_attn_bo': (0.0, 0.8),
     'L0_ffn_b1': (0.0, 0.8),
     'L0_ffn_b2': (0.0, 0.1),
     'L0_ffn_bs1': (0.0, 0.8),
     'L0_ffn_bs2': (0.0, 0.1),
     'L1_attn_bq': (0.0, 2.0),
     'L1_attn_bk': (0.0, 2.0),
     'L1_attn_bv': (0.0, 0.8),
     'L1_attn_bo': (0.0, 0.8)}
    factors = {'L0_ffn_W1': 7.835,
     'L0_ffn_W2': 7.155,
     'L0_ffn_Ws1': 5.488,
     'L0_ffn_Ws2': 4.934,
     'L1_attn_Wq': 8.0,
     'L1_attn_Wk': 8.0,
     'L1_attn_Wv': 8.0,
     'L1_attn_Wo': 8.0,
     'L1_ffn_router_w': 8.0,
     'L1_ffn_w_gate': 8.0,
     'L1_ffn_w_up': 8.0,
     'L1_ffn_w_down': 8.0,
     'L1_ffn_ws_gate_up': 8.0,
     'L1_ffn_ws_down': 8.0}
    for name, (base, spread) in spreads.items():
        noise = np.random.default_rng([zlib.crc32(name.encode()), seed]).standard_normal(out[name].shape)
        drawn = base * np.exp(spread * noise) if base else spread * noise
        out[name] = jnp.asarray(drawn.astype(out[name].dtype))
    for name, factor in factors.items():
        out[name] = (out[name] * factor).astype(out[name].dtype)
    return out
```

```python
import numpy as np
import concourse.bass as bass
from concourse import mybir
from contextlib import ExitStack

FP32 = mybir.dt.float32
BF16 = mybir.dt.bfloat16
I32 = mybir.dt.int32
U32 = mybir.dt.uint32
ALU = mybir.AluOpType
ACT = mybir.ActivationFunctionType
AX = mybir.AxisListType

P = 128
T = 2048
D = 128
NT = T // P
CH = 512
NC = T // CH
TPC = CH // P
H = 16
HD = D // H
KV0 = 4
NG = 4
HPG = H // NG
VW = HD + 1
E0, F0 = 8, 64
E1, F1, TOPK, CAP = 64, 96, 8, 64
NJ = E1 // 2
JB = 4
LN_EPS = 1e-5
MASKED = -1e30
YAT_TOP = 1.1
YAT_A = 2.1 * 2.1
YAT_B = 2 * 2.1 - YAT_TOP

IN_SHAPES = {
    "x": (T, D), "Wq0": (D, D), "bq0": (1, D), "Wk0": (D, KV0 * HD), "bk0": (1, KV0 * HD),
    "Wv0": (D, KV0 * HD), "bv0": (1, KV0 * HD), "ln_g": (D, 1), "ln_b": (D, 1), "Wo0": (D, D), "bo0": (1, D),
    "gate_W": (D, E0), "W1": (D, E0 * F0), "b1": (P, E0 // 2), "W2": (P, E0 // 2 * D), "b2": (E0, D),
    "Ws1": (D, F0), "bs1": (F0, 1), "Ws2": (F0, D), "bs2": (1, D), "route_scale": (1, 1),
    "Wq1": (D, D), "bq1": (1, D), "Wk1": (D, D), "bk1": (1, D), "Wv1": (D, D), "bv1": (1, D),
    "Wo1": (D, D), "bo1": (1, D), "router": (D, E1), "w_gate": (D, E1 * F1), "w_up": (D, E1 * F1),
    "w_down": (F1, E1 * D), "ws_gate_up": (D, 2 * F1), "ws_down": (F1, D),
}


def two_layers(nc, ins, out, scratch):
    ctx = ExitStack()
    with ctx:
        def sb(name, shape, dt=FP32):
            return ctx.enter_context(nc.sbuf_tensor(name, shape, dt))

        def sem(name):
            return ctx.enter_context(nc.semaphore(name))

        bank = [ctx.enter_context(nc.psum_tensor(f"bank{i}", [P, CH], FP32)) for i in range(4)]
        pair_bank = [ctx.enter_context(nc.psum_tensor(f"pair_bank{i}", [P, 2, CH], FP32)) for i in range(2)]

        X = sb("X", [P, NT, D])
        XN = sb("XN", [P, NT, D])
        XNT = sb("XNT", [P, T])
        QFT = sb("QFT", [P, H // 2, T], BF16)
        KFT = sb("KFT", [P, H // 2, T], BF16)
        Q32 = sb("Q32", [P, NT, D])
        K32 = sb("K32", [P, NT, D])
        VA = sb("VA", [P, NT, H * VW + 32 - VW])
        WORK = sb("WORK", [P, 2, HPG * 2 * CH])
        SG = sb("SG", [P, NT, D])
        AO = Q32
        ident = sb("ident", [P, P])
        identb = sb("identb", [P, P], BF16)
        mask_qk = sb("mask_qk", [P, P], BF16)
        mask_kq = sb("mask_kq", [P, P], BF16)
        block_mask = sb("block_mask", [P, H, 1])
        ones = sb("ones", [1, CH])
        ones_col = sb("ones_col", [P, 1])
        iota = sb("iota", [P, T])
        st = sb("st", [P, NT, 6])
        mv = sb("mv", [P, NT, 2])
        nrm = sb("nrm", [P, 4, NT * H * 2])
        OT = nrm[:, 0:2, :]
        small = sb("small", [P, 16, 24])

        wqkv0 = sb("wqkv0", [D, D + 2 * KV0 * HD])
        bqkv0 = sb("bqkv0", [1, D + 2 * KV0 * HD])
        wqkv1 = sb("wqkv1", [D, 3 * D])
        bqkv1 = sb("bqkv1", [1, 3 * D])
        ln_g, ln_b = sb("ln_g", [D, 1]), sb("ln_b", [D, 1])
        wo = [sb(f"wo{i}", [D, D]) for i in range(2)]
        bo = [sb(f"bo{i}", [1, D]) for i in range(2)]
        gate_w = sb("gate_w", [D, E0])
        w1, b1 = sb("w1", [D, E0 * F0]), sb("b1", [P, E0 // 2])
        w2, b2 = sb("w2", [P, E0 // 2, D]), sb("b2", [E0, D])
        ws1, bs1 = sb("ws1", [D, F0]), sb("bs1", [F0, 1])
        ws2, bs2 = sb("ws2", [F0, D]), sb("bs2", [1, D])
        rscale = sb("rscale", [P, 1])
        router = sb("router", [D, E1])
        wsgu, wsd = sb("wsgu", [D, 2 * F1]), sb("wsd", [F1, D])
        wgu = [sb("wgu", [D, 2, 2, JB, F1])[:],
               SG[:, JB:NT, :].rearrange("p t n -> p (t n)").rearrange("p (w h j f) -> p w h j f", w=2, h=2, j=JB)]
        wdn = Q32[:].rearrange("p t n -> p (t n)")[0:F1, :].rearrange("p (b h j n) -> p b h j n", b=2, h=2, j=JB)

        work = WORK[:, :, :].rearrange("p a b -> p (a b)")
        workb = work.bitcast(BF16)
        QF = workb[:, 0:8192].rearrange("p (b t n) -> p b t n", b=2, t=TPC)
        KF = workb[:, 8192:16384].rearrange("p (b t n) -> p b t n", b=2, t=TPC)
        HT = work[:, 0:2 * 5 * CH].rearrange("p (b m n) -> p b m n", b=2, m=5)
        MF = sb("MF", [P, TPC, 2, P], BF16)
        MX = sb("MX", [P, 2, HPG * TPC, NC])
        gates = sb("gates", [P, NT, E0 + 6])
        gatew = sb("gatew", [P, NT, E0])
        gateT = work[0:E0, 2 * 5 * CH:2 * 5 * CH + T]
        gsel = sb("gsel", [E0, E0 // 2, P])
        gblk = sb("gblk", [P, H, 32])
        crow = sb("crow", [1, H, 32])
        QNT = XNT
        LG = Q32[:, :, 0:E1]
        RP = Q32[:, :, E1:2 * E1]
        MK = K32[:, :, 0:E1]
        EX = K32[:, :, E1:2 * E1]
        MX8 = sb("MX8", [P, NT, 8])
        SC = work[0:E1, 0:T]
        IOD = work[0:E1, T:2 * T]
        TK = sb("TK", [E1, CAP])
        TOK = sb("TOK", [P, NJ])
        IDX = sb("IDX", [P, NJ], I32)
        WS = sb("WS", [P, NJ])
        GX = work[:, 0:NJ * (D + E1)].rearrange("p (j n) -> p j n", j=NJ)
        XBT = KFT[:, :, :].rearrange("p a b -> p (a b)").bitcast(FP32)[:, 0:NJ * P].rearrange("p (j n) -> p j n", j=NJ)
        YS = QFT[:, :, :].rearrange("p a b -> p (a b)")[:, 0:NJ * 3 * D].rearrange("p (k j n) -> p k j n", k=3, j=NJ)
        HH = XN[:].rearrange("p t n -> p (t n)")[0:F1, :].rearrange("p (b n) -> p b n", b=4)
        SHH = K32
        OH = KFT[:, :, :].rearrange("p a b -> p (a b)")[:, NJ * P * 2:NJ * P * 4].rearrange("p (b j n) -> p b j n", b=2, j=NJ)

        def sems(*names):
            return {n: sem(n) for n in names}

        S = sems(
            "x_in", "weights_in", "consts", "consts0", "dve_step", "pool_step", "out_stored",
            "moe_rows_out", "gathered", "moe_w_in")
        x_in = [sem(f"x_in{c}") for c in range(NC)]
        w_in = [sem(f"w_in{c}") for c in range(2)]
        gath = [sem(f"gath{c}") for c in range(4)]
        L = [
            {n: sem(f"l{i}_{n}") for n in (
                "var_ready", "std_ready", "xn_ready", "xnT_psum", "xnT_ready", "proj_psum", "even_evac", "odd_evac",
                "staged", "dup_staged", "featT_psum", "qfeat_evac", "kfeat_evac",
                "scores", "probs", "sums", "sums_evac", "sumsT", "ao_ready", "lnT_psum", "lnT_ready",
                "y_psum", "y_used", "x_done")}
            for i in range(2)]
        F = sems("gates_psum", "sig_ready", "gates_ready", "gateT_psum", "gateT_ready", "h_psum", "h_act",
                 "gsel_psum", "h_gated", "ffn_psum", "ffn_silu")
        M = sems("max_scores", "max_done", "minus_max", "mT_psum", "m_rows_a", "m_rows_b")
        R = sems("logits_psum", "logits_evac", "shifted", "exp_ready", "route_ready", "maskT_psum", "score_ready",
                 "slots_ready", "slotT_psum", "idx_ready", "xbT_psum", "xbT_ready", "gu_psum", "silu_ready",
                 "h_ready", "y_psum", "y_split", "onehot", "sh_psum", "sh_silu", "sh_ready", "z_psum", "z_silu")
        N1 = sems("qk_sq", "qk_norm", "qk_scaled", "qnT_psum", "qnT_ready", "g_psum", "g_ready")

        x_rows = ins["x"].rearrange("(t p) d -> p t d", p=P)
        out_rows = out.rearrange("(t p) d -> p t d", p=P)
        scratch_rows = scratch.rearrange("(t p) n -> p t n", p=P)
        wg_v = ins["w_gate"].rearrange("d (h j f) -> d h j f", h=2, j=NJ)
        wu_v = ins["w_up"].rearrange("d (h j f) -> d h j f", h=2, j=NJ)
        wd_v = ins["w_down"].rearrange("f (h j d) -> f h j d", h=2, j=NJ)
        NJB = NJ // JB

        WEIGHTS = [
            (wqkv0[:, 0:D], ins["Wq0"]), (wqkv0[:, D:D + 32], ins["Wk0"]), (wqkv0[:, D + 32:D + 64], ins["Wv0"]),
            (bqkv0[:, 0:D], ins["bq0"]), (bqkv0[:, D:D + 32], ins["bk0"]), (bqkv0[:, D + 32:D + 64], ins["bv0"]),
            (gate_w[:], ins["gate_W"]), (rscale[:], ins["route_scale"].to_broadcast([P, 1])),
            (w1[:], ins["W1"]), (b1[:], ins["b1"]), (w2[:].rearrange("p m d -> p (m d)"), ins["W2"]), (b2[:], ins["b2"]),
            (ws1[:], ins["Ws1"]), (bs1[:], ins["bs1"]), (ws2[:], ins["Ws2"]), (bs2[:], ins["bs2"]),
            (ln_g[:], ins["ln_g"]), (ln_b[:], ins["ln_b"]), (wo[0][:], ins["Wo0"]), (bo[0][:], ins["bo0"]),
            (wqkv1[:, 0:D], ins["Wq1"]), (wqkv1[:, D:2 * D], ins["Wk1"]), (wqkv1[:, 2 * D:3 * D], ins["Wv1"]),
            (bqkv1[:, 0:D], ins["bq1"]), (bqkv1[:, D:2 * D], ins["bk1"]), (bqkv1[:, 2 * D:3 * D], ins["bv1"]),
            (wo[1][:], ins["Wo1"]), (bo[1][:], ins["bo1"]), (router[:], ins["router"]),
            (wsgu[:], ins["ws_gate_up"]), (wsd[:], ins["ws_down"]),
        ]
        ALL_WEIGHTS = 16 * len(WEIGHTS)

        STEPS = [(c, g) for c in range(NC) for g in range(NG)]

        def causal_units(c):
            full = [[(2 * m, 0, CH), (2 * m + 1, CH, CH)] for m in range(TPC * c // 2)]
            b = TPC * c
            return full + [[(b, 0, CH), (b + 1, CH, CH - P), (b + 3, 2 * CH - P, P)], [(b + 2, 0, CH - 2 * P)]]

        def yat_units(c):
            return [[(2 * m, 0, CH), (2 * m + 1, CH, CH)] for m in range(NT // 2)]

        UNITS = [causal_units, yat_units]
        KSTEPS = [[(n, k) for n, (c, g) in enumerate(STEPS) for k in range(len(UNITS[l](c)))] for l in range(2)]
        width_of = lambda unit: unit[-1][1] + unit[-1][2]
        N_KSTEPS = [len(k) for k in KSTEPS]

        def scores(l, ks):
            return HPG * ks

        MAXIMA = [[(hd, i, kc) for hd in range(HPG) for i in range(TPC) for kc in range(c + 1)] for c, g in STEPS]
        MAX_BASE = np.cumsum([0] + [len(m) for m in MAXIMA]).tolist()

        def max_slot(n, slot):
            total, slots = len(MAXIMA[n + 1]), HPG * (len(UNITS[0](STEPS[n][0])) - 1)
            return slot * total // slots, (slot + 1) * total // slots

        block = ctx.enter_context(nc.Block())

        @block.sync
        def _(sp):
            for c in range(NC):
                sp.dma_start(X[:, c * TPC:(c + 1) * TPC, :], x_rows[:, c * TPC:(c + 1) * TPC, :]).then_inc(x_in[c], 16)
            for dst, src in WEIGHTS:
                sp.dma_start(dst, src).then_inc(S["weights_in"], 16)
            sp.wait_ge(L[1]["xn_ready"], NC)
            sp.dma_start(scratch_rows[:, :, 0:D], XN[:, :, :]).then_inc(S["moe_rows_out"], 16)
            sp.wait_ge(R["route_ready"], 1)
            sp.dma_start(scratch_rows[:, :, D:D + E1], EX).then_inc(S["moe_rows_out"], 16)
            for b in range(NJB):
                if b >= 2:
                    sp.wait_ge(R["y_psum"], b - 1)
                for h in range(2):
                    sp.dma_start(wgu[b % 2][:, 0, h], wg_v[:, h, b * JB:(b + 1) * JB, :]).then_inc(w_in[b % 2], 16)
                    sp.dma_start(wgu[b % 2][:, 1, h], wu_v[:, h, b * JB:(b + 1) * JB, :]).then_inc(w_in[b % 2], 16)
                    sp.dma_start(wdn[:, b % 2, h], wd_v[:, h, b * JB:(b + 1) * JB, :]).then_inc(w_in[b % 2], 16)
            for c in range(NC):
                sp.wait_ge(L[1]["x_done"], c + 1)
                sp.dma_start(out_rows[:, c * TPC:(c + 1) * TPC, :], X[:, c * TPC:(c + 1) * TPC, :]).then_inc(S["out_stored"], 16)
            sp.wait_ge(S["out_stored"], 16 * NC)

        @block.gpsimd
        def _(pool):
            n_pool = [0]

            def step(ins_):
                n_pool[0] += 1
                ins_.then_inc(S["pool_step"], 1)
                pool.wait_ge(S["pool_step"], n_pool[0])

            pool.memset(ident[:], 0.0)
            pool.memset(identb[:], 0.0)
            pool.memset(mask_qk[:], 0.0)
            pool.memset(mask_kq[:], 0.0)
            pool.memset(ones[:], 1.0)
            pool.memset(ones_col[:], 1.0)
            pool.memset(gsel[:], 0.0)
            pool.memset(gates[:], -1e30)
            pool.memset(MF[:], 0.0)
            pool.memset(block_mask[:], -1.0)
            pool.memset(gblk[:], 0.0)
            pool.memset(crow[:], 0.0)
            pool.iota(iota[:], pattern=[[1, T]], base=0, channel_multiplier=0, allow_small_or_imprecise_dtypes=True)
            step(pool.memset(VA[:], 1.0))
            for m in (ident, identb):
                pool.affine_select(out=m[:], in_=m[:], compare_op=ALU.not_equal, fill=1.0, base=0,
                                   pattern=[[-1, P]], channel_multiplier=1)
            pool.affine_select(out=mask_qk[:], in_=mask_qk[:], compare_op=ALU.is_ge, fill=MASKED, base=0,
                               pattern=[[-1, P]], channel_multiplier=1)
            pool.affine_select(out=mask_kq[:], in_=mask_kq[:], compare_op=ALU.is_ge, fill=MASKED, base=0,
                               pattern=[[1, P]], channel_multiplier=-1)
            step(pool.affine_select(out=block_mask[:, :, 0], in_=block_mask[:, :, 0], compare_op=ALU.is_ge, fill=0.0,
                                    base=0, pattern=[[-HD, H]], channel_multiplier=1))
            pool.affine_select(out=block_mask[:, :, 0], in_=block_mask[:, :, 0], compare_op=ALU.is_ge, fill=0.0,
                               base=HD - 1, pattern=[[HD, H]], channel_multiplier=-1)
            gs = gsel[:].rearrange("e m (h r) -> e (m h) r", h=2)
            pool.affine_select(out=gs, in_=gs, compare_op=ALU.not_equal, fill=1.0, base=0,
                               pattern=[[-1, E0], [0, F0]], channel_multiplier=1).then_inc(S["consts"], 1)

            def init_stage(l):
                if l == 0:
                    pool.wait_ge(F["ffn_psum"], NT)
                else:
                    pool.wait_ge(R["z_psum"], NT)
                step(pool.memset(work, 0.0))
                qv = QF.rearrange("p b t (h n) -> p (b t h) n", n=64)
                nk = H if l else KV0
                if l == 0:
                    for b in range(2):
                        last = pool.memset(KF[:, b, :, 0:nk * 64].rearrange("p t (h n) -> p t h n", n=64)[:, :, :, 0:2], 1.0)
                else:
                    kall = KF.rearrange("p b t (h n) -> p (b t h) n", n=64)
                    pool.memset(kall[:, :, 0:3], 1.0)
                    parts, rest = [], np.float32(YAT_TOP)
                    for _ in range(3):
                        bits = np.frombuffer(np.float32(rest).tobytes(), np.uint32)[0]
                        part = np.frombuffer(np.uint32(bits & 0xFFFF0000).tobytes(), np.float32)[0]
                        parts.append(float(part))
                        rest = np.float32(rest - part)
                    for i, v in enumerate(parts):
                        last = pool.memset(qv[:, :, i:i + 1], v)
                last.then_inc(L[l]["dup_staged"], 1)

            def duplicates(l):
                nk = H if l else KV0
                for c in range(NC):
                    pool.wait_ge(L[l]["staged"], c + 1)
                    q = QF[:, c % 2].rearrange("p t (h n) -> p (t h) n", n=64)
                    pool.tensor_copy(q[:, :, 16:24], q[:, :, 8:16])
                    pool.tensor_copy(q[:, :, 32:40], q[:, :, 8:16])
                    pool.tensor_copy(q[:, :, 48:56], q[:, :, 24:32])
                    k = KF[:, c % 2, :, 0:nk * 64].rearrange("p t (h n) -> p t h n", n=64)
                    pool.tensor_copy(k[:, :, :, 24:32], k[:, :, :, 8:16])
                    pool.tensor_copy(k[:, :, :, 40:48], k[:, :, :, 8:16])
                    pool.tensor_copy(k[:, :, :, 48:56], k[:, :, :, 16:24]).then_inc(L[l]["dup_staged"], 1)

            init_stage(0)
            duplicates(0)

            pool.wait_ge(R["idx_ready"], 1)
            pool.wait_ge(S["moe_rows_out"], 32)
            for j in range(NJ):
                pool.indirect_dma_start(
                    out=GX[:, j, :], out_offset=None, in_=scratch[:, :],
                    in_offset=bass.IndirectOffsetOnAxis(ap=IDX[:, j:j + 1].bitcast(U32), axis=0),
                ).then_inc(gath[j // (NJ // 4)], 16)
            init_stage(1)
            duplicates(1)

        @block.scalar
        def _(act):
            def norm(l):
                act.wait_ge(L[l]["var_ready"], 1)
                act.activation(nrm[:, 1, 0:NT], nrm[:, 0, 0:NT], ACT.Sqrt).then_inc(L[l]["std_ready"], 1)
                for c in range(NC):
                    act.wait_ge(L[l]["xnT_psum"], c + 1)
                    act.copy(XNT[:, c * CH:(c + 1) * CH], bank[c % 2][:]).then_inc(L[l]["xnT_ready"], 1)

            def evacuate_even(l, scale, nk):
                for t in range(0, NT, 2):
                    src = bank[0]
                    act.wait_ge(L[l]["proj_psum"], t + 1)
                    act.activation(Q32[:, t, :], src[:, 0:D], ACT.Copy, scale=scale)
                    act.copy(K32[:, t, 0:nk * HD], src[:, D:D + nk * HD])
                    act.copy(VA[:, t, 0:nk * VW].rearrange("p (h n) -> p h n", n=VW)[:, :, 0:HD],
                             src[:, D + nk * HD:D + 2 * nk * HD].rearrange("p (h n) -> p h n", n=HD)).then_inc(L[l]["even_evac"], 1)

            def evacuate_features(l):
                for t in range(NT):
                    act.wait_ge(L[l]["featT_psum"], t + 1)
                    src = pair_bank[t % 2][:, 0, :].bitcast(BF16).rearrange("p (a n) -> p a n", n=P)
                    act.copy(QFT[:, :, t * P:(t + 1) * P], src).then_inc(L[l]["qfeat_evac"], 1)

            norm(0)
            evacuate_even(0, float(HD) ** -0.5, KV0)

            act.wait_ge(F["gates_psum"], 1)
            act.activation(gates[:, :, 0:E0], bank[2][:, 0:NT * E0].rearrange("p (t e) -> p t e", e=E0),
                           ACT.Sigmoid).then_inc(F["sig_ready"], 1)
            act.wait_ge(F["gateT_psum"], 1)
            for c in range(NC):
                act.wait_ge(F["gateT_psum"], c + 1)
                act.copy(gateT[:, c * CH:(c + 1) * CH], bank[c % 2][0:E0, :]).then_inc(F["gateT_ready"], 1)
            def ffn_out(c):
                for t in range(c * TPC, (c + 1) * TPC):
                    act.wait_ge(F["ffn_psum"], t + 1)
                    act.copy(SG[:, t, :], pair_bank[t % 2][:, 0, 0:D]).then_inc(F["ffn_silu"], 1)

            for c in range(NC):
                for m in range(5):
                    rows = P if m < 4 else F0
                    act.wait_ge(F["h_psum"], 5 * c + m + 1)
                    if c >= 2 and m == 0:
                        act.wait_ge(F["ffn_psum"], TPC * (c - 1))
                    act.activation(HT[0:rows, c % 2, m, :], bank[(5 * c + m) % 2][0:rows, :], ACT.Gelu,
                                   bias=b1[:, m:m + 1] if m < 4 else bs1[:]).then_inc(F["h_act"], 1)
                if c >= 1:
                    ffn_out(c - 1)
            ffn_out(NC - 1)

            evacuate_features(0)

            act.preload_act_table_set("natural_log_exp_and_others")

            def m_rows(n):
                c, g = STEPS[n]
                act.wait_ge(M["mT_psum"], n + 1)
                src = bank[3][:, :].bitcast(BF16).rearrange("p (a n) -> p a n", n=CH)
                act.copy(QFT[0:2, 2 * g:2 * g + 2, c * CH:(c + 1) * CH], src[0:2]).then_inc(M["m_rows_a"], 1)

            m_rows(0)
            for ks, (n, k) in enumerate(KSTEPS[0]):
                c, g = STEPS[n]
                w = width_of(UNITS[0](c)[k])
                for hd in range(HPG):
                    if hd == 3 and k == len(UNITS[0](c)) - 1 and n + 1 < len(STEPS):
                        m_rows(n + 1)
                    u = HPG * ks + hd
                    act.wait_ge(L[0]["scores"], u + 1)
                    if ks >= 2 and hd == 0:
                        act.wait_ge(L[0]["sums"], ks - 1)
                    act.activation(WORK[:, ks % 2, hd * 2 * CH:hd * 2 * CH + w],
                                   pair_bank[u % 2][:].rearrange("p a b -> p (a b)")[:, 0:w],
                                   ACT.Exp).then_inc(L[0]["probs"], 1)

            def end_layer(l):
                for c in range(NC):
                    act.wait_ge(L[l]["lnT_psum"], c + 1)
                    if l == 0:
                        act.activation(XNT[:, c * CH:(c + 1) * CH], bank[c % 2][:], ACT.Identity, bias=ln_b[:],
                                       scale=ln_g[:]).then_inc(L[l]["lnT_ready"], 1)
                    else:
                        act.copy(XNT[:, c * CH:(c + 1) * CH], bank[c % 2][:]).then_inc(L[l]["lnT_ready"], 1)

            act.wait_ge(L[0]["ao_ready"], len(STEPS))
            act.activation(SG[:], SG[:], ACT.Silu).then_inc(F["ffn_silu"], 1)
            act.wait_ge(L[0]["ao_ready"], len(STEPS) + 1)
            act.activation(nrm[:, 1, 0:NT], nrm[:, 0, 0:NT], ACT.Sqrt).then_inc(L[0]["std_ready"], 1)
            end_layer(0)

            norm(1)
            for b in range(2):
                act.wait_ge(R["logits_psum"], b + 1)
                act.copy(LG[:, 8 * b:8 * b + 8, :], bank[b][:].rearrange("p (t e) -> p t e", e=E1)).then_inc(R["logits_evac"], 1)
            act.wait_ge(R["shifted"], 1)
            act.activation(EX, EX, ACT.Exp).then_inc(R["exp_ready"], 1)
            for b in range(NJB):
                act.wait_ge(R["xbT_psum"], b + 1)
                act.copy(XBT[:, b * JB:(b + 1) * JB, :].rearrange("p j n -> p (j n)"), bank[b % 2][:]).then_inc(R["xbT_ready"], 1)
            for b in range(NJB):
                act.wait_ge(R["gu_psum"], b + 1)
                if b >= 2:
                    act.wait_ge(R["h_ready"], b - 1)
                act.activation(HH[:, b % 2, :], pair_bank[b % 2][0:F1, 0, :], ACT.Silu).then_inc(R["silu_ready"], 1)
            for c in range(NC):
                act.wait_ge(R["sh_psum"], c + 1)
                if c >= 2:
                    act.wait_ge(R["sh_ready"], c - 1)
                act.activation(HH[:, c % 2, :], pair_bank[c % 2][0:F1, 0, :], ACT.Silu).then_inc(R["sh_silu"], 1)
            for t in range(NT):
                act.wait_ge(R["z_psum"], t + 1)
                act.activation(SG[:, t, :], bank[t % 2][:, 0:D], ACT.Silu).then_inc(R["z_silu"], 1)
            evacuate_even(1, 1.0, H)
            act.wait_ge(N1["qk_sq"], 1)
            act.activation(nrm[:, 1, :], nrm[:, 0, :], ACT.Sqrt).then_inc(N1["qk_norm"], 1)
            for c in range(NC):
                act.wait_ge(N1["qnT_psum"], c + 1)
                act.copy(QNT[:, c * CH:(c + 1) * CH], bank[c % 2][:]).then_inc(N1["qnT_ready"], 1)
            evacuate_features(1)
            act.preload_act_table_set("natural_log_exp_and_others")
            for ks, (n, k) in enumerate(KSTEPS[1]):
                for hd in range(HPG):
                    u = HPG * ks + hd
                    act.wait_ge(L[1]["scores"], u + 1)
                    if ks >= 2 and hd == 0:
                        act.wait_ge(L[1]["sums"], ks - 1)
                    last = act.activation(WORK[:, ks % 2, hd * 2 * CH:(hd + 1) * 2 * CH],
                                          pair_bank[u % 2][:].rearrange("p a b -> p (a b)"), ACT.Ln, scale=1.0 / YAT_A)
                    last.then_inc(L[1]["probs"], 1)
                act.wait_ge(L[1]["probs"], 5 * ks + 4)
                act.activation(WORK[:, ks % 2, :], WORK[:, ks % 2, :], ACT.Exp, scale=-1.0).then_inc(L[1]["probs"], 1)
            end_layer(1)

        @block.vector
        def _(dve):
            n_dve = [0]

            def step(ins_):
                n_dve[0] += 1
                ins_.then_inc(S["dve_step"], 1)
                dve.wait_ge(S["dve_step"], n_dve[0])

            def inverse_std(l, ready_sem, ready_value, first):
                n = NT
                dve.wait_ge(ready_sem, ready_value)
                refine(n, 0.0)

            def refine(n, add):
                v, s, r, y = (nrm[:, i, 0:n] for i in range(4))
                step(dve.tensor_scalar(s, s, 1e-30, None, ALU.max))
                step(dve.reciprocal(r, s))
                step(dve.tensor_tensor(y, v, r, ALU.mult))
                step(dve.tensor_tensor(y, y, s, ALU.add))
                step(dve.tensor_scalar(y, y, 0.5, add, ALU.mult, ALU.add))
                step(dve.reciprocal(y, y))

            def stats(src, l, c):
                for t in range(c * TPC, (c + 1) * TPC):
                    last = dve.bn_stats(st[:, t, :], src[:, t, :])
                step(last)
                for t in range(c * TPC, (c + 1) * TPC):
                    last = dve.bn_aggr(mv[:, t, :], st[:, t, :])
                step(last)

            def layernorm(l, src, dst, var_sem, std_wait, done_sem):
                step(dve.tensor_scalar(nrm[:, 0, 0:NT], mv[:, :, 1], LN_EPS, None, ALU.add))
                dve.sem_inc(var_sem, 1)
                dve.wait_ge(L[l]["std_ready"], std_wait)
                refine(NT, 0.0)
                for t in range(NT):
                    last = dve.tensor_scalar(dst[:, t, :], src[:, t, :], mv[:, t, 0:1], nrm[:, 3, t:t + 1],
                                             ALU.subtract, ALU.mult)
                    if t % TPC == TPC - 1:
                        last.then_inc(done_sem, 1)

            def evacuate_odd(l, scale, nk):
                for t in range(1, NT, 2):
                    src = bank[1]
                    dve.wait_ge(L[l]["proj_psum"], t + 1)
                    dve.tensor_scalar(Q32[:, t, :], src[:, 0:D], scale, None, ALU.mult)
                    dve.tensor_copy(K32[:, t, 0:nk * HD], src[:, D:D + nk * HD])
                    dve.tensor_copy(VA[:, t, 0:nk * VW].rearrange("p (h n) -> p h n", n=VW)[:, :, 0:HD],
                                    src[:, D + nk * HD:D + 2 * nk * HD].rearrange("p (h n) -> p h n", n=HD)).then_inc(L[l]["odd_evac"], 1)

            def split_features(l, nk):
                dve.wait_ge(L[l]["even_evac"], NT // 2)
                dve.wait_ge(L[l]["odd_evac"], NT // 2)
                for c in range(NC):
                    ts = slice(c * TPC, (c + 1) * TPC)
                    dve.wait_ge(L[l]["dup_staged"], 1)
                    if c >= 2:
                        dve.wait_ge(L[l]["featT_psum"], TPC * (c - 1))
                    q = QF[:, c % 2].rearrange("p t (h n) -> p (t h) n", n=64)
                    k = KF[:, c % 2, :, 0:nk * 64].rearrange("p t (h n) -> p t h n", n=64)
                    qs = Q32[:, ts, :].rearrange("p t (h n) -> p (t h) n", n=HD)
                    ks = K32[:, ts, 0:nk * HD].rearrange("p t (h n) -> p t h n", n=HD)
                    qr, kr = qs, ks
                    for part, (qa, ka) in enumerate(((8, 8), (24, 16), (40, 32))):
                        dve.tensor_copy(q[:, :, qa:qa + 8], qr)
                        last = dve.tensor_copy(k[:, :, :, ka:ka + 8], kr)
                        if part == 2:
                            break
                        step(last)
                        dve.tensor_tensor(qs, qr, q[:, :, qa:qa + 8], ALU.subtract)
                        step(dve.tensor_tensor(ks, kr, k[:, :, :, ka:ka + 8], ALU.subtract))
                    last.then_inc(L[l]["staged"], 1)
                    if c >= 1:
                        evacuate_kfeatures(l, nk, c - 1)
                evacuate_kfeatures(l, nk, NC - 1)

            def evacuate_kfeatures(l, nk, c):
                for t in range(c * TPC, (c + 1) * TPC):
                    dve.wait_ge(L[l]["featT_psum"], t + 1)
                    src = pair_bank[t % 2][:, 1, :].bitcast(BF16)[:, 0:nk * 64].rearrange("p (a n) -> p a n", n=P)
                    dve.tensor_copy(KFT[:, 0:nk // 2, t * P:(t + 1) * P], src).then_inc(L[l]["kfeat_evac"], 1)

            for c in range(NC):
                dve.wait_ge(x_in[c], 16)
                stats(X, 0, c)
            layernorm(0, X, XN, L[0]["var_ready"], 1, L[0]["xn_ready"])
            dve.wait_ge(S["consts"], 1)
            evacuate_odd(0, float(HD) ** -0.5, KV0)

            dve.wait_ge(F["sig_ready"], 1)
            dve.wait_ge(S["weights_in"], ALL_WEIGHTS)
            step(dve.tensor_scalar(gates[:, :, 0:E0], gates[:, :, 0:E0], rscale[:], None, ALU.mult))
            for t in range(NT):
                last = dve.max(MX8[:, t, :], gates[:, t, 0:E0])
            step(last)
            step(dve.tensor_tensor(nrm[:, 0, 0:NT], MX8[:, :, 0], MX8[:, :, 1], ALU.add))
            step(dve.reciprocal(nrm[:, 1, 0:NT], nrm[:, 0, 0:NT]))
            step(dve.memset(MX8[:, :, 2:8], -1e30))
            for t in range(NT):
                last = dve.match_replace(small[:, t, 0:E0 + 6], MX8[:, t, :], gates[:, t, :], 2e30)
            step(last)
            step(dve.tensor_scalar(small[:, :, 16:24], small[:, :, 0:E0], 1e30, None, ALU.is_gt))
            step(dve.tensor_tensor(small[:, :, 16:24], small[:, :, 16:24], gates[:, :, 0:E0], ALU.mult))
            dve.tensor_tensor(gatew[:], small[:, :, 16:24],
                              nrm[:, 1, 0:NT].unsqueeze(2).to_broadcast([P, NT, E0]), ALU.mult).then_inc(F["gates_ready"], 1)
            for c in range(NC):
                for m in range(4):
                    i = 4 * c + m
                    dve.wait_ge(F["h_act"], 5 * c + m + 1)
                    dve.wait_ge(F["gsel_psum"], i + 1)
                    dve.tensor_tensor(HT[:, c % 2, m, :], HT[:, c % 2, m, :], bank[2 + i % 2][:], ALU.mult).then_inc(F["h_gated"], 1)

            split_features(0, KV0)

            def maxima(n, lo, hi):
                for i in range(lo, hi):
                    hd, qt, kc = MAXIMA[n][i]
                    c, g = STEPS[n]
                    w = CH if kc < c else (qt + 1) * P
                    u = MAX_BASE[n] + i
                    dve.wait_ge(M["max_scores"], u + 1)
                    dve.reduce_max(MX[:, n % 2, hd * TPC + qt, kc:kc + 1], bank[u % 2][:, 0:w], AX.X).then_inc(M["max_done"], 1)

            def minus_max(n):
                c, g = STEPS[n]
                dve.wait_ge(M["max_done"], MAX_BASE[n + 1])
                m32 = small[:, 0, 0:16]
                m3 = m32.rearrange("p (a b) -> p a b", a=HPG)
                step(dve.tensor_reduce(m32, MX[:, n % 2, :, 0:c + 1], axis=AX.X, op=ALU.max))
                step(dve.tensor_scalar(m32, m32, -1.0, None, ALU.mult))
                if n >= 1:
                    dve.wait_ge(M["mT_psum"], n)
                hi = MF[:].rearrange("p t a (e n) -> p (a e) t n", n=64)
                step(dve.tensor_copy(hi[:, :, :, 0], m3))
                dve.tensor_tensor(hi[:, :, :, 1], m3, hi[:, :, :, 0], ALU.subtract).then_inc(M["minus_max"], 1)
                dve.wait_ge(M["mT_psum"], n + 1)
                src = bank[3][:, :].bitcast(BF16).rearrange("p (a n) -> p a n", n=CH)
                dve.tensor_copy(QFT[64:66, 2 * g:2 * g + 2, c * CH:(c + 1) * CH], src[64:66]).then_inc(M["m_rows_b"], 1)

            def evacuate_sums(l, n):
                dve.wait_ge(L[l]["sums"], sum(1 for m, _ in KSTEPS[l] if m <= n))
                if n >= 2:
                    dve.wait_ge(L[l]["sumsT"], n - 1)
                dve.tensor_copy(OT[:, n % 2, :], bank[2][:]).then_inc(L[l]["sums_evac"], 1)

            def normalize(l, n):
                c, g = STEPS[n]
                dve.wait_ge(L[l]["sumsT"], n + 1)
                src = bank[3][:].rearrange("p (t h n) -> p t h n", t=TPC, n=32)
                den = small[:, 1, 0:16].rearrange("p (t h) -> p t h", t=TPC)
                if l == 0:
                    step(dve.reciprocal(den, src[:, :, :, HD]))
                else:
                    step(dve.tensor_scalar(den, src[:, :, :, HD], 1e-6, None, ALU.add))
                    step(dve.reciprocal(den, den))
                dst = AO[:, c * TPC:(c + 1) * TPC, g * 32:(g + 1) * 32].rearrange("p t (h n) -> p t h n", n=HD)
                dve.tensor_tensor(dst, src[:, :, :, 0:HD], den.unsqueeze(3).to_broadcast([P, TPC, HPG, HD]),
                                  ALU.mult).then_inc(L[l]["ao_ready"], 1)

            maxima(0, 0, len(MAXIMA[0]))
            minus_max(0)
            for n in range(len(STEPS) + 1):
                more = n + 1 < len(STEPS)
                if more:
                    maxima(n + 1, 0, max_slot(n, 3)[0])
                if n >= 1:
                    evacuate_sums(0, n - 1)
                if more:
                    maxima(n + 1, *max_slot(n, 3))
                if n >= 1:
                    normalize(0, n - 1)
                if more:
                    maxima(n + 1, max_slot(n, 3)[1], len(MAXIMA[n + 1]))
                    minus_max(n + 1)

            def add_branches(l, stride):
                for t in range(NT):
                    dve.wait_ge(L[l]["y_psum"], t + 1)
                    dve.tensor_tensor(AO[:, t, :], bank[2 + t % 2][:, 0:D], SG[:, t, :], ALU.mult).then_inc(L[l]["y_used"], 1)
                    dve.wait_ge(L[l]["y_used"], t + 1)
                    last = dve.tensor_tensor(X[:, t, :], X[:, t, :], AO[:, t, :], ALU.add)
                    if t % TPC == TPC - 1:
                        last.then_inc(L[l]["x_done"], 1)

            dve.wait_ge(L[0]["ao_ready"], len(STEPS))
            for c in range(NC):
                stats(AO, 0, c)
            layernorm(0, AO, AO, L[0]["ao_ready"], 2, L[0]["ao_ready"])
            dve.wait_ge(F["ffn_silu"], NT + 1)
            add_branches(0, 0)

            dve.wait_ge(L[0]["x_done"], NC)
            for c in range(NC):
                stats(X, 1, c)
            layernorm(1, X, XN, L[1]["var_ready"], 1, L[1]["xn_ready"])

            dve.wait_ge(R["logits_evac"], 2)
            for t in range(NT):
                last = dve.max(MX8[:, t, :], LG[:, t, :])
            step(last)
            for t in range(NT):
                last = dve.match_replace(RP[:, t, :], MX8[:, t, :], LG[:, t, :], -3e38)
            step(last)
            dve.tensor_tensor(EX, LG, MX8[:, :, 0:1].to_broadcast([P, NT, E1]), ALU.subtract).then_inc(R["shifted"], 1)
            step(dve.tensor_tensor(MK, LG, RP, ALU.not_equal))
            dve.wait_ge(R["exp_ready"], 1)
            step(dve.tensor_tensor(EX, EX, MK, ALU.mult))
            step(dve.tensor_reduce(nrm[:, 0, 0:NT], EX, axis=AX.X, op=ALU.add))
            step(dve.reciprocal(nrm[:, 1, 0:NT], nrm[:, 0, 0:NT]))
            dve.tensor_tensor(EX, EX, nrm[:, 1, 0:NT].unsqueeze(2).to_broadcast([P, NT, E1]), ALU.mult).then_inc(R["route_ready"], 1)
            step(dve.tensor_scalar(IOD, iota[0:E1, :], -1.0, float(T), ALU.mult, ALU.add))
            for c in range(NC):
                dve.wait_ge(R["maskT_psum"], c + 1)
                last = dve.tensor_tensor(SC[:, c * CH:(c + 1) * CH], bank[c % 2][0:E1, :], IOD[:, c * CH:(c + 1) * CH], ALU.mult)
                last.then_inc(R["score_ready"], 1)
            dve.wait_ge(R["score_ready"], NC)
            for r in range(CAP // 8):
                step(dve.max(TK[:, 8 * r:8 * r + 8], SC))
                if r < CAP // 8 - 1:
                    step(dve.match_replace(SC, TK[:, 8 * r:8 * r + 8], SC, 0.0))
            dve.sem_inc(R["slots_ready"], 1)
            dve.wait_ge(R["slotT_psum"], 1)
            step(dve.tensor_scalar(TOK[:], bank[0][:, 0:NJ], -1.0, float(T), ALU.mult, ALU.add))
            dve.tensor_scalar(IDX[:], TOK[:], float(T - 1), None, ALU.min).then_inc(R["idx_ready"], 1)
            for q in range(4):
                dve.wait_ge(gath[q], 16 * NJ // 4)
            gx = GX.rearrange("p j n -> p (j n)")
            dve.tensor_copy(WS[0:64, :], gx[0:64, D:NJ * (D + E1):D + E1 + 1])
            step(dve.tensor_copy(WS[64:128, :], gx[64:128, D + NJ:NJ * (D + E1):D + E1 + 1]))
            for b in range(NJB):
                dve.wait_ge(R["silu_ready"], b + 1)
                if b >= 2:
                    dve.wait_ge(R["y_psum"], b - 1)
                dve.tensor_tensor(HH[:, 2 + b % 2, :], pair_bank[b % 2][0:F1, 1, :], HH[:, b % 2, :], ALU.mult).then_inc(R["h_ready"], 1)
                dve.wait_ge(R["y_psum"], b + 1)
                jb = slice(b * JB, (b + 1) * JB)
                y = SG[:, 0:JB, :]
                step(dve.tensor_tensor(y, bank[2 + b % 2][:].rearrange("p (j n) -> p j n", n=D),
                                       WS[:, jb].unsqueeze(2).to_broadcast([P, JB, D]), ALU.mult))
                step(dve.tensor_copy(YS[:, 0, jb, :], y))
                step(dve.tensor_tensor(y, y, YS[:, 0, jb, :], ALU.subtract))
                step(dve.tensor_copy(YS[:, 1, jb, :], y))
                step(dve.tensor_tensor(YS[:, 2, jb, :], y, YS[:, 1, jb, :], ALU.subtract))
                dve.sem_inc(R["y_split"], 1)
            for c in range(NC):
                dve.wait_ge(R["sh_silu"], c + 1)
                dve.tensor_tensor(SHH[:, c * TPC:(c + 1) * TPC, :].rearrange("p t n -> p (t n)")[0:F1, :], pair_bank[c % 2][0:F1, 1, :],
                                  HH[:, c % 2, :], ALU.mult).then_inc(R["sh_ready"], 1)

            for t in range(NT):
                if t >= 2:
                    dve.wait_ge(R["z_psum"], t - 1)
                dve.tensor_tensor(OH[:, t % 2], TOK[:].unsqueeze(2).to_broadcast([P, NJ, P]),
                                   iota[:, t * P:(t + 1) * P].unsqueeze(1).to_broadcast([P, NJ, P]),
                                   ALU.is_equal).then_inc(R["onehot"], 1)

            dve.wait_ge(R["z_psum"], NT)
            evacuate_odd(1, 1.0, H)
            dve.wait_ge(L[1]["even_evac"], NT // 2)
            dve.wait_ge(L[1]["odd_evac"], NT // 2)
            qflat, kflat = (a[:].rearrange("p t n -> p (t n)") for a in (Q32, K32))
            n1 = NT * H
            for i, src in enumerate((qflat, kflat)):
                tmp = XN[:].rearrange("p t n -> p (t n)")
                step(dve.tensor_tensor(tmp, src, src, ALU.mult))
                step(dve.tensor_reduce(nrm[:, 0, i * n1:(i + 1) * n1], tmp.rearrange("p (a n) -> p a n", n=HD), axis=AX.X, op=ALU.add))
            dve.sem_inc(N1["qk_sq"], 1)
            dve.wait_ge(N1["qk_norm"], 1)
            refine(2 * n1, 1e-8)
            for i, src in enumerate((qflat, kflat)):
                s3 = src.rearrange("p (a n) -> p a n", n=HD)
                dve.tensor_tensor(s3, s3, nrm[:, 3, i * n1:(i + 1) * n1].unsqueeze(2).to_broadcast([P, n1, HD]), ALU.mult).then_inc(N1["qk_scaled"], 1)
            dve.wait_ge(N1["qk_scaled"], 2)
            dve.wait_ge(N1["g_psum"], 1)
            gsrc = bank[2][:, 0:H * VW].rearrange("p (h n) -> p h n", n=VW)
            dve.tensor_tensor(gblk[:, :, 0:VW], gsrc, block_mask[:].to_broadcast([P, H, VW]), ALU.mult)
            dve.tensor_scalar(crow[:, :, 0:VW], bank[3][0:1, 0:H * VW].rearrange("p (h n) -> p h n", n=VW), -YAT_B, None, ALU.mult).then_inc(N1["g_ready"], 1)
            dve.wait_ge(N1["qnT_psum"], NC)
            step(dve.tensor_scalar(qflat, qflat, -1.0, None, ALU.mult))
            split_features(1, H)
            for n in range(len(STEPS)):
                evacuate_sums(1, n)
                normalize(1, n)
            dve.wait_ge(L[1]["ao_ready"], len(STEPS))
            add_branches(1, 0)

        @block.tensor
        def _(pe):
            def transpose_tiles(src, c, dst):
                for i in range(TPC):
                    last = pe.transpose(dst[:, i * P:(i + 1) * P], src[:, c * TPC + i, :], ident[:])
                return last

            def norm(l):
                for c in range(NC):
                    pe.wait_ge(L[l]["xn_ready"], c + 1)
                    if c >= 2:
                        pe.wait_ge(L[l]["xnT_ready"], c - 1)
                    transpose_tiles(XN, c, bank[c % 2]).then_inc(L[l]["xnT_psum"], 1)

            def project(l, w, b, n):
                pe.wait_ge(L[l]["xnT_ready"], NC)
                for t in range(NT):
                    if t >= 2:
                        pe.wait_ge(L[l]["even_evac" if t % 2 == 0 else "odd_evac"], t // 2)
                    pe.matmul(bank[t % 2][:, 0:n], XNT[:, t * P:(t + 1) * P], w[:], start=True, stop=False)
                    pe.matmul(bank[t % 2][:, 0:n], ones[0:1, 0:P], b[:], start=False, stop=True).then_inc(L[l]["proj_psum"], 1)

            def features(l, nk):
                for t in range(NT):
                    pe.wait_ge(L[l]["dup_staged"], t // TPC + 2)
                    if t >= 2:
                        pe.wait_ge(L[l]["qfeat_evac"], t - 1)
                        pe.wait_ge(L[l]["kfeat_evac"], t - 1)
                    c = t // TPC
                    qd = pair_bank[t % 2][:, 0, :].bitcast(BF16)
                    kd = pair_bank[t % 2][:, 1, :].bitcast(BF16)
                    for a in range(H // 2):
                        pe.transpose(qd[:, a * P:(a + 1) * P], QF[:, c % 2, t % TPC, a * P:(a + 1) * P], identb[:])
                    for a in range(nk // 2):
                        last = pe.transpose(kd[:, a * P:(a + 1) * P], KF[:, c % 2, t % TPC, a * P:(a + 1) * P], identb[:])
                    last.then_inc(L[l]["featT_psum"], 1)

            pe.wait_ge(S["consts"], 1)
            norm(0)
            pe.wait_ge(S["weights_in"], ALL_WEIGHTS)
            project(0, wqkv0, bqkv0, D + 2 * KV0 * HD)

            for t in range(NT):
                last = pe.matmul(bank[2][:, t * E0:(t + 1) * E0], XNT[:, t * P:(t + 1) * P], gate_w[:], start=True, stop=True)
            last.then_inc(F["gates_psum"], 1)
            pe.wait_ge(L[0]["even_evac"], NT // 2)
            pe.wait_ge(L[0]["odd_evac"], NT // 2)
            pe.wait_ge(F["gates_ready"], 1)
            for c in range(NC):
                if c >= 2:
                    pe.wait_ge(F["gateT_ready"], c - 1)
                for i in range(TPC):
                    last = pe.transpose(bank[c % 2][0:E0, i * P:(i + 1) * P], gatew[:, c * TPC + i, :], ident[:])
                last.then_inc(F["gateT_psum"], 1)
            pe.wait_ge(F["gateT_ready"], NC)

            def hidden(c):
                for m in range(5):
                    i = 5 * c + m
                    if i >= 2:
                        pe.wait_ge(F["h_act"], i - 1)
                    rows = P if m < 4 else F0
                    w = w1[:, m * P:(m + 1) * P] if m < 4 else ws1[:]
                    pe.matmul(bank[i % 2][0:rows, :], w, XNT[:, c * CH:(c + 1) * CH], start=True, stop=True).then_inc(F["h_psum"], 1)
                    if m < 4:
                        j = 4 * c + m
                        if j >= 2:
                            pe.wait_ge(F["h_gated"], j - 1)
                        pe.matmul(bank[2 + j % 2][:], gsel[:, m, :], gateT[:, c * CH:(c + 1) * CH], start=True, stop=True).then_inc(F["gsel_psum"], 1)

            def down(c):
                pe.wait_ge(F["h_gated"], 4 * (c + 1))
                pe.wait_ge(F["h_act"], 5 * (c + 1))
                for i in range(TPC):
                    t = c * TPC + i
                    if t >= 2:
                        pe.wait_ge(F["ffn_silu"], t - 1)
                    o = pair_bank[t % 2][:, 0, 0:D]
                    cols = slice(i * P, (i + 1) * P)
                    for m in range(4):
                        pe.matmul(o, HT[:, c % 2, m, cols], w2[:, m, :], start=m == 0, stop=False)
                    pe.matmul(o, HT[0:F0, c % 2, 4, cols], ws2[:], start=False, stop=False)
                    pe.matmul(o, gateT[:, t * P:(t + 1) * P], b2[:], start=False, stop=False)
                    pe.matmul(o, ones[0:1, 0:P], bs2[:], start=False, stop=True).then_inc(F["ffn_psum"], 1)

            for c in range(NC):
                hidden(c)
                if c >= 1:
                    down(c - 1)
            down(NC - 1)

            pe.wait_ge(F["ffn_silu"], NT)
            features(0, KV0)
            pe.wait_ge(L[0]["qfeat_evac"], NT)
            pe.wait_ge(L[0]["kfeat_evac"], NT)

            def key_head(l, h):
                return h if l else h % KV0

            def unit_scores(l, ks, hd):
                n, k = KSTEPS[l][ks]
                c, g = STEPS[n]
                u = HPG * ks + hd
                h = HPG * g + hd
                hk = key_head(l, h)
                r = 64 * (h % 2)
                if hd == 0 and k == 0 and l == 0:
                    pe.wait_ge(M["m_rows_a"], n + 1)
                    pe.wait_ge(M["m_rows_b"], n + 1)
                if u >= 2:
                    pe.wait_ge(L[l]["probs"], u - 1 if l == 0 else 5 * ((u - 2) // 4) + (u - 2) % 4 + 1)
                out_ = pair_bank[u % 2][:].rearrange("p a b -> p (a b)")
                unit = UNITS[l](c)[k]
                for blk, at, w in unit:
                    q0 = (c + 1) * CH - w
                    diag = l == 0 and blk >= TPC * c
                    last = pe.matmul(out_[:, at:at + w], KFT[r:r + 64, hk // 2, blk * P:(blk + 1) * P],
                                     QFT[r:r + 64, h // 2, q0:q0 + w], start=True, stop=not diag)
                    if diag:
                        last = pe.matmul(out_[:, at:at + P], identb[:], mask_kq[:], start=False, stop=True)
                last.then_inc(L[l]["scores"], 1)

            def unit_sums(l, ks, half):
                n, k = KSTEPS[l][ks]
                c, g = STEPS[n]
                nunits = len(UNITS[l](c))
                unit = UNITS[l](c)[k]
                part = unit[0:1] if half == 0 else unit[1:]
                if half == 0:
                    pe.wait_ge(L[l]["probs"], HPG * (ks + 1) if l == 0 else 5 * (ks + 1))
                    if k == 0:
                        if n >= 1:
                            pe.wait_ge(L[l]["sums_evac"], n)
                        if l == 1:
                            pe.matmul(bank[2][:], gblk[:, HPG * g:HPG * (g + 1), :].rearrange("p h n -> p (h n)"),
                                      QNT[:, c * CH:(c + 1) * CH], start=True, stop=False)
                            pe.matmul(bank[2][:], crow[:, HPG * g:HPG * (g + 1), :].rearrange("p h n -> p (h n)"),
                                      ones[:], start=False, stop=False)
                for i, (blk, at, w) in enumerate(part):
                    for hd in range(HPG):
                        hv = HPG * g + hd if l else hd
                        lastone = k == nunits - 1 and half == (1 if len(unit) > 1 else 0) and i == len(part) - 1
                        last = pe.matmul(bank[2][32 * hd:32 * hd + 32, CH - w:CH], VA[:, blk, hv * VW:hv * VW + 32],
                                         WORK[:, ks % 2, hd * 2 * CH + at:hd * 2 * CH + at + w],
                                         start=l == 0 and k == 0 and half == 0 and i == 0, stop=lastone)
                if half == 1 or len(unit) == 1:
                    if not (half == 1 and len(unit) == 1):
                        last.then_inc(L[l]["sums"], 1)

            def sums_transpose(l, n):
                pe.wait_ge(L[l]["sums_evac"], n + 1)
                if n >= 1:
                    pe.wait_ge(L[l]["ao_ready"], n)
                if l == 0:
                    k = min(n + 2, len(STEPS))
                    pe.wait_ge(M["m_rows_a"], k)
                    pe.wait_ge(M["m_rows_b"], k)
                for i in range(TPC):
                    last = pe.transpose(bank[3][:, i * P:(i + 1) * P], OT[:, n % 2, i * P:(i + 1) * P], ident[:])
                last.then_inc(L[l]["sumsT"], 1)

            def max_scores(n, lo, hi):
                c, g = STEPS[n]
                for i in range(lo, hi):
                    hd, qt, kc = MAXIMA[n][i]
                    u = MAX_BASE[n] + i
                    if u >= 2:
                        pe.wait_ge(M["max_done"], u - 1)
                    h = HPG * g + hd
                    r = 64 * (h % 2)
                    w = CH if kc < c else (qt + 1) * P
                    last = pe.matmul(bank[u % 2][:, 0:w], QFT[r:r + 64, h // 2, c * CH + qt * P:c * CH + (qt + 1) * P],
                                     KFT[r:r + 64, (h % KV0) // 2, kc * CH:kc * CH + w], start=True, stop=kc < c)
                    if kc == c:
                        last = pe.matmul(bank[u % 2][:, w - P:w], identb[:], mask_qk[:], start=False, stop=True)
                    last.then_inc(M["max_scores"], 1)

            def max_transpose(n):
                pe.wait_ge(M["minus_max"], n + 1)
                if n >= 2:
                    pe.wait_ge(L[0]["ao_ready"], n - 1)
                dst = bank[3][:].bitcast(BF16).rearrange("p (a n) -> p a n", n=CH)
                for a in range(2):
                    for i in range(TPC):
                        last = pe.transpose(dst[:, a, i * P:(i + 1) * P], MF[:, i, a, :], identb[:])
                last.then_inc(M["mT_psum"], 1)

            max_scores(0, 0, len(MAXIMA[0]))
            max_transpose(0)
            nsteps = len(STEPS)
            for ks, (n, k) in enumerate(KSTEPS[0]):
                c, g = STEPS[n]
                nk = len(UNITS[0](c))
                more = n + 1 < nsteps
                for hd in range(HPG):
                    unit_scores(0, ks, hd)
                    if ks >= 1 and hd == 1:
                        unit_sums(0, ks - 1, 0)
                    if ks >= 1 and hd == 2:
                        unit_sums(0, ks - 1, 1)
                    if more and k < nk - 1:
                        max_scores(n + 1, *max_slot(n, HPG * k + hd))
                    if k == 0 and hd == 3 and n >= 1:
                        sums_transpose(0, n - 1)
                    if more and k == nk - 1 and hd == 2:
                        max_transpose(n + 1)
            unit_sums(0, len(KSTEPS[0]) - 1, 0)
            sums_transpose(0, nsteps - 1)

            def end_layer(l, w, b):
                for c in range(NC):
                    if l == 0:
                        pe.wait_ge(L[0]["ao_ready"], nsteps + 1 + c + 1)
                    if c >= 2:
                        pe.wait_ge(L[l]["lnT_ready"], c - 1)
                    transpose_tiles(AO, c, bank[c % 2]).then_inc(L[l]["lnT_psum"], 1)
                for t in range(NT):
                    pe.wait_ge(L[l]["lnT_ready"], t // TPC + 1)
                    if t >= 2:
                        pe.wait_ge(L[l]["y_used"], t - 1)
                    o = bank[2 + t % 2][:, 0:D]
                    pe.matmul(o, XNT[:, t * P:(t + 1) * P], w[:], start=True, stop=False)
                    pe.matmul(o, ones[0:1, 0:P], b[:], start=False, stop=True).then_inc(L[l]["y_psum"], 1)

            end_layer(0, wo[0], bo[0])

            norm(1)
            pe.wait_ge(L[1]["xnT_ready"], NC)
            for t in range(NT):
                last = pe.matmul(bank[t // 8][:, (t % 8) * E1:(t % 8 + 1) * E1], XNT[:, t * P:(t + 1) * P], router[:], start=True, stop=True)
                if t % 8 == 7:
                    last.then_inc(R["logits_psum"], 1)
            pe.wait_ge(R["logits_evac"], 2)
            pe.wait_ge(R["route_ready"], 1)
            for c in range(NC):
                if c >= 2:
                    pe.wait_ge(R["score_ready"], c - 1)
                for i in range(TPC):
                    last = pe.transpose(bank[c % 2][0:E1, i * P:(i + 1) * P], MK[:, c * TPC + i, :], ident[:])
                last.then_inc(R["maskT_psum"], 1)
            pe.wait_ge(R["slots_ready"], 1)
            for half in range(2):
                last = pe.matmul(bank[0][64 * half:64 * half + 64, 0:NJ], TK[:], ident[0:E1, half * NJ:(half + 1) * NJ], start=True, stop=True)
            last.then_inc(R["slotT_psum"], 1)
            pe.wait_ge(R["idx_ready"], 1)
            for b in range(NJB):
                pe.wait_ge(gath[b * JB // (NJ // 4)], 16 * NJ // 4)
                if b >= 2:
                    pe.wait_ge(R["xbT_ready"], b - 1)
                for i in range(JB):
                    last = pe.transpose(bank[b % 2][:, i * P:(i + 1) * P], GX[:, b * JB + i, 0:D], ident[:])
                last.then_inc(R["xbT_psum"], 1)

            def gate_up(b):
                pe.wait_ge(R["xbT_ready"], b + 1)
                pe.wait_ge(w_in[b % 2], 96 * (b // 2 + 1))
                if b >= 2:
                    pe.wait_ge(R["h_ready"], b - 1)
                for which in range(2):
                    for i in range(JB):
                        for half in range(2):
                            last = pe.matmul(pair_bank[b % 2][0:F1, which, i * P + half * CAP:i * P + (half + 1) * CAP],
                                             wgu[b % 2][:, which, half, i, :],
                                             XBT[:, b * JB + i, half * CAP:(half + 1) * CAP], start=True, stop=True)
                last.then_inc(R["gu_psum"], 1)

            def expert_down(b):
                pe.wait_ge(R["h_ready"], b + 1)
                if b >= 2:
                    pe.wait_ge(R["y_split"], b - 1)
                for i in range(JB):
                    for half in range(2):
                        last = pe.matmul(bank[2 + b % 2][64 * half:64 * half + 64, i * D:(i + 1) * D],
                                         HH[:, 2 + b % 2, i * P + half * CAP:i * P + (half + 1) * CAP],
                                         wdn[:, b % 2, half, i, :], start=True, stop=True)
                last.then_inc(R["y_psum"], 1)

            gate_up(0)
            for b in range(NJB):
                if b + 1 < NJB:
                    gate_up(b + 1)
                expert_down(b)
            for c in range(NC):
                pe.wait_ge(R["h_ready"], NJB)
                if c >= 2:
                    pe.wait_ge(R["sh_ready"], c - 1)
                for which in range(2):
                    last = pe.matmul(pair_bank[c % 2][0:F1, which, :], wsgu[:, which * F1:(which + 1) * F1],
                                     XNT[:, c * CH:(c + 1) * CH], start=True, stop=True)
                last.then_inc(R["sh_psum"], 1)
            pe.wait_ge(R["sh_ready"], NC)
            pe.wait_ge(R["y_split"], NJB)
            for t in range(NT):
                pe.wait_ge(R["onehot"], t + 1)
                if t >= 2:
                    pe.wait_ge(R["z_silu"], t - 1)
                o = bank[t % 2][:, 0:D]
                pe.matmul(o, SHH[:].rearrange("p t n -> p (t n)")[0:F1, t * P:(t + 1) * P], wsd[:], start=True, stop=False)
                for j in range(NJ):
                    for part in range(3):
                        last = pe.matmul(o, OH[:, t % 2, j, :], YS[:, part, j, :], start=False, stop=j == NJ - 1 and part == 2)
                last.then_inc(R["z_psum"], 1)
            pe.wait_ge(R["z_silu"], NT)
            project(1, wqkv1, bqkv1, 3 * D)
            pe.wait_ge(N1["qk_scaled"], 2)
            for c in range(NC):
                if c >= 2:
                    pe.wait_ge(N1["qnT_ready"], c - 1)
                transpose_tiles(Q32, c, bank[c % 2]).then_inc(N1["qnT_psum"], 1)
            for t in range(NT):
                pe.matmul(bank[2][:, 0:H * VW], K32[:, t, :], VA[:, t, 0:H * VW], start=t == 0, stop=t == NT - 1)
            for t in range(NT):
                last = pe.matmul(bank[3][0:1, 0:H * VW], ones_col[:], VA[:, t, 0:H * VW], start=t == 0, stop=t == NT - 1)
            last.then_inc(N1["g_psum"], 1)
            features(1, H)
            pe.wait_ge(L[1]["qfeat_evac"], NT)
            pe.wait_ge(L[1]["kfeat_evac"], NT)
            pe.wait_ge(N1["g_ready"], 1)
            pe.wait_ge(N1["qnT_ready"], NC)
            for ks, (n, k) in enumerate(KSTEPS[1]):
                for hd in range(HPG):
                    unit_scores(1, ks, hd)
                    if ks >= 1 and hd == 1:
                        unit_sums(1, ks - 1, 0)
                    if ks >= 1 and hd == 2:
                        unit_sums(1, ks - 1, 1)
                if k == 0 and n >= 1:
                    sums_transpose(1, n - 1)
            unit_sums(1, len(KSTEPS[1]) - 1, 0)
            unit_sums(1, len(KSTEPS[1]) - 1, 1)
            sums_transpose(1, nsteps - 1)
            pe.wait_ge(L[1]["ao_ready"], nsteps)
            end_layer(1, wo[1], bo[1])


def kernel(**inputs):
    import concourse.bacc as bacc
    from concourse.bass_utils import run_bass_kernel_spmd

    a = {k: np.asarray(v) for k, v in inputs.items()}
    row = lambda n: a[n].reshape(1, -1)
    col = lambda n: a[n].reshape(-1, 1)
    laid = {
        "x": a["L0_attn_x"].reshape(T, D),
        "Wq0": a["L0_attn_Wq"], "bq0": row("L0_attn_bq"), "Wk0": a["L0_attn_Wk"], "bk0": row("L0_attn_bk"),
        "Wv0": a["L0_attn_Wv"], "bv0": row("L0_attn_bv"), "ln_g": col("L0_attn_ln_g"), "ln_b": col("L0_attn_ln_b"),
        "Wo0": a["L0_attn_Wo"], "bo0": row("L0_attn_bo"),
        "gate_W": a["L0_ffn_gate_W"],
        "W1": a["L0_ffn_W1"].transpose(1, 0, 2).reshape(D, E0 * F0),
        "b1": a["L0_ffn_b1"].reshape(E0 // 2, P).T,
        "W2": a["L0_ffn_W2"].reshape(E0 // 2, P, D).transpose(1, 0, 2).reshape(P, E0 // 2 * D),
        "b2": a["L0_ffn_b2"],
        "Ws1": a["L0_ffn_Ws1"], "bs1": col("L0_ffn_bs1"), "Ws2": a["L0_ffn_Ws2"], "bs2": row("L0_ffn_bs2"),
        "route_scale": a["L0_ffn_route_scale"].reshape(1, 1),
        "Wq1": a["L1_attn_Wq"], "bq1": row("L1_attn_bq"), "Wk1": a["L1_attn_Wk"], "bk1": row("L1_attn_bk"),
        "Wv1": a["L1_attn_Wv"], "bv1": row("L1_attn_bv"), "Wo1": a["L1_attn_Wo"], "bo1": row("L1_attn_bo"),
        "router": a["L1_ffn_router_w"].T,
        "w_gate": a["L1_ffn_w_gate"].transpose(1, 0, 2).reshape(D, E1 * F1),
        "w_up": a["L1_ffn_w_up"].transpose(1, 0, 2).reshape(D, E1 * F1),
        "w_down": a["L1_ffn_w_down"].transpose(1, 0, 2).reshape(F1, E1 * D),
        "ws_gate_up": a["L1_ffn_ws_gate_up"], "ws_down": a["L1_ffn_ws_down"],
    }
    nc = bacc.Bacc("TRN2", target_bir_lowering=False, num_devices=1)
    arrays, ins = {}, {}
    for name, shape in IN_SHAPES.items():
        arrays[f"in_{name}"] = np.ascontiguousarray(laid[name])
        assert arrays[f"in_{name}"].shape == shape, name
        ins[name] = nc.dram_tensor(f"in_{name}", shape, FP32, kind="ExternalInput").ap()
    out = nc.dram_tensor("out", (T, D), FP32, kind="ExternalOutput").ap()
    scratch = nc.dram_tensor("token_rows", (T, D + E1), FP32, kind="Internal").ap()
    two_layers(nc, ins, out, scratch)
    r = run_bass_kernel_spmd(nc, [arrays], core_ids=[0])
    return r.results[0]["out"].reshape(1, T, D)
```

```python
import numpy as np
import concourse.bass as bass
from concourse import mybir
from contextlib import ExitStack

FP32 = mybir.dt.float32
BF16 = mybir.dt.bfloat16
I32 = mybir.dt.int32
U32 = mybir.dt.uint32
ALU = mybir.AluOpType
ACT = mybir.ActivationFunctionType
AX = mybir.AxisListType

P = 128
T = 2048
D = 128
NT = T // P
CH = 512
NC = T // CH
TPC = CH // P
H = 16
HD = D // H
KV0 = 4
NG = 4
HPG = H // NG
VW = HD + 1
E0, F0 = 8, 64
E1, F1, TOPK, CAP = 64, 96, 8, 64
NJ = E1 // 2
JB = 4
MP = NT // 2
UB = 4
NPW = 3
NU = H * NC * MP
V2 = VW * VW
LN_EPS = 1e-5
MASKED = -1e30
YAT_TOP = 1.1
YAT_A = 2.1 * 2.1
YAT_B = 2 * 2.1 - YAT_TOP

IN_SHAPES = {
    "x": (T, D), "Wq0": (D, D), "bq0": (1, D), "Wk0": (D, KV0 * HD), "bk0": (1, KV0 * HD),
    "Wv0": (D, KV0 * HD), "bv0": (1, KV0 * HD), "ln_g": (D, 1), "ln_b": (D, 1), "Wo0": (D, D), "bo0": (1, D),
    "gate_W": (D, E0), "W1": (D, E0 * F0), "b1": (P, E0 // 2), "W2": (P, E0 // 2 * D), "b2": (E0, D),
    "Ws1": (D, F0), "bs1": (F0, 1), "Ws2": (F0, D), "bs2": (1, D), "route_scale": (1, 1),
    "Wq1": (D, D), "bq1": (1, D), "Wk1": (D, D), "bk1": (1, D), "Wv1": (D, D), "bv1": (1, D),
    "Wo1": (D, D), "bo1": (1, D), "router": (D, E1), "w_gate": (D, E1 * F1), "w_up": (D, E1 * F1),
    "w_down": (F1, E1 * D), "ws_gate_up": (D, 2 * F1), "ws_down": (F1, D),
}


def two_layers(nc, ins, out, scratch, lin):
    ctx = ExitStack()
    with ctx:
        def sb(name, shape, dt=FP32):
            return ctx.enter_context(nc.sbuf_tensor(name, shape, dt))

        def sem(name):
            return ctx.enter_context(nc.semaphore(name))

        bank = [ctx.enter_context(nc.psum_tensor(f"bank{i}", [P, CH], FP32)) for i in range(4)]
        pair_bank = [ctx.enter_context(nc.psum_tensor(f"pair_bank{i}", [P, 2, CH], FP32)) for i in range(2)]

        X = sb("X", [P, NT, D])
        XN = sb("XN", [P, NT, D])
        XNT = sb("XNT", [P, T])
        QFT = sb("QFT", [P, H // 2, T], BF16)
        KFT = sb("KFT", [P, H // 2, T], BF16)
        Q32 = sb("Q32", [P, NT, D])
        K32 = sb("K32", [P, NT, D])
        VA = sb("VA", [P, NT, H * VW + 32 - VW])
        WORK = sb("WORK", [P, 2, HPG * 2 * CH])
        SG = sb("SG", [P, NT, D])
        AO = Q32
        ident = sb("ident", [P, P])
        identb = sb("identb", [P, P], BF16)
        mask_qk = sb("mask_qk", [P, P], BF16)
        mask_kq = sb("mask_kq", [P, P], BF16)
        block_mask = sb("block_mask", [P, H, 1])
        ones = sb("ones", [1, CH])
        ones_col = sb("ones_col", [P, 1])
        iota = sb("iota", [P, T])
        st = sb("st", [P, NT, 6])
        mv = sb("mv", [P, NT, 2])
        nrm = sb("nrm", [P, 4, NT * H * 2])
        OT = nrm[:, 0:2, :]
        small = sb("small", [P, 16, 24])

        wqkv0 = sb("wqkv0", [D, D + 2 * KV0 * HD])
        bqkv0 = sb("bqkv0", [1, D + 2 * KV0 * HD])
        wqkv1 = sb("wqkv1", [D, 3 * D])
        bqkv1 = sb("bqkv1", [1, 3 * D])
        ln_g, ln_b = sb("ln_g", [D, 1]), sb("ln_b", [D, 1])
        wo = [sb(f"wo{i}", [D, D]) for i in range(2)]
        bo = [sb(f"bo{i}", [1, D]) for i in range(2)]
        gate_w = sb("gate_w", [D, E0])
        w1, b1 = sb("w1", [D, E0 * F0]), sb("b1", [P, E0 // 2])
        w2, b2 = sb("w2", [P, E0 // 2, D]), sb("b2", [E0, D])
        ws1, bs1 = sb("ws1", [D, F0]), sb("bs1", [F0, 1])
        ws2, bs2 = sb("ws2", [F0, D]), sb("bs2", [1, D])
        rscale = sb("rscale", [P, 1])
        router = sb("router", [D, E1])
        wsgu, wsd = sb("wsgu", [D, 2 * F1]), sb("wsd", [F1, D])
        wgu = [sb("wgu", [D, 2, 2, JB, F1])[:],
               SG[:, JB:NT, :].rearrange("p t n -> p (t n)").rearrange("p (w h j f) -> p w h j f", w=2, h=2, j=JB)]
        wdn = Q32[:].rearrange("p t n -> p (t n)")[0:F1, :].rearrange("p (b h j n) -> p b h j n", b=2, h=2, j=JB)

        work = WORK[:, :, :].rearrange("p a b -> p (a b)")
        workb = work.bitcast(BF16)
        QF = workb[:, 0:8192].rearrange("p (b t n) -> p b t n", b=2, t=TPC)
        KF = workb[:, 8192:16384].rearrange("p (b t n) -> p b t n", b=2, t=TPC)
        HT = work[:, 0:2 * 5 * CH].rearrange("p (b m n) -> p b m n", b=2, m=5)
        MF = sb("MF", [P, TPC, 2, P], BF16)
        MX = sb("MX", [P, 2, HPG * TPC, NC])
        gates = sb("gates", [P, NT, E0 + 6])
        gatew = sb("gatew", [P, NT, E0])
        gateT = work[0:E0, 2 * 5 * CH:2 * 5 * CH + T]
        gsel = sb("gsel", [E0, E0 // 2, P])
        xn = XN[:].rearrange("p t n -> p (t n)")
        RQ, RK = XN[:, 0:TPC, :], XN[:, TPC:2 * TPC, :]
        PW = work[:, 0:NPW * UB * CH].rearrange("p (b u n) -> p b u n", b=NPW, u=UB)
        NUM = work[:, NPW * UB * CH:].rearrange("p (t h n) -> p t h n", t=NT, h=H)
        DEN = nrm[:, 3, 0:NT * H].rearrange("p (t h) -> p t h", h=H)
        TS = nrm[0:V2, 0:2, :]
        at = iter(np.cumsum([0, 2 * CH, 2 * TPC * V2, H * VW]).tolist())
        a0, a1, a2, a3 = at
        UCOPY = XNT[:, a0:a1].rearrange("p (b n) -> p b n", b=2)
        TT = XNT[:, a1:a2].rearrange("p (b n) -> p b n", b=2)
        G32 = XNT[:, a2:a3]
        GC = XNT[0:1, a3:a3 + H * VW]
        MM = xn[:, 0:2 * MP * V2].rearrange("p (b m n) -> p b m n", b=2, m=MP)
        MT = xn[:, 2 * MP * V2:3 * MP * V2].rearrange("p (m n) -> p m n", m=MP)
        LROW = iota[:, 0:H * V2].rearrange("p (h n) -> p h n", h=H)
        LG = Q32[:, :, 0:E1]
        RP = Q32[:, :, E1:2 * E1]
        MK = K32[:, :, 0:E1]
        EX = K32[:, :, E1:2 * E1]
        MX8 = sb("MX8", [P, NT, 8])
        SC = work[0:E1, 0:T]
        IOD = work[0:E1, T:2 * T]
        TK = sb("TK", [E1, CAP])
        TOK = sb("TOK", [P, NJ])
        IDX = sb("IDX", [P, NJ], I32)
        WS = sb("WS", [P, NJ])
        GX = work[:, 0:NJ * (D + E1)].rearrange("p (j n) -> p j n", j=NJ)
        XBT = KFT[:, :, :].rearrange("p a b -> p (a b)").bitcast(FP32)[:, 0:NJ * P].rearrange("p (j n) -> p j n", j=NJ)
        YS = QFT[:, :, :].rearrange("p a b -> p (a b)")[:, 0:NJ * 3 * D].rearrange("p (k j n) -> p k j n", k=3, j=NJ)
        HH = XN[:].rearrange("p t n -> p (t n)")[0:F1, :].rearrange("p (b n) -> p b n", b=4)
        SHH = K32
        OH = KFT[:, :, :].rearrange("p a b -> p (a b)")[:, NJ * P * 2:NJ * P * 4].rearrange("p (b j n) -> p b j n", b=2, j=NJ)

        def sems(*names):
            return {n: sem(n) for n in names}

        S = sems(
            "x_in", "weights_in", "consts", "consts0", "dve_step", "pool_step", "out_stored",
            "moe_rows_out", "linear_out", "linear_in")
        x_in = [sem(f"x_in{c}") for c in range(NC)]
        w_in = [sem(f"w_in{c}") for c in range(2)]
        gath = [sem(f"gath{c}") for c in range(4)]
        L = [
            {n: sem(f"l{i}_{n}") for n in (
                "var_ready", "std_ready", "xn_ready", "xnT_psum", "xnT_ready", "proj_psum", "even_evac", "odd_evac",
                "staged", "dup_staged", "featT_psum", "qfeat_evac", "kfeat_evac",
                "scores", "probs", "sums", "sums_evac", "sumsT", "ao_ready", "lnT_psum", "lnT_ready",
                "y_psum", "y_used", "x_done")}
            for i in range(2)]
        F = sems("gates_psum", "sig_ready", "gates_ready", "gateT_psum", "gateT_ready", "h_psum", "h_act",
                 "gsel_psum", "h_gated", "ffn_psum", "ffn_silu")
        M = sems("max_scores", "max_done", "minus_max", "mT_psum", "m_rows_a", "m_rows_b")
        R = sems("logits_psum", "logits_evac", "shifted", "exp_ready", "route_ready", "maskT_psum", "score_ready",
                 "slots_ready", "slotT_psum", "idx_ready", "xbT_psum", "xbT_ready", "gu_psum", "silu_ready",
                 "h_ready", "y_psum", "y_split", "onehot", "sh_psum", "sh_silu", "sh_ready", "z_psum", "z_silu")
        N1 = sems("qk_sq", "qk_norm", "qk_scaled", "g_psum", "g_ready")
        Y = sems("distances", "copied", "product", "logs", "inverse", "sums", "sums_evac", "sumsT", "sumsT_evac",
                 "matrices", "combined")

        x_rows = ins["x"].rearrange("(t p) d -> p t d", p=P)
        out_rows = out.rearrange("(t p) d -> p t d", p=P)
        scratch_rows = scratch.rearrange("(t p) n -> p t n", p=P)
        wg_v = ins["w_gate"].rearrange("d (h j f) -> d h j f", h=2, j=NJ)
        wu_v = ins["w_up"].rearrange("d (h j f) -> d h j f", h=2, j=NJ)
        wd_v = ins["w_down"].rearrange("f (h j d) -> f h j d", h=2, j=NJ)
        NJB = NJ // JB

        WEIGHTS = [
            (wqkv0[:, 0:D], ins["Wq0"]), (wqkv0[:, D:D + 32], ins["Wk0"]), (wqkv0[:, D + 32:D + 64], ins["Wv0"]),
            (bqkv0[:, 0:D], ins["bq0"]), (bqkv0[:, D:D + 32], ins["bk0"]), (bqkv0[:, D + 32:D + 64], ins["bv0"]),
            (gate_w[:], ins["gate_W"]), (rscale[:], ins["route_scale"].to_broadcast([P, 1])),
            (w1[:], ins["W1"]), (b1[:], ins["b1"]), (w2[:].rearrange("p m d -> p (m d)"), ins["W2"]), (b2[:], ins["b2"]),
            (ws1[:], ins["Ws1"]), (bs1[:], ins["bs1"]), (ws2[:], ins["Ws2"]), (bs2[:], ins["bs2"]),
            (ln_g[:], ins["ln_g"]), (ln_b[:], ins["ln_b"]), (wo[0][:], ins["Wo0"]), (bo[0][:], ins["bo0"]),
            (wqkv1[:, 0:D], ins["Wq1"]), (wqkv1[:, D:2 * D], ins["Wk1"]), (wqkv1[:, 2 * D:3 * D], ins["Wv1"]),
            (bqkv1[:, 0:D], ins["bq1"]), (bqkv1[:, D:2 * D], ins["bk1"]), (bqkv1[:, 2 * D:3 * D], ins["bv1"]),
            (wo[1][:], ins["Wo1"]), (bo[1][:], ins["bo1"]), (router[:], ins["router"]),
            (wsgu[:], ins["ws_gate_up"]), (wsd[:], ins["ws_down"]),
        ]
        ALL_WEIGHTS = 16 * len(WEIGHTS)

        STEPS = [(c, g) for c in range(NC) for g in range(NG)]

        def causal_units(c):
            full = [[(2 * m, 0, CH), (2 * m + 1, CH, CH)] for m in range(TPC * c // 2)]
            b = TPC * c
            return full + [[(b, 0, CH), (b + 1, CH, CH - P), (b + 3, 2 * CH - P, P)], [(b + 2, 0, CH - 2 * P)]]

        def yat_units(c):
            return [[(2 * m, 0, CH), (2 * m + 1, CH, CH)] for m in range(NT // 2)]

        UNITS = [causal_units, yat_units]
        KSTEPS = [[(n, k) for n, (c, g) in enumerate(STEPS) for k in range(len(UNITS[l](c)))] for l in range(2)]
        width_of = lambda unit: unit[-1][1] + unit[-1][2]
        N_KSTEPS = [len(k) for k in KSTEPS]

        def scores(l, ks):
            return HPG * ks

        MAXIMA = [[(hd, i, kc) for hd in range(HPG) for i in range(TPC) for kc in range(c + 1)] for c, g in STEPS]
        MAX_BASE = np.cumsum([0] + [len(m) for m in MAXIMA]).tolist()

        def max_slot(n, slot):
            total, slots = len(MAXIMA[n + 1]), HPG * (len(UNITS[0](STEPS[n][0])) - 1)
            return slot * total // slots, (slot + 1) * total // slots

        block = ctx.enter_context(nc.Block())

        @block.sync
        def _(sp):
            for c in range(NC):
                sp.dma_start(X[:, c * TPC:(c + 1) * TPC, :], x_rows[:, c * TPC:(c + 1) * TPC, :]).then_inc(x_in[c], 16)
            for dst, src in WEIGHTS:
                sp.dma_start(dst, src).then_inc(S["weights_in"], 16)
            sp.wait_ge(L[1]["xn_ready"], NC)
            sp.dma_start(scratch_rows[:, :, 0:D], XN[:, :, :]).then_inc(S["moe_rows_out"], 16)
            sp.wait_ge(R["route_ready"], 1)
            sp.dma_start(scratch_rows[:, :, D:D + E1], EX).then_inc(S["moe_rows_out"], 16)
            for b in range(NJB):
                if b >= 2:
                    sp.wait_ge(R["y_psum"], b - 1)
                for h in range(2):
                    sp.dma_start(wgu[b % 2][:, 0, h], wg_v[:, h, b * JB:(b + 1) * JB, :]).then_inc(w_in[b % 2], 16)
                    sp.dma_start(wgu[b % 2][:, 1, h], wu_v[:, h, b * JB:(b + 1) * JB, :]).then_inc(w_in[b % 2], 16)
                    sp.dma_start(wdn[:, b % 2, h], wd_v[:, h, b * JB:(b + 1) * JB, :]).then_inc(w_in[b % 2], 16)
            sp.wait_ge(N1["g_ready"], 1)
            for h in range(H):
                sp.dma_start(lin[h:h + 1, 0:HD * VW].rearrange("a (i j) -> (a i) j", j=VW),
                             G32[h * HD:(h + 1) * HD, h * VW:(h + 1) * VW]).then_inc(S["linear_out"], 16)
            sp.dma_start(lin[:, HD * VW:V2].rearrange("h (a j) -> a h j", a=1), GC.rearrange("p (h j) -> p h j", j=VW)).then_inc(S["linear_out"], 16)
            sp.wait_ge(S["linear_out"], 16 * (H + 1))
            sp.dma_start(LROW, lin.rearrange("(a h) n -> a h n", a=1).to_broadcast([P, H, V2])).then_inc(S["linear_in"], 16)
            for c in range(NC):
                sp.wait_ge(L[1]["x_done"], c + 1)
                sp.dma_start(out_rows[:, c * TPC:(c + 1) * TPC, :], X[:, c * TPC:(c + 1) * TPC, :]).then_inc(S["out_stored"], 16)
            sp.wait_ge(S["out_stored"], 16 * NC)

        @block.gpsimd
        def _(pool):
            n_pool = [0]

            def step(ins_):
                n_pool[0] += 1
                ins_.then_inc(S["pool_step"], 1)
                pool.wait_ge(S["pool_step"], n_pool[0])

            pool.memset(ident[:], 0.0)
            pool.memset(identb[:], 0.0)
            pool.memset(mask_qk[:], 0.0)
            pool.memset(mask_kq[:], 0.0)
            pool.memset(ones[:], 1.0)
            pool.memset(ones_col[:], 1.0)
            pool.memset(gsel[:], 0.0)
            pool.memset(gates[:], -1e30)
            pool.memset(MF[:], 0.0)
            pool.memset(KFT[:, 0:KV0, :].rearrange("p a n -> p (a n)").bitcast(FP32), 0.0)
            pool.memset(block_mask[:], -1.0)
            pool.iota(iota[:], pattern=[[1, T]], base=0, channel_multiplier=0, allow_small_or_imprecise_dtypes=True)
            step(pool.memset(VA[:], 1.0))
            for m in (ident, identb):
                pool.affine_select(out=m[:], in_=m[:], compare_op=ALU.not_equal, fill=1.0, base=0,
                                   pattern=[[-1, P]], channel_multiplier=1)
            pool.affine_select(out=mask_qk[:], in_=mask_qk[:], compare_op=ALU.is_ge, fill=MASKED, base=0,
                               pattern=[[-1, P]], channel_multiplier=1)
            pool.affine_select(out=mask_kq[:], in_=mask_kq[:], compare_op=ALU.is_ge, fill=MASKED, base=0,
                               pattern=[[1, P]], channel_multiplier=-1)
            step(pool.affine_select(out=block_mask[:, :, 0], in_=block_mask[:, :, 0], compare_op=ALU.is_ge, fill=0.0,
                                    base=0, pattern=[[-HD, H]], channel_multiplier=1))
            pool.affine_select(out=block_mask[:, :, 0], in_=block_mask[:, :, 0], compare_op=ALU.is_ge, fill=0.0,
                               base=HD - 1, pattern=[[HD, H]], channel_multiplier=-1)
            gs = gsel[:].rearrange("e m (h r) -> e (m h) r", h=2)
            pool.affine_select(out=gs, in_=gs, compare_op=ALU.not_equal, fill=1.0, base=0,
                               pattern=[[-1, E0], [0, F0]], channel_multiplier=1).then_inc(S["consts"], 1)

            def init_stage(l):
                if l == 0:
                    pool.wait_ge(F["ffn_psum"], NT)
                else:
                    pool.wait_ge(R["z_psum"], NT)
                step(pool.memset(work, 0.0))
                qv = QF.rearrange("p b t (h n) -> p (b t h) n", n=64)
                nk = H if l else KV0
                if l == 0:
                    for b in range(2):
                        last = pool.memset(KF[:, b, :, 0:nk * 64].rearrange("p t (h n) -> p t h n", n=64)[:, :, :, 0:2], 1.0)
                else:
                    kall = KF.rearrange("p b t (h n) -> p (b t h) n", n=64)
                    pool.memset(kall[:, :, 0:3], 1.0)
                    parts, rest = [], np.float32(YAT_TOP)
                    for _ in range(3):
                        bits = np.frombuffer(np.float32(rest).tobytes(), np.uint32)[0]
                        part = np.frombuffer(np.uint32(bits & 0xFFFF0000).tobytes(), np.float32)[0]
                        parts.append(float(part))
                        rest = np.float32(rest - part)
                    for i, v in enumerate(parts):
                        last = pool.memset(qv[:, :, i:i + 1], v)
                last.then_inc(L[l]["dup_staged"], 1)

            def duplicates(l):
                nk = H if l else KV0
                for c in range(NC):
                    pool.wait_ge(L[l]["staged"], c + 1)
                    q = QF[:, c % 2].rearrange("p t (h n) -> p (t h) n", n=64)
                    pool.tensor_copy(q[:, :, 16:24], q[:, :, 8:16])
                    pool.tensor_copy(q[:, :, 32:40], q[:, :, 8:16])
                    pool.tensor_copy(q[:, :, 48:56], q[:, :, 24:32])
                    k = KF[:, c % 2, :, 0:nk * 64].rearrange("p t (h n) -> p t h n", n=64)
                    pool.tensor_copy(k[:, :, :, 24:32], k[:, :, :, 8:16])
                    pool.tensor_copy(k[:, :, :, 40:48], k[:, :, :, 8:16])
                    pool.tensor_copy(k[:, :, :, 48:56], k[:, :, :, 16:24]).then_inc(L[l]["dup_staged"], 1)

            init_stage(0)
            duplicates(0)

            pool.wait_ge(R["idx_ready"], 1)
            pool.wait_ge(S["moe_rows_out"], 32)
            for j in range(NJ):
                pool.indirect_dma_start(
                    out=GX[:, j, :], out_offset=None, in_=scratch[:, :],
                    in_offset=bass.IndirectOffsetOnAxis(ap=IDX[:, j:j + 1].bitcast(U32), axis=0),
                ).then_inc(gath[j // (NJ // 4)], 16)
            init_stage(1)
            duplicates(1)
            pool.wait_ge(S["linear_in"], 16)

            def pair_matrices(h):
                if h >= 1:
                    pool.wait_ge(Y["matrices"], h)
                if h >= 2:
                    pool.wait_ge(Y["sums"], NC * MP * (h - 1))
                V3 = VA[:, :, h * VW:(h + 1) * VW].rearrange("p (m b) j -> p m b j", b=2)
                K3 = K32[:, :, h * HD:(h + 1) * HD].rearrange("p (m b) i -> p m b i", b=2)
                m_ = MM[:, h % 2].rearrange("p m (i j) -> p m i j", j=VW)
                t_ = MT.rearrange("p m (i j) -> p m i j", j=VW)
                for b, dst in ((0, m_), (1, t_)):
                    pool.tensor_tensor(dst[:, :, 0:HD, :], V3[:, :, b, :].unsqueeze(2).to_broadcast([P, MP, HD, VW]),
                                       K3[:, :, 1 - b, :].unsqueeze(3).to_broadcast([P, MP, HD, VW]), ALU.mult)
                    last = pool.tensor_scalar(dst[:, :, HD, :], V3[:, :, b, :], YAT_TOP, None, ALU.mult)
                step(last)
                pool.tensor_tensor(MM[:, h % 2], MM[:, h % 2], MT, ALU.add).then_inc(Y["matrices"], 1)

            def combine(i):
                h, c = divmod(i, NC)
                pool.wait_ge(Y["sumsT_evac"], i + 1)
                t_ = TT[:, i % 2, :].rearrange("p (q i j) -> p q i j", q=TPC, j=VW)
                step(pool.tensor_tensor(TT[:, i % 2, :].rearrange("p (q n) -> p q n", n=V2), TT[:, i % 2, :].rearrange("p (q n) -> p q n", n=V2),
                                        LROW[:, h, :].unsqueeze(1).to_broadcast([P, TPC, V2]), ALU.add))
                step(pool.tensor_tensor(t_[:, :, 0:HD], t_[:, :, 0:HD],
                                        Q32[:, c * TPC:(c + 1) * TPC, h * HD:(h + 1) * HD].unsqueeze(3).to_broadcast([P, TPC, HD, VW]),
                                        ALU.mult))
                step(pool.tensor_tensor(t_[:, :, 0:4], t_[:, :, 0:4], t_[:, :, 4:8], ALU.add))
                step(pool.tensor_tensor(t_[:, :, 0:2], t_[:, :, 0:2], t_[:, :, 2:4], ALU.add))
                step(pool.tensor_tensor(t_[:, :, 0], t_[:, :, 0], t_[:, :, 1], ALU.add))
                ts = slice(c * TPC, (c + 1) * TPC)
                pool.tensor_tensor(NUM[:, ts, h, :], t_[:, :, 0, 0:HD], t_[:, :, HD, 0:HD], ALU.add)
                pool.tensor_tensor(DEN[:, ts, h], t_[:, :, 0, HD], t_[:, :, HD, HD], ALU.add).then_inc(Y["combined"], 1)

            pair_matrices(0)
            pair_matrices(1)
            for i in range(H * NC):
                combine(i)
                if i % NC == NC - 1 and i // NC + 2 < H:
                    pair_matrices(i // NC + 2)

        @block.scalar
        def _(act):
            def norm(l):
                act.wait_ge(L[l]["var_ready"], 1)
                act.activation(nrm[:, 1, 0:NT], nrm[:, 0, 0:NT], ACT.Sqrt).then_inc(L[l]["std_ready"], 1)
                for c in range(NC):
                    act.wait_ge(L[l]["xnT_psum"], c + 1)
                    act.copy(XNT[:, c * CH:(c + 1) * CH], bank[c % 2][:]).then_inc(L[l]["xnT_ready"], 1)

            def evacuate_even(l, scale, nk):
                for t in range(0, NT, 2):
                    src = bank[0]
                    act.wait_ge(L[l]["proj_psum"], t + 1)
                    act.activation(Q32[:, t, :], src[:, 0:D], ACT.Copy, scale=scale)
                    act.copy(K32[:, t, 0:nk * HD], src[:, D:D + nk * HD])
                    act.copy(VA[:, t, 0:nk * VW].rearrange("p (h n) -> p h n", n=VW)[:, :, 0:HD],
                             src[:, D + nk * HD:D + 2 * nk * HD].rearrange("p (h n) -> p h n", n=HD)).then_inc(L[l]["even_evac"], 1)

            def evacuate_features(l):
                for t in range(NT):
                    act.wait_ge(L[l]["featT_psum"], t + 1)
                    src = pair_bank[t % 2][:, 0, :].bitcast(BF16).rearrange("p (a n) -> p a n", n=P)
                    act.copy(QFT[:, :, t * P:(t + 1) * P], src).then_inc(L[l]["qfeat_evac"], 1)

            norm(0)
            evacuate_even(0, float(HD) ** -0.5, KV0)

            act.wait_ge(F["gates_psum"], 1)
            act.activation(gates[:, :, 0:E0], bank[2][:, 0:NT * E0].rearrange("p (t e) -> p t e", e=E0),
                           ACT.Sigmoid).then_inc(F["sig_ready"], 1)
            act.wait_ge(F["gateT_psum"], 1)
            for c in range(NC):
                act.wait_ge(F["gateT_psum"], c + 1)
                act.copy(gateT[:, c * CH:(c + 1) * CH], bank[c % 2][0:E0, :]).then_inc(F["gateT_ready"], 1)
            def ffn_out(c):
                for t in range(c * TPC, (c + 1) * TPC):
                    act.wait_ge(F["ffn_psum"], t + 1)
                    act.copy(SG[:, t, :], pair_bank[t % 2][:, 0, 0:D]).then_inc(F["ffn_silu"], 1)

            for c in range(NC):
                for m in range(5):
                    rows = P if m < 4 else F0
                    act.wait_ge(F["h_psum"], 5 * c + m + 1)
                    if c >= 2 and m == 0:
                        act.wait_ge(F["ffn_psum"], TPC * (c - 1))
                    act.activation(HT[0:rows, c % 2, m, :], bank[(5 * c + m) % 2][0:rows, :], ACT.Gelu,
                                   bias=b1[:, m:m + 1] if m < 4 else bs1[:]).then_inc(F["h_act"], 1)
                if c >= 1:
                    ffn_out(c - 1)
            ffn_out(NC - 1)

            evacuate_features(0)

            act.preload_act_table_set("natural_log_exp_and_others")

            def m_rows(n):
                c, g = STEPS[n]
                act.wait_ge(M["mT_psum"], n + 1)
                src = bank[3][:, :].bitcast(BF16).rearrange("p (a n) -> p a n", n=CH)
                act.copy(QFT[0:2, 2 * g:2 * g + 2, c * CH:(c + 1) * CH], src[0:2]).then_inc(M["m_rows_a"], 1)

            m_rows(0)
            for ks, (n, k) in enumerate(KSTEPS[0]):
                c, g = STEPS[n]
                w = width_of(UNITS[0](c)[k])
                for hd in range(HPG):
                    if hd == 3 and k == len(UNITS[0](c)) - 1 and n + 1 < len(STEPS):
                        m_rows(n + 1)
                    u = HPG * ks + hd
                    act.wait_ge(L[0]["scores"], u + 1)
                    if ks >= 2 and hd == 0:
                        act.wait_ge(L[0]["sums"], ks - 1)
                    act.activation(WORK[:, ks % 2, hd * 2 * CH:hd * 2 * CH + w],
                                   pair_bank[u % 2][:].rearrange("p a b -> p (a b)")[:, 0:w],
                                   ACT.Exp).then_inc(L[0]["probs"], 1)

            def end_layer(l):
                for c in range(NC):
                    act.wait_ge(L[l]["lnT_psum"], c + 1)
                    if l == 0:
                        act.activation(XNT[:, c * CH:(c + 1) * CH], bank[c % 2][:], ACT.Identity, bias=ln_b[:],
                                       scale=ln_g[:]).then_inc(L[l]["lnT_ready"], 1)
                    else:
                        act.copy(XNT[:, c * CH:(c + 1) * CH], bank[c % 2][:]).then_inc(L[l]["lnT_ready"], 1)

            act.wait_ge(L[0]["ao_ready"], len(STEPS))
            act.activation(SG[:], SG[:], ACT.Silu).then_inc(F["ffn_silu"], 1)
            act.wait_ge(L[0]["ao_ready"], len(STEPS) + 1)
            act.activation(nrm[:, 1, 0:NT], nrm[:, 0, 0:NT], ACT.Sqrt).then_inc(L[0]["std_ready"], 1)
            end_layer(0)

            norm(1)
            for b in range(2):
                act.wait_ge(R["logits_psum"], b + 1)
                act.copy(LG[:, 8 * b:8 * b + 8, :], bank[b][:].rearrange("p (t e) -> p t e", e=E1)).then_inc(R["logits_evac"], 1)
            act.wait_ge(R["shifted"], 1)
            act.activation(EX, EX, ACT.Exp).then_inc(R["exp_ready"], 1)
            for b in range(NJB):
                act.wait_ge(R["xbT_psum"], b + 1)
                act.copy(XBT[:, b * JB:(b + 1) * JB, :].rearrange("p j n -> p (j n)"), bank[b % 2][:]).then_inc(R["xbT_ready"], 1)
            for b in range(NJB):
                act.wait_ge(R["gu_psum"], b + 1)
                if b >= 2:
                    act.wait_ge(R["h_ready"], b - 1)
                act.activation(HH[:, b % 2, :], pair_bank[b % 2][0:F1, 0, :], ACT.Silu).then_inc(R["silu_ready"], 1)
            for c in range(NC):
                act.wait_ge(R["sh_psum"], c + 1)
                if c >= 2:
                    act.wait_ge(R["sh_ready"], c - 1)
                act.activation(HH[:, c % 2, :], pair_bank[c % 2][0:F1, 0, :], ACT.Silu).then_inc(R["sh_silu"], 1)
            for t in range(NT):
                act.wait_ge(R["z_psum"], t + 1)
                act.activation(SG[:, t, :], bank[t % 2][:, 0:D], ACT.Silu).then_inc(R["z_silu"], 1)
            evacuate_even(1, 1.0, H)
            act.wait_ge(N1["qk_sq"], 1)
            act.activation(nrm[:, 1, :], nrm[:, 0, :], ACT.Sqrt).then_inc(N1["qk_norm"], 1)
            evacuate_features(1)
            act.preload_act_table_set("natural_log_exp_and_others")
            def evacuate_pair_sums(i):
                act.wait_ge(Y["sums"], MP * (i + 1))
                if i >= 2:
                    act.wait_ge(Y["sumsT"], i - 1)
                act.copy(TS[:, i % 2, :], bank[i % 2][0:V2, :]).then_inc(Y["sums_evac"], 1)

            def evacuate_transposed(i):
                act.wait_ge(Y["sumsT"], i + 1)
                if i >= 2:
                    act.wait_ge(Y["combined"], i - 1)
                act.copy(TT[:, i % 2, :], bank[2 + i % 2][:, 0:TPC * V2]).then_inc(Y["sumsT_evac"], 1)

            NB = NU // UB
            BPI = MP // UB
            for b in range(NB + 3):
                if b < NB:
                    act.wait_ge(Y["product"], UB * (b + 1))
                    w = PW[:, b % NPW, :, :].rearrange("p a n -> p (a n)")
                    act.activation(w, w, ACT.Ln, scale=1.0 / YAT_A).then_inc(Y["logs"], 1)
                    act.wait_ge(Y["logs"], b + 1)
                    act.activation(w, w, ACT.Exp, scale=-1.0).then_inc(Y["inverse"], 1)
                done = b - 2
                if done >= 0 and done % BPI == BPI - 1:
                    evacuate_pair_sums(done // BPI)
                done = b - 4
                if done >= 0 and done % BPI == BPI - 1:
                    evacuate_transposed(done // BPI)
            evacuate_transposed(NU // MP - 1)
            end_layer(1)

        @block.vector
        def _(dve):
            n_dve = [0]

            def step(ins_):
                n_dve[0] += 1
                ins_.then_inc(S["dve_step"], 1)
                dve.wait_ge(S["dve_step"], n_dve[0])

            def inverse_std(l, ready_sem, ready_value, first):
                n = NT
                dve.wait_ge(ready_sem, ready_value)
                refine(n, 0.0)

            def refine(n, add):
                v, s, r, y = (nrm[:, i, 0:n] for i in range(4))
                step(dve.tensor_scalar(s, s, 1e-30, None, ALU.max))
                step(dve.reciprocal(r, s))
                step(dve.tensor_tensor(y, v, r, ALU.mult))
                step(dve.tensor_tensor(y, y, s, ALU.add))
                step(dve.tensor_scalar(y, y, 0.5, add, ALU.mult, ALU.add))
                step(dve.reciprocal(y, y))

            def stats(src, l, c):
                for t in range(c * TPC, (c + 1) * TPC):
                    last = dve.bn_stats(st[:, t, :], src[:, t, :])
                step(last)
                for t in range(c * TPC, (c + 1) * TPC):
                    last = dve.bn_aggr(mv[:, t, :], st[:, t, :])
                step(last)

            def layernorm(l, src, dst, var_sem, std_wait, done_sem):
                step(dve.tensor_scalar(nrm[:, 0, 0:NT], mv[:, :, 1], LN_EPS, None, ALU.add))
                dve.sem_inc(var_sem, 1)
                dve.wait_ge(L[l]["std_ready"], std_wait)
                refine(NT, 0.0)
                for t in range(NT):
                    last = dve.tensor_scalar(dst[:, t, :], src[:, t, :], mv[:, t, 0:1], nrm[:, 3, t:t + 1],
                                             ALU.subtract, ALU.mult)
                    if t % TPC == TPC - 1:
                        last.then_inc(done_sem, 1)

            def evacuate_odd(l, scale, nk):
                for t in range(1, NT, 2):
                    src = bank[1]
                    dve.wait_ge(L[l]["proj_psum"], t + 1)
                    dve.tensor_scalar(Q32[:, t, :], src[:, 0:D], scale, None, ALU.mult)
                    dve.tensor_copy(K32[:, t, 0:nk * HD], src[:, D:D + nk * HD])
                    dve.tensor_copy(VA[:, t, 0:nk * VW].rearrange("p (h n) -> p h n", n=VW)[:, :, 0:HD],
                                    src[:, D + nk * HD:D + 2 * nk * HD].rearrange("p (h n) -> p h n", n=HD)).then_inc(L[l]["odd_evac"], 1)

            def split_features(l, nk):
                dve.wait_ge(L[l]["even_evac"], NT // 2)
                dve.wait_ge(L[l]["odd_evac"], NT // 2)
                for c in range(NC):
                    ts = slice(c * TPC, (c + 1) * TPC)
                    dve.wait_ge(L[l]["dup_staged"], 1)
                    if c >= 2:
                        dve.wait_ge(L[l]["featT_psum"], TPC * (c - 1))
                    q = QF[:, c % 2].rearrange("p t (h n) -> p (t h) n", n=64)
                    k = KF[:, c % 2, :, 0:nk * 64].rearrange("p t (h n) -> p t h n", n=64)
                    qs = Q32[:, ts, :].rearrange("p t (h n) -> p (t h) n", n=HD)
                    ks = K32[:, ts, 0:nk * HD].rearrange("p t (h n) -> p t h n", n=HD)
                    rq = RQ.rearrange("p t (h n) -> p (t h) n", n=HD)
                    rk = RK[:, :, 0:nk * HD].rearrange("p t (h n) -> p t h n", n=HD)
                    for part, (qa, ka) in enumerate(((8, 8), (24, 16), (40, 32))):
                        dve.tensor_copy(q[:, :, qa:qa + 8], qs)
                        last = dve.tensor_copy(k[:, :, :, ka:ka + 8], ks)
                        if part < 2:
                            step(last)
                            dve.tensor_tensor(rq, qs, q[:, :, qa:qa + 8], ALU.subtract)
                            step(dve.tensor_tensor(rk, ks, k[:, :, :, ka:ka + 8], ALU.subtract))
                            qs, ks = rq, rk
                    last.then_inc(L[l]["staged"], 1)
                    if c >= 1:
                        evacuate_kfeatures(l, nk, c - 1)
                evacuate_kfeatures(l, nk, NC - 1)

            def evacuate_kfeatures(l, nk, c):
                for t in range(c * TPC, (c + 1) * TPC):
                    dve.wait_ge(L[l]["featT_psum"], t + 1)
                    src = pair_bank[t % 2][:, 1, :].bitcast(BF16)[:, 0:nk * 64].rearrange("p (a n) -> p a n", n=P)
                    if l == 0:
                        dve.tensor_copy(KFT[0:64, 0:nk:2, t * P:(t + 1) * P], src[0:64])
                        dve.tensor_copy(KFT[64:128, 1:nk:2, t * P:(t + 1) * P], src[64:128]).then_inc(L[l]["kfeat_evac"], 1)
                    else:
                        dve.tensor_copy(KFT[:, 0:nk // 2, t * P:(t + 1) * P], src).then_inc(L[l]["kfeat_evac"], 1)

            for c in range(NC):
                dve.wait_ge(x_in[c], 16)
                stats(X, 0, c)
            layernorm(0, X, XN, L[0]["var_ready"], 1, L[0]["xn_ready"])
            dve.wait_ge(S["consts"], 1)
            evacuate_odd(0, float(HD) ** -0.5, KV0)

            dve.wait_ge(F["sig_ready"], 1)
            dve.wait_ge(S["weights_in"], ALL_WEIGHTS)
            step(dve.tensor_scalar(gates[:, :, 0:E0], gates[:, :, 0:E0], rscale[:], None, ALU.mult))
            for t in range(NT):
                last = dve.max(MX8[:, t, :], gates[:, t, 0:E0])
            step(last)
            step(dve.tensor_tensor(nrm[:, 0, 0:NT], MX8[:, :, 0], MX8[:, :, 1], ALU.add))
            step(dve.reciprocal(nrm[:, 1, 0:NT], nrm[:, 0, 0:NT]))
            step(dve.memset(MX8[:, :, 2:8], -1e30))
            for t in range(NT):
                last = dve.match_replace(small[:, t, 0:E0 + 6], MX8[:, t, :], gates[:, t, :], 2e30)
            step(last)
            step(dve.tensor_scalar(small[:, :, 16:24], small[:, :, 0:E0], 1e30, None, ALU.is_gt))
            step(dve.tensor_tensor(small[:, :, 16:24], small[:, :, 16:24], gates[:, :, 0:E0], ALU.mult))
            dve.tensor_tensor(gatew[:], small[:, :, 16:24],
                              nrm[:, 1, 0:NT].unsqueeze(2).to_broadcast([P, NT, E0]), ALU.mult).then_inc(F["gates_ready"], 1)
            for c in range(NC):
                for m in range(4):
                    i = 4 * c + m
                    dve.wait_ge(F["h_act"], 5 * c + m + 1)
                    dve.wait_ge(F["gsel_psum"], i + 1)
                    dve.tensor_tensor(HT[:, c % 2, m, :], HT[:, c % 2, m, :], bank[2 + i % 2][:], ALU.mult).then_inc(F["h_gated"], 1)

            split_features(0, KV0)

            def maxima(n, lo, hi):
                for i in range(lo, hi):
                    hd, qt, kc = MAXIMA[n][i]
                    c, g = STEPS[n]
                    w = CH if kc < c else (qt + 1) * P
                    u = MAX_BASE[n] + i
                    dve.wait_ge(M["max_scores"], u + 1)
                    dve.reduce_max(MX[:, n % 2, hd * TPC + qt, kc:kc + 1], bank[u % 2][:, 0:w], AX.X).then_inc(M["max_done"], 1)

            def minus_max(n):
                c, g = STEPS[n]
                dve.wait_ge(M["max_done"], MAX_BASE[n + 1])
                m32 = small[:, 0, 0:16]
                m3 = m32.rearrange("p (a b) -> p a b", a=HPG)
                step(dve.tensor_reduce(m32, MX[:, n % 2, :, 0:c + 1], axis=AX.X, op=ALU.max))
                step(dve.tensor_scalar(m32, m32, -1.0, None, ALU.mult))
                if n >= 1:
                    dve.wait_ge(M["mT_psum"], n)
                hi = MF[:].rearrange("p t a (e n) -> p (a e) t n", n=64)
                step(dve.tensor_copy(hi[:, :, :, 0], m3))
                dve.tensor_tensor(hi[:, :, :, 1], m3, hi[:, :, :, 0], ALU.subtract).then_inc(M["minus_max"], 1)
                dve.wait_ge(M["mT_psum"], n + 1)
                src = bank[3][:, :].bitcast(BF16).rearrange("p (a n) -> p a n", n=CH)
                dve.tensor_copy(QFT[64:66, 2 * g:2 * g + 2, c * CH:(c + 1) * CH], src[64:66]).then_inc(M["m_rows_b"], 1)

            def evacuate_sums(l, n):
                dve.wait_ge(L[l]["sums"], sum(1 for m, _ in KSTEPS[l] if m <= n))
                if n >= 2:
                    dve.wait_ge(L[l]["sumsT"], n - 1)
                dve.tensor_copy(OT[:, n % 2, :], bank[2][:]).then_inc(L[l]["sums_evac"], 1)

            def normalize(l, n):
                c, g = STEPS[n]
                dve.wait_ge(L[l]["sumsT"], n + 1)
                src = bank[3][:].rearrange("p (t h n) -> p t h n", t=TPC, n=32)
                den = small[:, 1, 0:16].rearrange("p (t h) -> p t h", t=TPC)
                if l == 0:
                    step(dve.reciprocal(den, src[:, :, :, HD]))
                else:
                    step(dve.tensor_scalar(den, src[:, :, :, HD], 1e-6, None, ALU.add))
                    step(dve.reciprocal(den, den))
                dst = AO[:, c * TPC:(c + 1) * TPC, g * 32:(g + 1) * 32].rearrange("p t (h n) -> p t h n", n=HD)
                dve.tensor_tensor(dst, src[:, :, :, 0:HD], den.unsqueeze(3).to_broadcast([P, TPC, HPG, HD]),
                                  ALU.mult).then_inc(L[l]["ao_ready"], 1)

            maxima(0, 0, len(MAXIMA[0]))
            minus_max(0)
            for n in range(len(STEPS) + 1):
                more = n + 1 < len(STEPS)
                if more:
                    maxima(n + 1, 0, max_slot(n, 3)[0])
                if n >= 1:
                    evacuate_sums(0, n - 1)
                if more:
                    maxima(n + 1, *max_slot(n, 3))
                if n >= 1:
                    normalize(0, n - 1)
                if more:
                    maxima(n + 1, max_slot(n, 3)[1], len(MAXIMA[n + 1]))
                    minus_max(n + 1)

            def add_branches(l, stride):
                for t in range(NT):
                    dve.wait_ge(L[l]["y_psum"], t + 1)
                    dve.tensor_tensor(AO[:, t, :], bank[2 + t % 2][:, 0:D], SG[:, t, :], ALU.mult).then_inc(L[l]["y_used"], 1)
                    dve.wait_ge(L[l]["y_used"], t + 1)
                    last = dve.tensor_tensor(X[:, t, :], X[:, t, :], AO[:, t, :], ALU.add)
                    if t % TPC == TPC - 1:
                        last.then_inc(L[l]["x_done"], 1)

            dve.wait_ge(L[0]["ao_ready"], len(STEPS))
            for c in range(NC):
                stats(AO, 0, c)
            layernorm(0, AO, AO, L[0]["ao_ready"], 2, L[0]["ao_ready"])
            dve.wait_ge(F["ffn_silu"], NT + 1)
            add_branches(0, 0)

            dve.wait_ge(L[0]["x_done"], NC)
            for c in range(NC):
                stats(X, 1, c)
            layernorm(1, X, XN, L[1]["var_ready"], 1, L[1]["xn_ready"])

            dve.wait_ge(R["logits_evac"], 2)
            for t in range(NT):
                last = dve.max(MX8[:, t, :], LG[:, t, :])
            step(last)
            for t in range(NT):
                last = dve.match_replace(RP[:, t, :], MX8[:, t, :], LG[:, t, :], -3e38)
            step(last)
            dve.tensor_tensor(EX, LG, MX8[:, :, 0:1].to_broadcast([P, NT, E1]), ALU.subtract).then_inc(R["shifted"], 1)
            step(dve.tensor_tensor(MK, LG, RP, ALU.not_equal))
            dve.wait_ge(R["exp_ready"], 1)
            step(dve.tensor_tensor(EX, EX, MK, ALU.mult))
            step(dve.tensor_reduce(nrm[:, 0, 0:NT], EX, axis=AX.X, op=ALU.add))
            step(dve.reciprocal(nrm[:, 1, 0:NT], nrm[:, 0, 0:NT]))
            dve.tensor_tensor(EX, EX, nrm[:, 1, 0:NT].unsqueeze(2).to_broadcast([P, NT, E1]), ALU.mult).then_inc(R["route_ready"], 1)
            step(dve.tensor_scalar(IOD, iota[0:E1, :], -1.0, float(T), ALU.mult, ALU.add))
            for c in range(NC):
                dve.wait_ge(R["maskT_psum"], c + 1)
                last = dve.tensor_tensor(SC[:, c * CH:(c + 1) * CH], bank[c % 2][0:E1, :], IOD[:, c * CH:(c + 1) * CH], ALU.mult)
                last.then_inc(R["score_ready"], 1)
            dve.wait_ge(R["score_ready"], NC)
            for r in range(CAP // 8):
                step(dve.max(TK[:, 8 * r:8 * r + 8], SC))
                if r < CAP // 8 - 1:
                    step(dve.match_replace(SC, TK[:, 8 * r:8 * r + 8], SC, 0.0))
            dve.sem_inc(R["slots_ready"], 1)
            dve.wait_ge(R["slotT_psum"], 1)
            step(dve.tensor_scalar(TOK[:], bank[0][:, 0:NJ], -1.0, float(T), ALU.mult, ALU.add))
            dve.tensor_scalar(IDX[:], TOK[:], float(T - 1), None, ALU.min).then_inc(R["idx_ready"], 1)
            for q in range(4):
                dve.wait_ge(gath[q], 16 * NJ // 4)
            gx = GX.rearrange("p j n -> p (j n)")
            dve.tensor_copy(WS[0:64, :], gx[0:64, D:NJ * (D + E1):D + E1 + 1])
            step(dve.tensor_copy(WS[64:128, :], gx[64:128, D + NJ:NJ * (D + E1):D + E1 + 1]))
            for b in range(NJB):
                dve.wait_ge(R["silu_ready"], b + 1)
                if b >= 2:
                    dve.wait_ge(R["y_psum"], b - 1)
                dve.tensor_tensor(HH[:, 2 + b % 2, :], pair_bank[b % 2][0:F1, 1, :], HH[:, b % 2, :], ALU.mult).then_inc(R["h_ready"], 1)
                dve.wait_ge(R["y_psum"], b + 1)
                jb = slice(b * JB, (b + 1) * JB)
                y = SG[:, 0:JB, :]
                step(dve.tensor_tensor(y, bank[2 + b % 2][:].rearrange("p (j n) -> p j n", n=D),
                                       WS[:, jb].unsqueeze(2).to_broadcast([P, JB, D]), ALU.mult))
                step(dve.tensor_copy(YS[:, 0, jb, :], y))
                step(dve.tensor_tensor(y, y, YS[:, 0, jb, :], ALU.subtract))
                step(dve.tensor_copy(YS[:, 1, jb, :], y))
                step(dve.tensor_tensor(YS[:, 2, jb, :], y, YS[:, 1, jb, :], ALU.subtract))
                dve.sem_inc(R["y_split"], 1)
            for c in range(NC):
                dve.wait_ge(R["sh_silu"], c + 1)
                dve.tensor_tensor(SHH[:, c * TPC:(c + 1) * TPC, :].rearrange("p t n -> p (t n)")[0:F1, :], pair_bank[c % 2][0:F1, 1, :],
                                  HH[:, c % 2, :], ALU.mult).then_inc(R["sh_ready"], 1)

            for t in range(NT):
                if t >= 2:
                    dve.wait_ge(R["z_psum"], t - 1)
                dve.tensor_tensor(OH[:, t % 2], TOK[:].unsqueeze(2).to_broadcast([P, NJ, P]),
                                   iota[:, t * P:(t + 1) * P].unsqueeze(1).to_broadcast([P, NJ, P]),
                                   ALU.is_equal).then_inc(R["onehot"], 1)

            dve.wait_ge(R["z_psum"], NT)
            evacuate_odd(1, 1.0, H)
            dve.wait_ge(L[1]["even_evac"], NT // 2)
            dve.wait_ge(L[1]["odd_evac"], NT // 2)
            qflat, kflat = (a[:].rearrange("p t n -> p (t n)") for a in (Q32, K32))
            n1 = NT * H
            for i, src in enumerate((qflat, kflat)):
                tmp = XN[:].rearrange("p t n -> p (t n)")
                step(dve.tensor_tensor(tmp, src, src, ALU.mult))
                step(dve.tensor_reduce(nrm[:, 0, i * n1:(i + 1) * n1], tmp.rearrange("p (a n) -> p a n", n=HD), axis=AX.X, op=ALU.add))
            dve.sem_inc(N1["qk_sq"], 1)
            dve.wait_ge(N1["qk_norm"], 1)
            refine(2 * n1, 1e-8)
            for i, (src, sign) in enumerate(((qflat, 1.0), (kflat, -1.0))):
                s3 = src.rearrange("p (a n) -> p a n", n=HD)
                dve.scalar_tensor_tensor(s3, s3, sign, nrm[:, 3, i * n1:(i + 1) * n1].unsqueeze(2).to_broadcast([P, n1, HD]),
                                         ALU.mult, ALU.mult).then_inc(N1["qk_scaled"], 1)
            dve.wait_ge(N1["qk_scaled"], 2)
            dve.wait_ge(N1["g_psum"], 1)
            dve.tensor_copy(G32, bank[2][:, 0:H * VW])
            dve.tensor_scalar(GC, bank[3][0:1, 0:H * VW], -YAT_B, None, ALU.mult).then_inc(N1["g_ready"], 1)
            split_features(1, H)
            for u in range(NU):
                dve.wait_ge(Y["distances"], u + 1)
                if u % UB == 0 and u // UB >= NPW:
                    dve.wait_ge(Y["sums"], UB * (u // UB - NPW + 1))
                dve.tensor_copy(UCOPY[:, u % 2, :], pair_bank[u % 2][:, 1, :]).then_inc(Y["copied"], 1)
                dve.wait_ge(Y["copied"], u + 1)
                dve.tensor_tensor(PW[:, (u // UB) % NPW, u % UB, :], pair_bank[u % 2][:, 0, :], UCOPY[:, u % 2, :],
                                  ALU.mult).then_inc(Y["product"], 1)
            dve.wait_ge(Y["combined"], NU // MP)
            step(dve.tensor_scalar(DEN, DEN, 1e-6, None, ALU.add))
            step(dve.reciprocal(DEN, DEN))
            dve.tensor_tensor(AO[:].rearrange("p t (h n) -> p t h n", n=HD), NUM,
                              DEN.unsqueeze(3).to_broadcast([P, NT, H, HD]), ALU.mult).then_inc(L[1]["ao_ready"], 1)
            add_branches(1, 0)

        @block.tensor
        def _(pe):
            def transpose_tiles(src, c, dst):
                for i in range(TPC):
                    last = pe.transpose(dst[:, i * P:(i + 1) * P], src[:, c * TPC + i, :], ident[:])
                return last

            def norm(l):
                for c in range(NC):
                    pe.wait_ge(L[l]["xn_ready"], c + 1)
                    if c >= 2:
                        pe.wait_ge(L[l]["xnT_ready"], c - 1)
                    transpose_tiles(XN, c, bank[c % 2]).then_inc(L[l]["xnT_psum"], 1)

            def project(l, w, b, n):
                pe.wait_ge(L[l]["xnT_ready"], NC)
                for t in range(NT):
                    if t >= 2:
                        pe.wait_ge(L[l]["even_evac" if t % 2 == 0 else "odd_evac"], t // 2)
                    pe.matmul(bank[t % 2][:, 0:n], XNT[:, t * P:(t + 1) * P], w[:], start=True, stop=False)
                    pe.matmul(bank[t % 2][:, 0:n], ones[0:1, 0:P], b[:], start=False, stop=True).then_inc(L[l]["proj_psum"], 1)

            def features(l, nk):
                for t in range(NT):
                    pe.wait_ge(L[l]["dup_staged"], t // TPC + 2)
                    if t >= 2:
                        pe.wait_ge(L[l]["qfeat_evac"], t - 1)
                        pe.wait_ge(L[l]["kfeat_evac"], t - 1)
                    c = t // TPC
                    qd = pair_bank[t % 2][:, 0, :].bitcast(BF16)
                    kd = pair_bank[t % 2][:, 1, :].bitcast(BF16)
                    for a in range(H // 2):
                        pe.transpose(qd[:, a * P:(a + 1) * P], QF[:, c % 2, t % TPC, a * P:(a + 1) * P], identb[:])
                    for a in range(nk // 2):
                        last = pe.transpose(kd[:, a * P:(a + 1) * P], KF[:, c % 2, t % TPC, a * P:(a + 1) * P], identb[:])
                    last.then_inc(L[l]["featT_psum"], 1)

            pe.wait_ge(S["consts"], 1)
            norm(0)
            pe.wait_ge(S["weights_in"], ALL_WEIGHTS)
            project(0, wqkv0, bqkv0, D + 2 * KV0 * HD)

            for t in range(NT):
                last = pe.matmul(bank[2][:, t * E0:(t + 1) * E0], XNT[:, t * P:(t + 1) * P], gate_w[:], start=True, stop=True)
            last.then_inc(F["gates_psum"], 1)
            pe.wait_ge(L[0]["even_evac"], NT // 2)
            pe.wait_ge(L[0]["odd_evac"], NT // 2)
            pe.wait_ge(F["gates_ready"], 1)
            for c in range(NC):
                if c >= 2:
                    pe.wait_ge(F["gateT_ready"], c - 1)
                for i in range(TPC):
                    last = pe.transpose(bank[c % 2][0:E0, i * P:(i + 1) * P], gatew[:, c * TPC + i, :], ident[:])
                last.then_inc(F["gateT_psum"], 1)
            pe.wait_ge(F["gateT_ready"], NC)

            def hidden(c):
                for m in range(5):
                    i = 5 * c + m
                    if i >= 2:
                        pe.wait_ge(F["h_act"], i - 1)
                    rows = P if m < 4 else F0
                    w = w1[:, m * P:(m + 1) * P] if m < 4 else ws1[:]
                    pe.matmul(bank[i % 2][0:rows, :], w, XNT[:, c * CH:(c + 1) * CH], start=True, stop=True).then_inc(F["h_psum"], 1)
                    if m < 4:
                        j = 4 * c + m
                        if j >= 2:
                            pe.wait_ge(F["h_gated"], j - 1)
                        pe.matmul(bank[2 + j % 2][:], gsel[:, m, :], gateT[:, c * CH:(c + 1) * CH], start=True, stop=True).then_inc(F["gsel_psum"], 1)

            def down(c):
                pe.wait_ge(F["h_gated"], 4 * (c + 1))
                pe.wait_ge(F["h_act"], 5 * (c + 1))
                for i in range(TPC):
                    t = c * TPC + i
                    if t >= 2:
                        pe.wait_ge(F["ffn_silu"], t - 1)
                    o = pair_bank[t % 2][:, 0, 0:D]
                    cols = slice(i * P, (i + 1) * P)
                    for m in range(4):
                        pe.matmul(o, HT[:, c % 2, m, cols], w2[:, m, :], start=m == 0, stop=False)
                    pe.matmul(o, HT[0:F0, c % 2, 4, cols], ws2[:], start=False, stop=False)
                    pe.matmul(o, gateT[:, t * P:(t + 1) * P], b2[:], start=False, stop=False)
                    pe.matmul(o, ones[0:1, 0:P], bs2[:], start=False, stop=True).then_inc(F["ffn_psum"], 1)

            for c in range(NC):
                hidden(c)
                if c >= 1:
                    down(c - 1)
            down(NC - 1)

            pe.wait_ge(F["ffn_silu"], NT)
            features(0, KV0)
            pe.wait_ge(L[0]["qfeat_evac"], NT)
            pe.wait_ge(L[0]["kfeat_evac"], NT)

            def unit_scores(l, ks, hd):
                n, k = KSTEPS[l][ks]
                c, g = STEPS[n]
                u = HPG * ks + hd
                h = HPG * g + hd
                if hd == 0 and k == 0 and l == 0:
                    pe.wait_ge(M["m_rows_a"], n + 1)
                    pe.wait_ge(M["m_rows_b"], n + 1)
                if u >= 2:
                    pe.wait_ge(L[l]["probs"], u - 1)
                out_ = pair_bank[u % 2][:].rearrange("p a b -> p (a b)")
                unit = UNITS[l](c)[k]
                for blk, at, w in unit:
                    q0 = (c + 1) * CH - w
                    diag = blk >= TPC * c
                    last = pe.matmul(out_[:, at:at + w], KFT[:, h % KV0, blk * P:(blk + 1) * P],
                                     QFT[:, h // 2, q0:q0 + w], start=True, stop=not diag)
                    if diag:
                        last = pe.matmul(out_[:, at:at + P], identb[:], mask_kq[:], start=False, stop=True)
                last.then_inc(L[l]["scores"], 1)

            def unit_sums(l, ks, half):
                n, k = KSTEPS[l][ks]
                c, g = STEPS[n]
                nunits = len(UNITS[l](c))
                unit = UNITS[l](c)[k]
                part = unit[0:1] if half == 0 else unit[1:]
                if half == 0:
                    pe.wait_ge(L[l]["probs"], HPG * (ks + 1))
                    if k == 0:
                        if n >= 1:
                            pe.wait_ge(L[l]["sums_evac"], n)
                for i, (blk, at, w) in enumerate(part):
                    for hd in range(HPG):
                        hv = HPG * g + hd if l else hd
                        lastone = k == nunits - 1 and half == (1 if len(unit) > 1 else 0) and i == len(part) - 1
                        last = pe.matmul(bank[2][32 * hd:32 * hd + 32, CH - w:CH], VA[:, blk, hv * VW:hv * VW + 32],
                                         WORK[:, ks % 2, hd * 2 * CH + at:hd * 2 * CH + at + w],
                                         start=l == 0 and k == 0 and half == 0 and i == 0, stop=lastone)
                if half == 1 or len(unit) == 1:
                    if not (half == 1 and len(unit) == 1):
                        last.then_inc(L[l]["sums"], 1)

            def sums_transpose(l, n):
                pe.wait_ge(L[l]["sums_evac"], n + 1)
                if n >= 1:
                    pe.wait_ge(L[l]["ao_ready"], n)
                if l == 0:
                    k = min(n + 2, len(STEPS))
                    pe.wait_ge(M["m_rows_a"], k)
                    pe.wait_ge(M["m_rows_b"], k)
                for i in range(TPC):
                    last = pe.transpose(bank[3][:, i * P:(i + 1) * P], OT[:, n % 2, i * P:(i + 1) * P], ident[:])
                last.then_inc(L[l]["sumsT"], 1)

            def max_scores(n, lo, hi):
                c, g = STEPS[n]
                for i in range(lo, hi):
                    hd, qt, kc = MAXIMA[n][i]
                    u = MAX_BASE[n] + i
                    if u >= 2:
                        pe.wait_ge(M["max_done"], u - 1)
                    h = HPG * g + hd
                    w = CH if kc < c else (qt + 1) * P
                    last = pe.matmul(bank[u % 2][:, 0:w], QFT[:, h // 2, c * CH + qt * P:c * CH + (qt + 1) * P],
                                     KFT[:, h % KV0, kc * CH:kc * CH + w], start=True, stop=kc < c)
                    if kc == c:
                        last = pe.matmul(bank[u % 2][:, w - P:w], identb[:], mask_qk[:], start=False, stop=True)
                    last.then_inc(M["max_scores"], 1)

            def max_transpose(n):
                pe.wait_ge(M["minus_max"], n + 1)
                if n >= 2:
                    pe.wait_ge(L[0]["ao_ready"], n - 1)
                dst = bank[3][:].bitcast(BF16).rearrange("p (a n) -> p a n", n=CH)
                for a in range(2):
                    for i in range(TPC):
                        last = pe.transpose(dst[:, a, i * P:(i + 1) * P], MF[:, i, a, :], identb[:])
                last.then_inc(M["mT_psum"], 1)

            max_scores(0, 0, len(MAXIMA[0]))
            max_transpose(0)
            nsteps = len(STEPS)
            for ks, (n, k) in enumerate(KSTEPS[0]):
                c, g = STEPS[n]
                nk = len(UNITS[0](c))
                more = n + 1 < nsteps
                for hd in range(HPG):
                    unit_scores(0, ks, hd)
                    if ks >= 1 and hd == 1:
                        unit_sums(0, ks - 1, 0)
                    if ks >= 1 and hd == 2:
                        unit_sums(0, ks - 1, 1)
                    if more and k < nk - 1:
                        max_scores(n + 1, *max_slot(n, HPG * k + hd))
                    if k == 0 and hd == 3 and n >= 1:
                        sums_transpose(0, n - 1)
                    if more and k == nk - 1 and hd == 2:
                        max_transpose(n + 1)
            unit_sums(0, len(KSTEPS[0]) - 1, 0)
            sums_transpose(0, nsteps - 1)

            def end_layer(l, w, b):
                for c in range(NC):
                    if l == 0:
                        pe.wait_ge(L[0]["ao_ready"], nsteps + 1 + c + 1)
                    else:
                        pe.wait_ge(L[1]["ao_ready"], 1)
                    if c >= 2:
                        pe.wait_ge(L[l]["lnT_ready"], c - 1)
                    transpose_tiles(AO, c, bank[c % 2]).then_inc(L[l]["lnT_psum"], 1)
                for t in range(NT):
                    pe.wait_ge(L[l]["lnT_ready"], t // TPC + 1)
                    if t >= 2:
                        pe.wait_ge(L[l]["y_used"], t - 1)
                    o = bank[2 + t % 2][:, 0:D]
                    pe.matmul(o, XNT[:, t * P:(t + 1) * P], w[:], start=True, stop=False)
                    pe.matmul(o, ones[0:1, 0:P], b[:], start=False, stop=True).then_inc(L[l]["y_psum"], 1)

            end_layer(0, wo[0], bo[0])

            norm(1)
            pe.wait_ge(L[1]["xnT_ready"], NC)
            for t in range(NT):
                last = pe.matmul(bank[t // 8][:, (t % 8) * E1:(t % 8 + 1) * E1], XNT[:, t * P:(t + 1) * P], router[:], start=True, stop=True)
                if t % 8 == 7:
                    last.then_inc(R["logits_psum"], 1)
            pe.wait_ge(R["logits_evac"], 2)
            pe.wait_ge(R["route_ready"], 1)
            for c in range(NC):
                if c >= 2:
                    pe.wait_ge(R["score_ready"], c - 1)
                for i in range(TPC):
                    last = pe.transpose(bank[c % 2][0:E1, i * P:(i + 1) * P], MK[:, c * TPC + i, :], ident[:])
                last.then_inc(R["maskT_psum"], 1)
            pe.wait_ge(R["slots_ready"], 1)
            for half in range(2):
                last = pe.matmul(bank[0][64 * half:64 * half + 64, 0:NJ], TK[:], ident[0:E1, half * NJ:(half + 1) * NJ], start=True, stop=True)
            last.then_inc(R["slotT_psum"], 1)
            pe.wait_ge(R["idx_ready"], 1)
            for b in range(NJB):
                pe.wait_ge(gath[b * JB // (NJ // 4)], 16 * NJ // 4)
                if b >= 2:
                    pe.wait_ge(R["xbT_ready"], b - 1)
                for i in range(JB):
                    last = pe.transpose(bank[b % 2][:, i * P:(i + 1) * P], GX[:, b * JB + i, 0:D], ident[:])
                last.then_inc(R["xbT_psum"], 1)

            def gate_up(b):
                pe.wait_ge(R["xbT_ready"], b + 1)
                pe.wait_ge(w_in[b % 2], 96 * (b // 2 + 1))
                if b >= 2:
                    pe.wait_ge(R["h_ready"], b - 1)
                for which in range(2):
                    for i in range(JB):
                        for half in range(2):
                            last = pe.matmul(pair_bank[b % 2][0:F1, which, i * P + half * CAP:i * P + (half + 1) * CAP],
                                             wgu[b % 2][:, which, half, i, :],
                                             XBT[:, b * JB + i, half * CAP:(half + 1) * CAP], start=True, stop=True)
                last.then_inc(R["gu_psum"], 1)

            def expert_down(b):
                pe.wait_ge(R["h_ready"], b + 1)
                if b >= 2:
                    pe.wait_ge(R["y_split"], b - 1)
                for i in range(JB):
                    for half in range(2):
                        last = pe.matmul(bank[2 + b % 2][64 * half:64 * half + 64, i * D:(i + 1) * D],
                                         HH[:, 2 + b % 2, i * P + half * CAP:i * P + (half + 1) * CAP],
                                         wdn[:, b % 2, half, i, :], start=True, stop=True)
                last.then_inc(R["y_psum"], 1)

            gate_up(0)
            for b in range(NJB):
                if b + 1 < NJB:
                    gate_up(b + 1)
                expert_down(b)
            for c in range(NC):
                pe.wait_ge(R["h_ready"], NJB)
                if c >= 2:
                    pe.wait_ge(R["sh_ready"], c - 1)
                for which in range(2):
                    last = pe.matmul(pair_bank[c % 2][0:F1, which, :], wsgu[:, which * F1:(which + 1) * F1],
                                     XNT[:, c * CH:(c + 1) * CH], start=True, stop=True)
                last.then_inc(R["sh_psum"], 1)
            pe.wait_ge(R["sh_ready"], NC)
            pe.wait_ge(R["y_split"], NJB)
            for t in range(NT):
                pe.wait_ge(R["onehot"], t + 1)
                if t >= 2:
                    pe.wait_ge(R["z_silu"], t - 1)
                o = bank[t % 2][:, 0:D]
                pe.matmul(o, SHH[:].rearrange("p t n -> p (t n)")[0:F1, t * P:(t + 1) * P], wsd[:], start=True, stop=False)
                for j in range(NJ):
                    for part in range(3):
                        last = pe.matmul(o, OH[:, t % 2, j, :], YS[:, part, j, :], start=False, stop=j == NJ - 1 and part == 2)
                last.then_inc(R["z_psum"], 1)
            pe.wait_ge(R["z_silu"], NT)
            project(1, wqkv1, bqkv1, 3 * D)
            pe.wait_ge(N1["qk_scaled"], 2)
            for t in range(NT):
                pe.matmul(bank[2][:, 0:H * VW], K32[:, t, :], VA[:, t, 0:H * VW], start=t == 0, stop=t == NT - 1)
            for t in range(NT):
                last = pe.matmul(bank[3][0:1, 0:H * VW], ones_col[:], VA[:, t, 0:H * VW], start=t == 0, stop=t == NT - 1)
            last.then_inc(N1["g_psum"], 1)
            features(1, H)
            pe.wait_ge(L[1]["qfeat_evac"], NT)
            pe.wait_ge(L[1]["kfeat_evac"], NT)
            pe.wait_ge(N1["g_ready"], 1)

            def distances(u):
                i, m = divmod(u, MP)
                h, c = divmod(i, NC)
                r = 64 * (h % 2)
                if u >= 2:
                    pe.wait_ge(Y["product"], u - 1)
                for b in range(2):
                    blk = 2 * m + b
                    last = pe.matmul(pair_bank[u % 2][:, b, :], KFT[r:r + 64, h // 2, blk * P:(blk + 1) * P],
                                     QFT[r:r + 64, h // 2, c * CH:(c + 1) * CH], start=True, stop=True)
                last.then_inc(Y["distances"], 1)

            def pair_sums(u):
                i, m = divmod(u, MP)
                h, c = divmod(i, NC)
                if u % UB == 0:
                    pe.wait_ge(Y["inverse"], u // UB + 1)
                if m == 0:
                    pe.wait_ge(Y["matrices"], h + 1)
                    if i >= 2:
                        pe.wait_ge(Y["sums_evac"], i - 1)
                last = pe.matmul(bank[i % 2][0:V2, :], MM[:, h % 2, m, :], PW[:, (u // UB) % NPW, u % UB, :],
                                 start=m == 0, stop=m == MP - 1)
                last.then_inc(Y["sums"], 1)

            def pair_sums_transpose(i):
                pe.wait_ge(Y["sums_evac"], i + 1)
                if i >= 2:
                    pe.wait_ge(Y["sumsT_evac"], i - 1)
                for q in range(TPC):
                    last = pe.transpose(bank[2 + i % 2][:, q * V2:(q + 1) * V2], TS[:, i % 2, q * P:(q + 1) * P], ident[0:V2, 0:V2])
                last.then_inc(Y["sumsT"], 1)

            LAG = 2 * UB
            for u in range(NU + LAG):
                if u < NU:
                    distances(u)
                if u >= LAG:
                    pair_sums(u - LAG)
                    if (u - LAG) % MP == 6 and u - LAG >= MP:
                        pair_sums_transpose((u - LAG) // MP - 1)
            pair_sums_transpose(NU // MP - 1)
            end_layer(1, wo[1], bo[1])


def kernel(**inputs):
    import concourse.bacc as bacc
    from concourse.bass_utils import run_bass_kernel_spmd

    a = {k: np.asarray(v) for k, v in inputs.items()}
    row = lambda n: a[n].reshape(1, -1)
    col = lambda n: a[n].reshape(-1, 1)
    laid = {
        "x": a["L0_attn_x"].reshape(T, D),
        "Wq0": a["L0_attn_Wq"], "bq0": row("L0_attn_bq"), "Wk0": a["L0_attn_Wk"], "bk0": row("L0_attn_bk"),
        "Wv0": a["L0_attn_Wv"], "bv0": row("L0_attn_bv"), "ln_g": col("L0_attn_ln_g"), "ln_b": col("L0_attn_ln_b"),
        "Wo0": a["L0_attn_Wo"], "bo0": row("L0_attn_bo"),
        "gate_W": a["L0_ffn_gate_W"],
        "W1": a["L0_ffn_W1"].transpose(1, 0, 2).reshape(D, E0 * F0),
        "b1": a["L0_ffn_b1"].reshape(E0 // 2, P).T,
        "W2": a["L0_ffn_W2"].reshape(E0 // 2, P, D).transpose(1, 0, 2).reshape(P, E0 // 2 * D),
        "b2": a["L0_ffn_b2"],
        "Ws1": a["L0_ffn_Ws1"], "bs1": col("L0_ffn_bs1"), "Ws2": a["L0_ffn_Ws2"], "bs2": row("L0_ffn_bs2"),
        "route_scale": a["L0_ffn_route_scale"].reshape(1, 1),
        "Wq1": a["L1_attn_Wq"], "bq1": row("L1_attn_bq"), "Wk1": a["L1_attn_Wk"], "bk1": row("L1_attn_bk"),
        "Wv1": a["L1_attn_Wv"], "bv1": row("L1_attn_bv"), "Wo1": a["L1_attn_Wo"], "bo1": row("L1_attn_bo"),
        "router": a["L1_ffn_router_w"].T,
        "w_gate": a["L1_ffn_w_gate"].transpose(1, 0, 2).reshape(D, E1 * F1),
        "w_up": a["L1_ffn_w_up"].transpose(1, 0, 2).reshape(D, E1 * F1),
        "w_down": a["L1_ffn_w_down"].transpose(1, 0, 2).reshape(F1, E1 * D),
        "ws_gate_up": a["L1_ffn_ws_gate_up"], "ws_down": a["L1_ffn_ws_down"],
    }
    nc = bacc.Bacc("TRN2", target_bir_lowering=False, num_devices=1)
    arrays, ins = {}, {}
    for name, shape in IN_SHAPES.items():
        arrays[f"in_{name}"] = np.ascontiguousarray(laid[name])
        assert arrays[f"in_{name}"].shape == shape, name
        ins[name] = nc.dram_tensor(f"in_{name}", shape, FP32, kind="ExternalInput").ap()
    out = nc.dram_tensor("out", (T, D), FP32, kind="ExternalOutput").ap()
    scratch = nc.dram_tensor("token_rows", (T, D + E1), FP32, kind="Internal").ap()
    lin = nc.dram_tensor("linear_part", (H, V2), FP32, kind="Internal").ap()
    two_layers(nc, ins, out, scratch, lin)
    r = run_bass_kernel_spmd(nc, [arrays], core_ids=[0])
    return r.results[0]["out"].reshape(1, T, D)
```

```python
import numpy as np
import concourse.bass as bass
from concourse import mybir
from contextlib import ExitStack

FP32 = mybir.dt.float32
BF16 = mybir.dt.bfloat16
I32 = mybir.dt.int32
U32 = mybir.dt.uint32
ALU = mybir.AluOpType
ACT = mybir.ActivationFunctionType
AX = mybir.AxisListType

P = 128
T = 2048
D = 128
NT = T // P
CH = 512
NC = T // CH
TPC = CH // P
H = 16
HD = D // H
KV0 = 4
NG = 4
HPG = H // NG
VW = HD + 1
E0, F0 = 8, 64
E1, F1, TOPK, CAP = 64, 96, 8, 64
NJ = E1 // 2
JB = 4
ROUNDS = CAP // 8
EPT = P // 8
QPR = E1 // EPT
MP = NT // 2
UB = 4
NPW = 3
NU = H * NC * MP
V2 = VW * VW
LN_EPS = 1e-5
MASKED = -1e30
YAT_TOP = 1.1
YAT_A = 2.1 * 2.1
YAT_B = 2 * 2.1 - YAT_TOP

IN_SHAPES = {
    "x": (T, D), "Wq0": (D, D), "bq0": (1, D), "Wk0": (D, KV0 * HD), "bk0": (1, KV0 * HD),
    "Wv0": (D, KV0 * HD), "bv0": (1, KV0 * HD), "ln_g": (D, 1), "ln_b": (D, 1), "Wo0": (D, D), "bo0": (1, D),
    "gate_W": (D, E0), "W1": (D, E0 * F0), "b1": (P, E0 // 2), "W2": (P, E0 // 2 * D), "b2": (E0, D),
    "Ws1": (D, F0), "bs1": (F0, 1), "Ws2": (F0, D), "bs2": (1, D), "route_scale": (1, 1),
    "Wq1": (D, D), "bq1": (1, D), "Wk1": (D, D), "bk1": (1, D), "Wv1": (D, D), "bv1": (1, D),
    "Wo1": (D, D), "bo1": (1, D), "router": (D, E1), "w_gate": (D, E1 * F1), "w_up": (D, E1 * F1),
    "w_down": (F1, E1 * D), "ws_gate_up": (D, 2 * F1), "ws_down": (F1, D),
}


def two_layers(nc, ins, out, scratch, lin, slot_out):
    ctx = ExitStack()
    with ctx:
        def sb(name, shape, dt=FP32):
            return ctx.enter_context(nc.sbuf_tensor(name, shape, dt))

        def sem(name):
            return ctx.enter_context(nc.semaphore(name))

        bank = [ctx.enter_context(nc.psum_tensor(f"bank{i}", [P, CH], FP32)) for i in range(4)]
        pair_bank = [ctx.enter_context(nc.psum_tensor(f"pair_bank{i}", [P, 2, CH], FP32)) for i in range(2)]

        X = sb("X", [P, NT, D])
        XN = sb("XN", [P, NT, D])
        XNT = sb("XNT", [P, T])
        QFT = sb("QFT", [P, H // 2, T], BF16)
        KFT = sb("KFT", [P, H // 2, T], BF16)
        Q32 = sb("Q32", [P, NT, D])
        K32 = sb("K32", [P, NT, D])
        VA = sb("VA", [P, NT, H * VW + 32 - VW])
        WORK = sb("WORK", [P, 2, HPG * 2 * CH])
        SG = sb("SG", [P, NT, D])
        AO = Q32
        ident = sb("ident", [P, P])
        identb = sb("identb", [P, P], BF16)
        mask_qk = sb("mask_qk", [P, P], BF16)
        mask_kq = sb("mask_kq", [P, P], BF16)
        expert_row = sb("expert_row", [E1, EPT, 8])
        expert_tile = sb("expert_tile", [E1, QPR])
        row_expert = sb("row_expert", [P, EPT])
        row_slot = sb("row_slot", [P, 8])
        first_row = sb("first_row", [P, P])
        ones_col = sb("ones_col", [P, 1])
        iota = sb("iota", [P, T])
        st = sb("st", [P, NT, 6])
        mv = sb("mv", [P, NT, 2])
        nrm = sb("nrm", [P, 4, NT * H * 2])
        OT = nrm[:, 0:2, :]
        small = sb("small", [P, 16, 24])

        wqkv0 = sb("wqkv0", [D, D + 2 * KV0 * HD])
        bqkv0 = sb("bqkv0", [P, D + 2 * KV0 * HD])
        wqkv1 = sb("wqkv1", [D, 3 * D])
        bqkv1 = sb("bqkv1", [P, 3 * D])
        ln_g, ln_b = sb("ln_g", [D, 1]), sb("ln_b", [D, 1])
        wo = [sb(f"wo{i}", [D, D]) for i in range(2)]
        bo = [sb(f"bo{i}", [P, D]) for i in range(2)]
        gate_w = sb("gate_w", [D, E0])
        w1, b1 = sb("w1", [D, E0 * F0]), sb("b1", [P, E0 // 2])
        w2, b2 = sb("w2", [P, E0 // 2, D]), sb("b2", [P, D])
        ws1, bs1 = sb("ws1", [D, F0]), sb("bs1", [F0, 1])
        ws2, bs2 = sb("ws2", [F0, D]), sb("bs2", [P, D])
        rscale = sb("rscale", [P, 1])
        router = sb("router", [D, E1])
        wsgu, wsd = sb("wsgu", [D, 2 * F1]), sb("wsd", [F1, D])
        wgu0 = sb("wgu0", [D, 2 * 2 * JB * F1])
        G32 = sb("G32", [P, H * VW])
        GC = sb("GC", [1, H * VW])

        work = WORK[:, :, :].rearrange("p a b -> p (a b)")
        workb = work.bitcast(BF16)
        QF = workb[:, 0:8192].rearrange("p (b t n) -> p b t n", b=2, t=TPC)
        KF = workb[:, 8192:16384].rearrange("p (b t n) -> p b t n", b=2, t=TPC)
        NM = E0 * F0 // P + 1
        free_keys = KFT[:, H // 4:, :].rearrange("p a n -> p (a n)").bitcast(FP32)
        free_xn = XN[:, 2 * TPC:, :].rearrange("p t n -> p (t n)")
        ht_slots = [free_keys[:, i * CH:(i + 1) * CH] for i in range(8)] + [free_xn[:, i * CH:(i + 1) * CH] for i in range(2)]
        HT = lambda c, m: ht_slots[c % 2 * NM + m]
        MF = sb("MF", [P, TPC, 2, P], BF16)
        MX = sb("MX", [P, 2, HPG * TPC, NC])
        gates = sb("gates", [P, NT, E0 + 6])
        gatew = sb("gatew", [P, NT, E0])
        gateT = iota[:]
        gsel = sb("gsel", [P, E0 // 2, P])
        xn = XN[:].rearrange("p t n -> p (t n)")
        split_rest = [XN[:, 0:2 * TPC, :], XNT[:, 0:2 * CH].rearrange("p (t n) -> p t n", n=D)]
        PW = work[:, 0:NPW * UB * CH].rearrange("p (b u n) -> p b u n", b=NPW, u=UB)
        NUM = work[:, NPW * UB * CH:].rearrange("p (t h n) -> p t h n", t=NT, h=H)
        DEN = nrm[:, 3, 0:NT * H].rearrange("p (t h) -> p t h", h=H)
        TS = nrm[0:V2, 0:2, :]
        a0, a1, a2 = np.cumsum([0, 2 * CH, 2 * TPC * V2]).tolist()
        UCOPY = XNT[:, a0:a1].rearrange("p (b n) -> p b n", b=2)
        TT = XNT[:, a1:a2].rearrange("p (b n) -> p b n", b=2)
        MM = xn[:, 0:2 * MP * V2].rearrange("p (b m n) -> p b m n", b=2, m=MP)
        MT = xn[:, 2 * MP * V2:3 * MP * V2].rearrange("p (m n) -> p m n", m=MP)
        LROW = iota[:, 0:H * V2].rearrange("p (h n) -> p h n", h=H)
        LG, RP, MK, EX = (work[:, T + i * NT * E1:T + (i + 1) * NT * E1].rearrange("p (t e) -> p t e", t=NT) for i in range(4))
        MX8 = sb("MX8", [P, NT, 8])
        SC = work[0:E1, NJ * (D + E1):NJ * (D + E1) + T]
        IOD = work[0:E1, 0:T]
        TK = sb("TK", [E1, CAP])
        TOK = sb("TOK", [P, NJ])
        IDX = sb("IDX", [P, NJ], I32)
        WS = sb("WS", [P, NJ])
        WT = sb("WT", [E1, CAP])
        AR = sb("AR", [E1, 2, EPT, 8])
        upto = sb("upto", [P, P], BF16)
        all_ones = sb("all_ones", [P, P], BF16)
        expert_base = sb("expert_base", [P, E1])
        slot_rows = sb("slot_rows", [P, NT, TOPK], I32)
        early_qft = QFT[:, :, :].rearrange("p a b -> p (a b)").bitcast(FP32)
        CODE = early_qft[:, 0:NT * E1].rearrange("p (t e) -> p t e", e=E1)
        VALID = early_qft[:, NT * E1:2 * NT * E1].rearrange("p (t e) -> p t e", e=E1)
        MKB = early_qft[:, 2 * NT * E1:2 * NT * E1 + NT * E1 // 2].bitcast(BF16).rearrange("p (t e) -> p t e", e=E1)
        GPD = TOPK // 2
        GY = wgu0[:].rearrange("p (b k n) -> p b k n", b=3, k=GPD)
        WSEL = work[:, NJ * (D + E1):NJ * (D + E1) + ROUNDS * E1].rearrange("p (r q a) -> p r q a", r=ROUNDS, q=QPR)
        YW = XNT[:, 2 * CH:4 * CH].rearrange("p (b j n) -> p b j n", b=2, j=JB)
        SQ = work[:, NJ * (D + E1) + T // 2:NJ * (D + E1) + T // 2 + CH]
        GX = work[:, 0:NJ * (D + E1)].rearrange("p (j n) -> p j n", j=NJ)
        XBT = KFT[:, :, :].rearrange("p a b -> p (a b)").bitcast(FP32)[:, 0:NJ * P].rearrange("p (j n) -> p j n", j=NJ)
        HH = XN[:].rearrange("p t n -> p (t n)")[0:F1, :].rearrange("p (b n) -> p b n", b=4)
        SHH = SG[:].rearrange("p t n -> p (t n)")[0:F1, :]
        later_kft = KFT[:, :, :].rearrange("p a b -> p (a b)").bitcast(FP32)[:, NJ * P:2 * NJ * P]
        later_qft = QFT[:, :, :].rearrange("p a b -> p (a b)").bitcast(FP32)[:, H // 4 * T - 2 * 2 * JB * D:]
        NGU, NDN = 2 * 2 * JB * F1, 2 * JB * D
        wgu = [m.rearrange("p (w h j f) -> p w h j f", w=2, h=2, j=JB) for m in (
            wgu0[:], later_kft[:, 0:NGU], later_kft[:, NGU:2 * NGU])]
        wdn = [m[0:F1].rearrange("p (h j n) -> p h j n", h=2, j=JB) for m in (
            later_qft[:, 0:NDN], later_qft[:, NDN:2 * NDN], later_kft[:, 2 * NGU:2 * NGU + NDN])]

        AOT = [XNT[:], xn]

        def sems(*names):
            return {n: sem(n) for n in names}

        S = sems(
            "consts", "selectors", "dve_step", "pool_step", "out_stored",
            "moe_rows_out", "linear_out", "linear_in")
        weights_in = [sem(f"weights_in{c}") for c in range(3)]
        x_in = [sem(f"x_in{c}") for c in range(NC)]
        gu_in = [sem(f"gate_up_in{c}") for c in range(3)]
        dn_in = [sem(f"down_in{c}") for c in range(3)]
        y_stored = [sem(f"y_stored{c}") for c in range(2)]
        outputs_in = [sem(f"outputs_in{c}") for c in range(3)]
        gathered = [sem(f"gathered{c}") for c in range(ROUNDS)]
        L = [
            {n: sem(f"l{i}_{n}") for n in (
                "var_ready", "std_ready", "xn_ready", "xnT_psum", "xnT_ready", "proj_psum", "qkv_evac",
                "staged", "dup_staged", "featT_psum", "qfeat_evac", "kfeat_evac",
                "ao_ready", "lnT_psum", "lnT_ready", "y_psum", "y_used", "x_done")}
            for i in range(2)]
        A = {n: sem(f"attention_{n}") for n in ("scores", "probs", "sums", "sums_evac", "sumsT")}
        F = sems("gates_psum", "sig_ready", "gates_ready", "gateT_psum", "gateT_ready", "h_psum", "h_act",
                 "gsel_psum", "h_gated", "ffn_silu")
        M = sems("max_scores", "max_done", "minus_max", "mT_psum", "m_rows_a", "m_rows_b")
        R = sems("logits_psum", "logits_evac", "shifted", "exp_ready", "mask_ready", "route_ready", "maskT_psum", "score_ready",
                 "slots_ready", "slotT_psum", "idx_ready", "mask_copied", "xbT_psum", "xbT_ready",
                 "wsel_ready", "wT_psum", "wT_ready", "ws_psum", "ws_ready", "gu_psum", "silu_ready", "h_ready",
                 "y_psum", "y_weighted", "zero_stored", "rank_psum", "rows_ready",
                 "sh_psum", "sh_silu", "sh_ready", "shared_psum", "shared_evac", "z_added", "z_silu")
        N1 = sems("dup_queries", "qk_sq", "qk_norm", "qk_scaled", "g_psum", "g_ready")
        Y = sems("distances", "copied", "product", "logs", "inverse", "sums", "sums_evac", "sumsT", "sumsT_evac",
                 "matrices", "combined")

        x_rows = ins["x"].rearrange("(t p) d -> p t d", p=P)
        out_rows = out.rearrange("(t p) d -> p t d", p=P)
        scratch_rows = scratch.rearrange("(t p) n -> p t n", p=P)
        slot_out_rows = slot_out[1:1 + E1 * CAP, :].rearrange("(e s) d -> s e d", s=CAP)
        wg_v = ins["w_gate"].rearrange("d (h j f) -> d h j f", h=2, j=NJ)
        wu_v = ins["w_up"].rearrange("d (h j f) -> d h j f", h=2, j=NJ)
        wd_v = ins["w_down"].rearrange("f (h j d) -> f h j d", h=2, j=NJ)
        NJB = NJ // JB

        WEIGHTS = [
            [(wqkv0[:, 0:D], ins["Wq0"]), (wqkv0[:, D:D + 32], ins["Wk0"]), (wqkv0[:, D + 32:D + 64], ins["Wv0"]),
             (gate_w[:], ins["gate_W"]),
             (bqkv0[0:1, 0:D], ins["bq0"]), (bqkv0[0:1, D:D + 32], ins["bk0"]), (bqkv0[0:1, D + 32:D + 64], ins["bv0"])],
            [(rscale[:], ins["route_scale"].to_broadcast([P, 1])),
             (w1[:], ins["W1"]), (b1[:], ins["b1"]), (w2[:].rearrange("p m d -> p (m d)"), ins["W2"]),
             (ws1[:], ins["Ws1"]), (bs1[:], ins["bs1"]), (ws2[:], ins["Ws2"]),
             (b2[0:E0], ins["b2"]), (bs2[0:1], ins["bs2"])],
            [(ln_g[:], ins["ln_g"]), (ln_b[:], ins["ln_b"]), (wo[0][:], ins["Wo0"]),
             (wqkv1[:, 0:D], ins["Wq1"]), (wqkv1[:, D:2 * D], ins["Wk1"]), (wqkv1[:, 2 * D:3 * D], ins["Wv1"]),
             (wo[1][:], ins["Wo1"]), (router[:], ins["router"]),
             (wsgu[:], ins["ws_gate_up"]), (wsd[:], ins["ws_down"]), (bo[0][0:1], ins["bo0"]),
             (bqkv1[0:1, 0:D], ins["bq1"]), (bqkv1[0:1, D:2 * D], ins["bk1"]), (bqkv1[0:1, 2 * D:3 * D], ins["bv1"]),
             (bo[1][0:1], ins["bo1"])],
        ]

        STEPS = [(c, g) for c in range(NC) for g in range(NG)]

        def causal_units(c):
            full = [[(2 * m, 0, CH), (2 * m + 1, CH, CH)] for m in range(TPC * c // 2)]
            b = TPC * c
            return full + [[(b, 0, CH), (b + 1, CH, CH - P), (b + 3, 2 * CH - P, P)], [(b + 2, 0, CH - 2 * P)]]

        KSTEPS = [(n, k) for n, (c, g) in enumerate(STEPS) for k in range(len(causal_units(c)))]
        width_of = lambda unit: unit[-1][1] + unit[-1][2]

        MAXIMA = [[(hd, i, kc) for hd in range(HPG) for i in range(TPC) for kc in range(c + 1)] for c, g in STEPS]
        MAX_BASE = np.cumsum([0] + [len(m) for m in MAXIMA]).tolist()

        PIECES = (("logits", 0), ("logits", 1), ("values", 0), ("values", 1), ("logits", 2), ("values", 2),
                  ("logits", 3), ("values", 3))
        NPC = len(PIECES)
        KS_WIDTH = [width_of(causal_units(STEPS[n][0])[k]) for n, k in KSTEPS]
        PIECE_WIDTH = [KS_WIDTH[ks] if what == "logits" else KS_WIDTH[max(ks - 1, 0)]
                       for ks in range(len(KSTEPS)) for what, _ in PIECES]
        FIRST_KS = [ks for ks, (n, k) in enumerate(KSTEPS) if k == 0] + [len(KSTEPS)]

        def maxima_plan():
            plan, first = [], 0
            for n in range(len(STEPS) - 1):
                end = NPC * (FIRST_KS[n + 1] - 1) + 2
                total, at = sum(PIECE_WIDTH[first:end]), 0
                for piece in range(first, end):
                    at += PIECE_WIDTH[piece]
                    plan.append(MAX_BASE[n + 1] + len(MAXIMA[n + 1]) * at // total)
                first = end
            return plan + [MAX_BASE[-1]] * (NPC * len(KSTEPS) - len(plan))

        MAX_PLAN = maxima_plan()
        MAX_OF = [(n, i) for n, m in enumerate(MAXIMA) for i in range(len(m))]

        EARLY_TILES = 8
        LATE_ROUNDS = (NT - EARLY_TILES) // 2
        late_tiles = lambda r: range(EARLY_TILES + 2 * r, EARLY_TILES + 2 * r + 2) if r < LATE_ROUNDS else ()
        SPLIT_AFTER = (3, 5)
        REFINE_AFTER, SCALE_AFTER, RANKS_AFTER, SHARED_AFTER, LINEAR_AFTER = 0, 1, 1, (4, 5), 6

        hidden_step = lambda c, m: NM * c + m + max(0, c - 1)
        down_step = lambda c: NM * min(c + 2, NC) + c
        H_STEPS = down_step(NC - 1) + 1

        ACT_KEYS = (1, 2)
        keys_by_vector = lambda l, tiles: sum(1 for t in range(tiles) if l == 0 or t // TPC not in ACT_KEYS)

        block = ctx.enter_context(nc.Block())

        @block.sync
        def _(sp):
            for c in range(NC):
                sp.dma_start(X[:, c * TPC:(c + 1) * TPC, :], x_rows[:, c * TPC:(c + 1) * TPC, :]).then_inc(x_in[c], 16)
            for group, weights in enumerate(WEIGHTS):
                for i, (dst, src) in enumerate(weights):
                    if group == 0 and i == 4:
                        sp.wait_ge(S["consts"], 1)
                    sp.dma_start(dst, src).then_inc(weights_in[group], 16)
            sp.wait_ge(L[1]["xn_ready"], NC)
            sp.dma_start(scratch_rows[:, :, 0:D], XN[:, :, :]).then_inc(S["moe_rows_out"], 16)
            sp.wait_ge(R["route_ready"], 1)
            sp.dma_start(scratch_rows[:, :, D:D + E1], EX).then_inc(S["moe_rows_out"], 16)
            sp.dma_start(slot_out[0:1, :], first_row[1:2, :]).then_inc(R["zero_stored"], 16)

            def store_outputs(b):
                sp.wait_ge(R["y_weighted"], b + 1)
                for h in range(2):
                    sp.dma_start(slot_out_rows[:, h * NJ + b * JB:h * NJ + (b + 1) * JB, :],
                                 YW[h * CAP:(h + 1) * CAP, b % 2]).then_inc(y_stored[b % 2], 16)

            for b in range(NJB):
                if b >= len(wgu):
                    sp.wait_ge(R["gu_psum"], b - len(wgu) + 1)
                for h in range(2):
                    sp.dma_start(wgu[b % len(wgu)][:, 0, h], wg_v[:, h, b * JB:(b + 1) * JB, :]).then_inc(gu_in[b % len(wgu)], 16)
                    sp.dma_start(wgu[b % len(wgu)][:, 1, h], wu_v[:, h, b * JB:(b + 1) * JB, :]).then_inc(gu_in[b % len(wgu)], 16)
                if b >= len(wdn):
                    sp.wait_ge(R["y_psum"], b - len(wdn) + 1)
                for h in range(2):
                    sp.dma_start(wdn[b % len(wdn)][:, h], wd_v[:, h, b * JB:(b + 1) * JB, :]).then_inc(dn_in[b % len(wdn)], 16)
                if b >= len(wdn):
                    store_outputs(b - len(wdn))
            for b in range(NJB - len(wdn), NJB):
                store_outputs(b)
            sp.wait_ge(N1["g_ready"], 1)
            for h in range(H):
                sp.dma_start(lin[h:h + 1, 0:HD * VW].rearrange("a (i j) -> (a i) j", j=VW),
                             G32[h * HD:(h + 1) * HD, h * VW:(h + 1) * VW]).then_inc(S["linear_out"], 16)
            sp.dma_start(lin[:, HD * VW:V2].rearrange("h (a j) -> a h j", a=1), GC[:].rearrange("p (h j) -> p h j", j=VW)).then_inc(S["linear_out"], 16)
            sp.wait_ge(S["linear_out"], 16 * (H + 1))
            sp.dma_start(LROW, lin.rearrange("(a h) n -> a h n", a=1).to_broadcast([P, H, V2])).then_inc(S["linear_in"], 16)
            for c in range(NC):
                sp.wait_ge(L[1]["x_done"], c + 1)
                sp.dma_start(out_rows[:, c * TPC:(c + 1) * TPC, :], X[:, c * TPC:(c + 1) * TPC, :]).then_inc(S["out_stored"], 16)
            sp.wait_ge(S["out_stored"], 16 * NC)

        @block.gpsimd
        def _(pool):
            n_pool = [0]

            def step(ins_):
                n_pool[0] += 1
                ins_.then_inc(S["pool_step"], 1)
                pool.wait_ge(S["pool_step"], n_pool[0])

            for m in (bqkv0, b2, bs2, bo[0], bqkv1, bo[1], identb, first_row, ident):
                last = pool.memset(m[:], 0.0)
            step(last)
            pool.memset(first_row[0:1, :], 1.0)
            for m in (ident, identb):
                last = pool.affine_select(out=m[:], in_=m[:], compare_op=ALU.not_equal, fill=1.0, base=0,
                                          pattern=[[-1, P]], channel_multiplier=1)
            last.then_inc(S["consts"], 1)
            pool.memset(gsel[:], 0.0)
            pool.memset(gateT, 0.0)
            pool.memset(VA[:], 1.0)
            step(pool.memset(gates[:], -1e30))
            gs = gsel[0:E0].rearrange("e m (h r) -> e (m h) r", h=2)
            pool.affine_select(out=gs, in_=gs, compare_op=ALU.not_equal, fill=1.0, base=0,
                               pattern=[[-1, E0], [0, F0]], channel_multiplier=1).then_inc(S["consts"], 1)
            pool.memset(mask_qk[:], 0.0)
            pool.memset(mask_kq[:], 0.0)
            pool.memset(ones_col[:], 1.0)
            pool.memset(MF[:], 0.0)
            for m in (expert_row, row_slot):
                pool.memset(m[:], 0.0)
            for m in (expert_tile, row_expert):
                pool.memset(m[:], 1.0)
            step(pool.memset(KFT[:, 0:KV0, :].rearrange("p a n -> p (a n)").bitcast(FP32), 0.0))
            pool.affine_select(out=mask_qk[:], in_=mask_qk[:], compare_op=ALU.is_ge, fill=MASKED, base=0,
                               pattern=[[-1, P]], channel_multiplier=1)
            pool.affine_select(out=mask_kq[:], in_=mask_kq[:], compare_op=ALU.is_ge, fill=MASKED, base=0,
                               pattern=[[1, P]], channel_multiplier=-1).then_inc(S["consts"], 1)

            def gather_selectors():
                for q in range(QPR):
                    step(pool.affine_select(out=expert_row[:], in_=expert_row[:], compare_op=ALU.not_equal, fill=1.0, base=-EPT * q,
                                            pattern=[[-1, EPT], [0, 8]], channel_multiplier=1))
                pool.affine_select(out=expert_tile[:], in_=expert_tile[:], compare_op=ALU.is_ge, fill=0.0, base=0,
                                   pattern=[[-EPT, QPR]], channel_multiplier=1)
                step(pool.affine_select(out=row_expert[:], in_=row_expert[:], compare_op=ALU.is_ge, fill=0.0, base=0,
                                        pattern=[[-8, EPT]], channel_multiplier=1))
                pool.affine_select(out=expert_tile[:], in_=expert_tile[:], compare_op=ALU.is_ge, fill=0.0, base=EPT - 1,
                                   pattern=[[EPT, QPR]], channel_multiplier=-1)
                pool.affine_select(out=row_expert[:], in_=row_expert[:], compare_op=ALU.is_ge, fill=0.0, base=7,
                                   pattern=[[8, EPT]], channel_multiplier=-1)
                pool.iota(expert_base[:], pattern=[[CAP, E1]], base=0, channel_multiplier=0, allow_small_or_imprecise_dtypes=True)
                step(pool.memset(upto[:], 1.0))
                pool.affine_select(out=upto[:], in_=upto[:], compare_op=ALU.is_ge, fill=0.0, base=0,
                                   pattern=[[1, P]], channel_multiplier=-1)
                pool.memset(all_ones[:], 1.0)
                for a in range(EPT):
                    step(pool.affine_select(out=row_slot[:], in_=row_slot[:], compare_op=ALU.not_equal, fill=1.0, base=-8 * a,
                                            pattern=[[-1, 8]], channel_multiplier=1))

            def init_stage(l):
                if l == 1:
                    pool.wait_ge(R["xbT_psum"], NJB)
                    pool.wait_ge(R["ws_ready"], 1)
                qv = QF.rearrange("p b t (h n) -> p (b t h) n", n=64)
                kv = KF.rearrange("p b t (h n) -> p (b t h) n", n=64)
                for v in (qv, kv):
                    pool.memset(v[:, :, 0:8], 0.0)
                    step(pool.memset(v[:, :, 56:64], 0.0))
                nk = H if l else KV0
                if l == 0:
                    for b in range(2):
                        last = pool.memset(KF[:, b, :, 0:nk * 64].rearrange("p t (h n) -> p t h n", n=64)[:, :, :, 0:2], 1.0)
                else:
                    pool.memset(kv[:, :, 0:3], 1.0)
                    parts, rest = [], np.float32(YAT_TOP)
                    for _ in range(3):
                        bits = np.frombuffer(np.float32(rest).tobytes(), np.uint32)[0]
                        part = np.frombuffer(np.uint32(bits & 0xFFFF0000).tobytes(), np.float32)[0]
                        parts.append(float(part))
                        rest = np.float32(rest - part)
                    for i, v in enumerate(parts):
                        last = pool.memset(qv[:, :, i:i + 1], v)
                last.then_inc(L[l]["dup_staged"], 1)

            def duplicates(l, c):
                nk = H if l else KV0
                pool.wait_ge(L[l]["staged"], c + 1)
                q = QF[:, c % 2].rearrange("p t (h n) -> p (t h) n", n=64)
                if l == 0:
                    pool.tensor_copy(q[:, :, 16:24], q[:, :, 8:16])
                    pool.tensor_copy(q[:, :, 32:40], q[:, :, 8:16])
                pool.tensor_copy(q[:, :, 48:56], q[:, :, 24:32])
                k = KF[:, c % 2, :, 0:nk * 64].rearrange("p t (h n) -> p t h n", n=64)
                pool.tensor_copy(k[:, :, :, 24:32], k[:, :, :, 8:16])
                last = pool.tensor_copy(k[:, :, :, 40:48], k[:, :, :, 8:16])
                if l == 0:
                    last = pool.tensor_copy(k[:, :, :, 48:56], k[:, :, :, 16:24])
                last.then_inc(L[l]["dup_staged"], 1)

            init_stage(0)
            for c in range(NC):
                duplicates(0, c)
            pool.wait_ge(F["h_act"], H_STEPS)
            pool.iota(iota[:], pattern=[[1, T]], base=0, channel_multiplier=0,
                      allow_small_or_imprecise_dtypes=True)
            gather_selectors()
            pool.sem_inc(S["selectors"], 1)

            pool.wait_ge(R["route_ready"], 1)
            step(pool.tensor_copy(MKB, MK))
            pool.sem_inc(R["mask_copied"], 1)
            pool.wait_ge(S["moe_rows_out"], 32)
            for r in range(ROUNDS):
                pool.wait_ge(R["idx_ready"], r + 1)
                for j in range(r * QPR, (r + 1) * QPR):
                    pool.indirect_dma_start(
                        out=GX[:, j, :], out_offset=None, in_=scratch[:, :],
                        in_offset=bass.IndirectOffsetOnAxis(ap=IDX[:, j:j + 1].bitcast(U32), axis=0),
                    ).then_inc(gathered[r], 16)
            for b in range(NJB):
                pool.wait_ge(R["silu_ready"], b + 1)
                pool.tensor_tensor(HH[:, 2 + b % 2, :], HH[:, 2 + b % 2, :], HH[:, b % 2, :], ALU.mult).then_inc(R["h_ready"], 1)
                if b == 0:
                    init_stage(1)
            for c in range(NC):
                duplicates(1, c)
            pool.wait_ge(S["linear_in"], 16)

            def pair_matrices(h):
                if h >= 1:
                    pool.wait_ge(Y["matrices"], h)
                if h >= 2:
                    pool.wait_ge(Y["sums"], NC * MP * (h - 1))
                V3 = VA[:, :, h * VW:(h + 1) * VW].rearrange("p (m b) j -> p m b j", b=2)
                K3 = K32[:, :, h * HD:(h + 1) * HD].rearrange("p (m b) i -> p m b i", b=2)
                m_ = MM[:, h % 2].rearrange("p m (i j) -> p m i j", j=VW)
                t_ = MT.rearrange("p m (i j) -> p m i j", j=VW)
                for b, dst in ((0, m_), (1, t_)):
                    pool.tensor_tensor(dst[:, :, 0:HD, :], V3[:, :, b, :].unsqueeze(2).to_broadcast([P, MP, HD, VW]),
                                       K3[:, :, 1 - b, :].unsqueeze(3).to_broadcast([P, MP, HD, VW]), ALU.mult)
                    last = pool.tensor_scalar(dst[:, :, HD, :], V3[:, :, b, :], YAT_TOP, None, ALU.mult)
                step(last)
                pool.tensor_tensor(MM[:, h % 2], MM[:, h % 2], MT, ALU.add).then_inc(Y["matrices"], 1)

            def combine(i):
                h, c = divmod(i, NC)
                pool.wait_ge(Y["sumsT_evac"], i + 1)
                t_ = TT[:, i % 2, :].rearrange("p (q i j) -> p q i j", q=TPC, j=VW)
                step(pool.tensor_tensor(TT[:, i % 2, :].rearrange("p (q n) -> p q n", n=V2), TT[:, i % 2, :].rearrange("p (q n) -> p q n", n=V2),
                                        LROW[:, h, :].unsqueeze(1).to_broadcast([P, TPC, V2]), ALU.add))
                step(pool.tensor_tensor(t_[:, :, 0:HD], t_[:, :, 0:HD],
                                        Q32[:, c * TPC:(c + 1) * TPC, h * HD:(h + 1) * HD].unsqueeze(3).to_broadcast([P, TPC, HD, VW]),
                                        ALU.mult))
                step(pool.tensor_tensor(t_[:, :, 0:4], t_[:, :, 0:4], t_[:, :, 4:8], ALU.add))
                step(pool.tensor_tensor(t_[:, :, 0:2], t_[:, :, 0:2], t_[:, :, 2:4], ALU.add))
                step(pool.tensor_tensor(t_[:, :, 0], t_[:, :, 0], t_[:, :, 1], ALU.add))
                ts = slice(c * TPC, (c + 1) * TPC)
                pool.tensor_tensor(NUM[:, ts, h, :], t_[:, :, 0, 0:HD], t_[:, :, HD, 0:HD], ALU.add)
                pool.tensor_tensor(DEN[:, ts, h], t_[:, :, 0, HD], t_[:, :, HD, HD], ALU.add).then_inc(Y["combined"], 1)

            def gather_outputs(i):
                t, half = divmod(i, 2)
                for k in range(GPD):
                    pool.indirect_dma_start(
                        out=GY[:, i % 3, k, :], out_offset=None, in_=slot_out[:, :],
                        in_offset=bass.IndirectOffsetOnAxis(ap=slot_rows[:, t, half * GPD + k:half * GPD + k + 1].bitcast(U32), axis=0),
                    ).then_inc(outputs_in[i % 3], 16)

            def add_outputs(i):
                t = i // 2
                pool.wait_ge(outputs_in[i % 3], 16 * GPD * (i // 3 + 1))
                step(pool.tensor_tensor(GY[:, i % 3, 0:2], GY[:, i % 3, 0:2], GY[:, i % 3, 2:4], ALU.add))
                step(pool.tensor_tensor(GY[:, i % 3, 0], GY[:, i % 3, 0], GY[:, i % 3, 1], ALU.add))
                step(pool.tensor_tensor(SG[:, t, :], SG[:, t, :], GY[:, i % 3, 0], ALU.add))

            pair_matrices(0)
            pair_matrices(1)
            pool.wait_ge(R["rows_ready"], 1)
            pool.wait_ge(R["zero_stored"], 16)
            for b in range(2):
                pool.wait_ge(y_stored[b], 32 * NJB // 2)
            pool.wait_ge(R["shared_evac"], NC)
            for i in range(H * NC):
                combine(i)
                if i < 2 * NT:
                    gather_outputs(i)
                if 2 <= i < 2 * NT + 2:
                    add_outputs(i - 2)
                if i == 2 * NT + 1:
                    pool.sem_inc(R["z_added"], 1)
                if i % NC == NC - 1 and i // NC + 2 < H:
                    pair_matrices(i // NC + 2)

        @block.scalar
        def _(act):
            def norm(l):
                act.wait_ge(L[l]["var_ready"], 1)
                act.activation(nrm[:, 1, 0:NT], nrm[:, 0, 0:NT], ACT.Sqrt).then_inc(L[l]["std_ready"], 1)
                for c in range(NC):
                    act.wait_ge(L[l]["xnT_psum"], c + 1)
                    act.copy(XNT[:, c * CH:(c + 1) * CH], bank[c % 2][:]).then_inc(L[l]["xnT_ready"], 1)

            def evacuate_qkv(l, scale, nk, tiles, src_of):
                for t in tiles:
                    src = src_of(t)
                    act.wait_ge(L[l]["proj_psum"], t + 1)
                    act.activation(Q32[:, t, :], src[:, 0:D], ACT.Copy, scale=scale)
                    act.copy(K32[:, t, 0:nk * HD], src[:, D:D + nk * HD])
                    act.copy(VA[:, t, 0:nk * VW].rearrange("p (h n) -> p h n", n=VW)[:, :, 0:HD],
                             src[:, D + nk * HD:D + 2 * nk * HD].rearrange("p (h n) -> p h n", n=HD)).then_inc(L[l]["qkv_evac"], 1)

            def evacuate_features(l, c):
                for t in range(c * TPC, (c + 1) * TPC):
                    act.wait_ge(L[l]["featT_psum"], t + 1)
                    src = pair_bank[t % 2][:, 0, :].bitcast(BF16).rearrange("p (a n) -> p a n", n=P)
                    last = act.copy(QFT[:, :, t * P:(t + 1) * P], src)
                    if l == 1 and c in ACT_KEYS:
                        last = act.copy(KFT[:, :, t * P:(t + 1) * P],
                                        pair_bank[t % 2][:, 1, :].bitcast(BF16).rearrange("p (a n) -> p a n", n=P))
                    last.then_inc(L[l]["qfeat_evac"], 1)

            def duplicates(c):
                act.wait_ge(L[1]["staged"], c + 1)
                q = QF[:, c % 2].rearrange("p t (h n) -> p (t h) n", n=64)
                act.copy(q[:, :, 16:24], q[:, :, 8:16])
                act.copy(q[:, :, 32:40], q[:, :, 8:16]).then_inc(N1["dup_queries"], 1)

            norm(0)

            act.wait_ge(F["gates_psum"], 1)
            act.activation(gates[:, :, 0:E0], bank[2][:, 0:NT * E0].rearrange("p (t e) -> p t e", e=E0),
                           ACT.Sigmoid).then_inc(F["sig_ready"], 1)
            evacuate_qkv(0, float(HD) ** -0.5, KV0, range(NT), lambda t: bank[t % 2])
            act.wait_ge(F["gateT_psum"], 1)
            for c in range(NC):
                act.wait_ge(F["gateT_psum"], c + 1)
                act.copy(gateT[0:E0, c * CH:(c + 1) * CH], bank[c % 2][0:E0, :]).then_inc(F["gateT_ready"], 1)
            def ffn_out(c):
                i = down_step(c)
                act.wait_ge(F["h_psum"], i + 1)
                act.copy(SG[:, c * TPC:(c + 1) * TPC, :], bank[i % 2][:].rearrange("p (t n) -> p t n", n=D)).then_inc(F["h_act"], 1)

            for c in range(NC + 1):
                for m in range(NM if c < NC else 0):
                    rows = P if m < NM - 1 else F0
                    i = hidden_step(c, m)
                    act.wait_ge(F["h_psum"], i + 1)
                    act.activation(HT(c, m)[0:rows, :], bank[i % 2][0:rows, :], ACT.Gelu,
                                   bias=b1[:, m:m + 1] if m < NM - 1 else bs1[:]).then_inc(F["h_act"], 1)
                if c >= 1:
                    ffn_out(c - 1)
                    evacuate_features(0, c - 1)

            act.preload_act_table_set("natural_log_exp_and_others")

            def m_rows(n):
                c, g = STEPS[n]
                act.wait_ge(M["mT_psum"], n + 1)
                src = bank[3][:, :].bitcast(BF16).rearrange("p (a n) -> p a n", n=CH)
                act.copy(QFT[0:2, 2 * g:2 * g + 2, c * CH:(c + 1) * CH], src[0:2]).then_inc(M["m_rows_a"], 1)

            def evacuate_sums(n):
                act.wait_ge(A["sums"], FIRST_KS[n + 1])
                if n >= 2:
                    act.wait_ge(A["sumsT"], n - 1)
                act.copy(OT[:, n % 2, :], bank[2][:]).then_inc(A["sums_evac"], 1)

            m_rows(0)
            for ks, (n, k) in enumerate(KSTEPS):
                c, g = STEPS[n]
                w = width_of(causal_units(c)[k])
                for hd in range(HPG):
                    if hd == 3 and k == len(causal_units(c)) - 1 and n + 1 < len(STEPS):
                        m_rows(n + 1)
                    u = HPG * ks + hd
                    act.wait_ge(A["scores"], u + 1)
                    if ks >= 2 and hd == 0:
                        act.wait_ge(A["sums"], ks - 1)
                    act.activation(WORK[:, ks % 2, hd * 2 * CH:hd * 2 * CH + w],
                                   pair_bank[u % 2][:].rearrange("p a b -> p (a b)")[:, 0:w],
                                   ACT.Exp).then_inc(A["probs"], 1)
                if k == 0 and n >= 1:
                    evacuate_sums(n - 1)
            evacuate_sums(len(STEPS) - 1)

            def end_layer(l):
                for c in range(NC):
                    act.wait_ge(L[l]["lnT_psum"], c + 1)
                    if l == 0:
                        act.activation(XNT[:, c * CH:(c + 1) * CH], bank[c % 2][:], ACT.Identity, bias=ln_b[:],
                                       scale=ln_g[:]).then_inc(L[l]["lnT_ready"], 1)
                    else:
                        act.copy(AOT[1][:, c * CH:(c + 1) * CH], bank[c % 2][:]).then_inc(L[l]["lnT_ready"], 1)

            act.wait_ge(L[0]["ao_ready"], len(STEPS) + 1)
            act.activation(nrm[:, 1, 0:NT], nrm[:, 0, 0:NT], ACT.Sqrt).then_inc(L[0]["std_ready"], 1)
            act.activation(SG[:], SG[:], ACT.Silu).then_inc(F["ffn_silu"], 1)
            end_layer(0)

            norm(1)
            for b in range(2):
                act.wait_ge(R["logits_psum"], b + 1)
                act.copy(LG[:, 8 * b:8 * b + 8, :], bank[b][:].rearrange("p (t e) -> p t e", e=E1)).then_inc(R["logits_evac"], 1)
            pair_side = lambda t: pair_bank[t % 2][:, 0, :]
            evacuate_qkv(1, 1.0, H, range(0, EARLY_TILES), pair_side)
            act.wait_ge(R["shifted"], 1)
            act.activation(EX, EX, ACT.Exp).then_inc(R["exp_ready"], 1)
            def shared_silu(c):
                act.wait_ge(R["sh_psum"], c + 1)
                if c >= 2:
                    act.wait_ge(R["sh_ready"], c - 1)
                act.activation(HH[:, c % 2, :], pair_bank[c % 2][0:F1, 0, :], ACT.Silu).then_inc(R["sh_silu"], 1)

            act.wait_ge(S["moe_rows_out"], 32)
            for r in range(ROUNDS + 2):
                evacuate_qkv(1, 1.0, H, late_tiles(r), pair_side)
                if r - LATE_ROUNDS in (0, 1):
                    shared_silu(r - LATE_ROUNDS)
                b = r - 2
                if b >= 0:
                    act.wait_ge(R["xbT_psum"], b + 1)
                    act.copy(XBT[:, b * JB:(b + 1) * JB, :].rearrange("p j n -> p (j n)"), bank[2 + b % 2][:]).then_inc(R["xbT_ready"], 1)
            shared_silu(2)
            shared_silu(3)
            act.wait_ge(N1["qk_sq"], 1)
            act.activation(nrm[:, 1, :], nrm[:, 0, :], ACT.Sqrt).then_inc(N1["qk_norm"], 1)
            for b in range(NJB):
                act.wait_ge(R["gu_psum"], b + 1)
                if b < 2:
                    act.wait_ge(R["sh_ready"], NC)
                else:
                    act.wait_ge(R["h_ready"], b - 1)
                act.activation(HH[:, b % 2, :], pair_bank[b % 2][0:F1, 0, :], ACT.Silu)
                if b >= 2:
                    act.wait_ge(R["y_psum"], b - 1)
                act.copy(HH[:, 2 + b % 2, :], pair_bank[b % 2][0:F1, 1, :]).then_inc(R["silu_ready"], 1)
                if b == SPLIT_AFTER[0] + 2:
                    duplicates(0)
                if b in SHARED_AFTER:
                    for c in range(2 * SHARED_AFTER.index(b), 2 * SHARED_AFTER.index(b) + 2):
                        act.wait_ge(R["shared_psum"], c + 1)
                        act.copy(SG[:, c * TPC:(c + 1) * TPC, :], bank[c % 2][:].rearrange("p (t n) -> p t n", n=D)).then_inc(R["shared_evac"], 1)
            duplicates(1)
            for c in range(NC):
                evacuate_features(1, c)
                if c + 2 < NC:
                    duplicates(c + 2)
            act.preload_act_table_set("natural_log_exp_and_others")
            def evacuate_pair_sums(i):
                act.wait_ge(Y["sums"], MP * (i + 1))
                if i >= 2:
                    act.wait_ge(Y["sumsT"], i - 1)
                act.copy(TS[:, i % 2, :], bank[i % 2][0:V2, :]).then_inc(Y["sums_evac"], 1)

            def evacuate_transposed(i):
                act.wait_ge(Y["sumsT"], i + 1)
                if i >= 2:
                    act.wait_ge(Y["combined"], i - 1)
                act.copy(TT[:, i % 2, :], bank[2 + i % 2][:, 0:TPC * V2]).then_inc(Y["sumsT_evac"], 1)

            NB = NU // UB
            BPI = MP // UB
            for b in range(NB + 3):
                if b < NB:
                    act.wait_ge(Y["product"], UB * (b + 1))
                    w = PW[:, b % NPW, :, :].rearrange("p a n -> p (a n)")
                    act.activation(w, w, ACT.Ln, scale=1.0 / YAT_A).then_inc(Y["logs"], 1)
                    act.wait_ge(Y["logs"], b + 1)
                    act.activation(w, w, ACT.Exp, scale=-1.0).then_inc(Y["inverse"], 1)
                done = b - 2
                if done >= 0 and done % BPI == BPI - 1:
                    evacuate_pair_sums(done // BPI)
                done = b - 4
                if done >= 0 and done % BPI == BPI - 1:
                    evacuate_transposed(done // BPI)
            evacuate_transposed(NU // MP - 1)
            act.wait_ge(R["z_added"], 1)
            act.activation(SG[:], SG[:], ACT.Silu).then_inc(R["z_silu"], 1)
            end_layer(1)

        @block.vector
        def _(dve):
            n_dve = [0]

            def step(ins_):
                n_dve[0] += 1
                ins_.then_inc(S["dve_step"], 1)
                dve.wait_ge(S["dve_step"], n_dve[0])

            def refine(n, add):
                v, s, r, y = (nrm[:, i, 0:n] for i in range(4))
                step(dve.tensor_scalar(s, s, 1e-30, None, ALU.max))
                step(dve.reciprocal(r, s))
                step(dve.tensor_tensor(y, v, r, ALU.mult))
                step(dve.tensor_tensor(y, y, s, ALU.add))
                step(dve.tensor_scalar(y, y, 0.5, add, ALU.mult, ALU.add))
                step(dve.reciprocal(y, y))

            def stats(src, l, c):
                for t in range(c * TPC, (c + 1) * TPC):
                    last = dve.bn_stats(st[:, t, :], src[:, t, :])
                step(last)
                for t in range(c * TPC, (c + 1) * TPC):
                    last = dve.bn_aggr(mv[:, t, :], st[:, t, :])
                step(last)

            def layernorm(l, src, dst, var_sem, std_wait, done_sem):
                step(dve.tensor_scalar(nrm[:, 0, 0:NT], mv[:, :, 1], LN_EPS, None, ALU.add))
                dve.sem_inc(var_sem, 1)
                dve.wait_ge(L[l]["std_ready"], std_wait)
                refine(NT, 0.0)
                for t in range(NT):
                    last = dve.tensor_scalar(dst[:, t, :], src[:, t, :], mv[:, t, 0:1], nrm[:, 3, t:t + 1],
                                             ALU.subtract, ALU.mult)
                    if t % TPC == TPC - 1:
                        last.then_inc(done_sem, 1)

            def split_features(l, nk, c):
                ts = slice(c * TPC, (c + 1) * TPC)
                dve.wait_ge(L[l]["dup_staged"], 1)
                if c >= 2:
                    dve.wait_ge(L[l]["featT_psum"], TPC * (c - 1))
                q = QF[:, c % 2].rearrange("p t (h n) -> p (t h) n", n=64)
                k = KF[:, c % 2, :, 0:nk * 64].rearrange("p t (h n) -> p t h n", n=64)
                qs = Q32[:, ts, :].rearrange("p t (h n) -> p (t h) n", n=HD)
                ks = K32[:, ts, 0:nk * HD].rearrange("p t (h n) -> p t h n", n=HD)
                rq = split_rest[l][:, 0:TPC, :].rearrange("p t (h n) -> p (t h) n", n=HD)
                rk = split_rest[l][:, TPC:, 0:nk * HD].rearrange("p t (h n) -> p t h n", n=HD)
                for part, (qa, ka) in enumerate(((8, 8), (24, 16), (40, 32))):
                    dve.tensor_copy(q[:, :, qa:qa + 8], qs)
                    last = dve.tensor_copy(k[:, :, :, ka:ka + 8], ks)
                    if part < 2:
                        step(last)
                        dve.tensor_tensor(rq, qs, q[:, :, qa:qa + 8], ALU.subtract)
                        step(dve.tensor_tensor(rk, ks, k[:, :, :, ka:ka + 8], ALU.subtract))
                        qs, ks = rq, rk
                if l == 1:
                    last = dve.tensor_copy(k[:, :, :, 48:56], k[:, :, :, 16:24])
                last.then_inc(L[l]["staged"], 1)

            def evacuate_kfeatures(l, nk, c):
                for t in range(c * TPC, (c + 1) * TPC):
                    dve.wait_ge(L[l]["featT_psum"], t + 1)
                    src = pair_bank[t % 2][:, 1, :].bitcast(BF16)[:, 0:nk * 64].rearrange("p (a n) -> p a n", n=P)
                    if l == 0:
                        dve.tensor_copy(KFT[0:64, 0:nk:2, t * P:(t + 1) * P], src[0:64])
                        dve.tensor_copy(KFT[64:128, 1:nk:2, t * P:(t + 1) * P], src[64:128]).then_inc(L[l]["kfeat_evac"], 1)
                    else:
                        dve.tensor_copy(KFT[:, 0:nk // 2, t * P:(t + 1) * P], src).then_inc(L[l]["kfeat_evac"], 1)

            for c in range(NC):
                dve.wait_ge(x_in[c], 16)
                stats(X, 0, c)
            layernorm(0, X, XN, L[0]["var_ready"], 1, L[0]["xn_ready"])
            dve.wait_ge(S["consts"], 2)

            dve.wait_ge(F["sig_ready"], 1)
            dve.wait_ge(weights_in[1], 16 * len(WEIGHTS[1]))
            step(dve.tensor_scalar(gates[:, :, 0:E0], gates[:, :, 0:E0], rscale[:], None, ALU.mult))
            for t in range(NT):
                last = dve.max(MX8[:, t, :], gates[:, t, 0:E0])
            step(last)
            step(dve.tensor_tensor(nrm[:, 0, 0:NT], MX8[:, :, 0], MX8[:, :, 1], ALU.add))
            step(dve.reciprocal(nrm[:, 1, 0:NT], nrm[:, 0, 0:NT]))
            step(dve.memset(MX8[:, :, 2:8], -1e30))
            for t in range(NT):
                last = dve.match_replace(small[:, t, 0:E0 + 6], MX8[:, t, :], gates[:, t, :], 2e30)
            step(last)
            step(dve.tensor_scalar(small[:, :, 16:24], small[:, :, 0:E0], 1e30, None, ALU.is_gt))
            step(dve.tensor_tensor(small[:, :, 16:24], small[:, :, 16:24], gates[:, :, 0:E0], ALU.mult))
            dve.tensor_tensor(gatew[:], small[:, :, 16:24],
                              nrm[:, 1, 0:NT].unsqueeze(2).to_broadcast([P, NT, E0]), ALU.mult).then_inc(F["gates_ready"], 1)
            dve.wait_ge(L[0]["qkv_evac"], NT)
            for c in range(NC):
                for m in range(NM - 1):
                    i = (NM - 1) * c + m
                    dve.wait_ge(F["h_act"], hidden_step(c, m) + 1)
                    dve.wait_ge(F["gsel_psum"], i + 1)
                    dve.tensor_tensor(HT(c, m), HT(c, m), bank[2 + i % 2][:], ALU.mult).then_inc(F["h_gated"], 1)

                split_features(0, KV0, c)
                if c >= 1:
                    evacuate_kfeatures(0, KV0, c - 1)
            evacuate_kfeatures(0, KV0, NC - 1)

            def maxima(lo, hi):
                for u in range(lo, hi):
                    n, i = MAX_OF[u]
                    hd, qt, kc = MAXIMA[n][i]
                    c, g = STEPS[n]
                    w = CH if kc < c else (qt + 1) * P
                    dve.wait_ge(M["max_scores"], u + 1)
                    dve.reduce_max(MX[:, n % 2, hd * TPC + qt, kc:kc + 1], bank[u % 2][:, 0:w], AX.X).then_inc(M["max_done"], 1)

            def minus_max(n):
                c, g = STEPS[n]
                dve.wait_ge(M["max_done"], MAX_BASE[n + 1])
                m32 = small[:, 0, 0:16]
                m3 = m32.rearrange("p (a b) -> p a b", a=HPG)
                step(dve.tensor_reduce(m32, MX[:, n % 2, :, 0:c + 1], axis=AX.X, op=ALU.max))
                step(dve.tensor_scalar(m32, m32, -1.0, None, ALU.mult))
                if n >= 1:
                    dve.wait_ge(M["mT_psum"], n)
                hi = MF[:].rearrange("p t a (e n) -> p (a e) t n", n=64)
                step(dve.tensor_copy(hi[:, :, :, 0], m3))
                dve.tensor_tensor(hi[:, :, :, 1], m3, hi[:, :, :, 0], ALU.subtract).then_inc(M["minus_max"], 1)

            def max_rows(n):
                c, g = STEPS[n]
                dve.wait_ge(M["mT_psum"], n + 1)
                src = bank[3][:, :].bitcast(BF16).rearrange("p (a n) -> p a n", n=CH)
                dve.tensor_copy(QFT[64:66, 2 * g:2 * g + 2, c * CH:(c + 1) * CH], src[64:66]).then_inc(M["m_rows_b"], 1)

            def normalize(n):
                c, g = STEPS[n]
                dve.wait_ge(A["sumsT"], n + 1)
                src = bank[3][:].rearrange("p (t h n) -> p t h n", t=TPC, n=32)
                den = small[:, 1, 0:16].rearrange("p (t h) -> p t h", t=TPC)
                step(dve.reciprocal(den, src[:, :, :, HD]))
                dst = AO[:, c * TPC:(c + 1) * TPC, g * 32:(g + 1) * 32].rearrange("p t (h n) -> p t h n", n=HD)
                dve.tensor_tensor(dst, src[:, :, :, 0:HD], den.unsqueeze(3).to_broadcast([P, TPC, HPG, HD]),
                                  ALU.mult).then_inc(L[0]["ao_ready"], 1)

            maxima(0, MAX_BASE[1])
            minus_max(0)
            max_rows(0)
            for n in range(len(STEPS) + 1):
                first = NPC * FIRST_KS[n]
                done = MAX_PLAN[first - 1] if n >= 1 else MAX_BASE[1]
                if n < len(STEPS):
                    maxima(done, MAX_PLAN[first + NPC])
                if n >= 1:
                    normalize(n - 1)
                if n == len(STEPS) - 1:
                    dve.wait_ge(L[0]["ao_ready"], n)
                    for c in range(NC - 1):
                        stats(AO, 0, c)
                if n + 1 < len(STEPS):
                    last = NPC * (FIRST_KS[n + 1] - 1)
                    maxima(MAX_PLAN[first + NPC], MAX_BASE[n + 2])
                    minus_max(n + 1)
                    maxima(MAX_BASE[n + 2], MAX_PLAN[last + 4])
                    max_rows(n + 1)
                    maxima(MAX_PLAN[last + 4], MAX_PLAN[last + NPC - 1])

            def add_branches(l):
                for c in range(NC):
                    ts = slice(c * TPC, (c + 1) * TPC)
                    dve.wait_ge(L[l]["y_psum"], c + 1)
                    dve.tensor_tensor(AO[:, ts, :], bank[2 + c % 2][:].rearrange("p (t n) -> p t n", n=D), SG[:, ts, :],
                                      ALU.mult).then_inc(L[l]["y_used"], 1)
                    dve.wait_ge(L[l]["y_used"], c + 1)
                    dve.tensor_tensor(X[:, ts, :], X[:, ts, :], AO[:, ts, :], ALU.add).then_inc(L[l]["x_done"], 1)
                    if l == 0:
                        dve.wait_ge(L[0]["x_done"], c + 1)
                        stats(X, 1, c)

            dve.wait_ge(L[0]["ao_ready"], len(STEPS))
            stats(AO, 0, NC - 1)
            layernorm(0, AO, AO, L[0]["ao_ready"], 2, L[0]["ao_ready"])
            dve.wait_ge(F["ffn_silu"], 1)
            add_branches(0)

            layernorm(1, X, XN, L[1]["var_ready"], 1, L[1]["xn_ready"])

            n1 = NT * H
            flat = [a[:].rearrange("p t n -> p (t n)") for a in (Q32, K32)]

            def squares():
                dve.wait_ge(L[1]["qkv_evac"], NT)
                for i, src in enumerate(flat):
                    for c in range(NC):
                        at = i * n1 + c * TPC * H
                        step(dve.tensor_tensor(SQ, src[:, c * CH:(c + 1) * CH], src[:, c * CH:(c + 1) * CH], ALU.mult))
                        step(dve.tensor_reduce(nrm[:, 0, at:at + TPC * H], SQ.rearrange("p (a n) -> p a n", n=HD), axis=AX.X, op=ALU.add))
                dve.sem_inc(N1["qk_sq"], 1)

            def scale_queries_keys():
                for i, (src, sign) in enumerate(zip(flat, (1.0, -1.0))):
                    s3 = src.rearrange("p (a n) -> p a n", n=HD)
                    dve.scalar_tensor_tensor(s3, s3, sign, nrm[:, 3, i * n1:(i + 1) * n1].unsqueeze(2).to_broadcast([P, n1, HD]),
                                             ALU.mult, ALU.mult).then_inc(N1["qk_scaled"], 1)
                dve.wait_ge(N1["qk_scaled"], 2)

            def find_slot_rows():
                for half in range(2):
                    ts = slice(half * NT // 2, (half + 1) * NT // 2)
                    rank = bank[half][:].rearrange("p (t e) -> p t e", e=E1)
                    dve.wait_ge(R["rank_psum"], half + 1)
                    dve.scalar_tensor_tensor(VALID[:, ts], rank, CAP + 0.5, MKB[:, ts], ALU.is_le, ALU.mult)
                    step(dve.tensor_tensor(CODE[:, ts], rank, expert_base[:].unsqueeze(1).to_broadcast([P, NT // 2, E1]), ALU.add))
                    step(dve.tensor_tensor(CODE[:, ts], CODE[:, ts], VALID[:, ts], ALU.mult))
                for t in range(NT):
                    last = dve.max(MX8[:, t, :], CODE[:, t, :])
                step(last)
                dve.tensor_copy(slot_rows[:], MX8[:]).then_inc(R["rows_ready"], 1)

            dve.wait_ge(S["selectors"], 1)
            step(dve.tensor_scalar(IOD, iota[0:E1, :], -1.0, float(T), ALU.mult, ALU.add))
            dve.wait_ge(R["logits_evac"], 2)
            for t in range(NT):
                last = dve.max(MX8[:, t, :], LG[:, t, :])
            step(last)
            for t in range(NT):
                last = dve.match_replace(RP[:, t, :], MX8[:, t, :], LG[:, t, :], -3e38)
            step(last)
            dve.tensor_tensor(EX, LG, MX8[:, :, 0:1].to_broadcast([P, NT, E1]), ALU.subtract).then_inc(R["shifted"], 1)
            step(dve.tensor_tensor(MK, LG, RP, ALU.not_equal))
            dve.sem_inc(R["mask_ready"], 1)
            dve.wait_ge(R["exp_ready"], 1)
            step(dve.tensor_tensor(EX, EX, MK, ALU.mult))
            step(dve.tensor_reduce(nrm[:, 0, 0:NT], EX, axis=AX.X, op=ALU.add))
            step(dve.reciprocal(nrm[:, 1, 0:NT], nrm[:, 0, 0:NT]))
            dve.tensor_tensor(EX, EX, nrm[:, 1, 0:NT].unsqueeze(2).to_broadcast([P, NT, E1]), ALU.mult).then_inc(R["route_ready"], 1)
            for c in range(NC):
                dve.wait_ge(R["maskT_psum"], c + 1)
                last = dve.tensor_tensor(SC[:, c * CH:(c + 1) * CH], bank[c % 2][0:E1, :], IOD[:, c * CH:(c + 1) * CH], ALU.mult)
                last.then_inc(R["score_ready"], 1)
            dve.wait_ge(R["score_ready"], NC)

            def round_indices(r):
                dve.wait_ge(R["slotT_psum"], r + 1)
                cols = slice(r * QPR, (r + 1) * QPR)
                step(dve.tensor_scalar(TOK[:, cols], bank[r % 2][:, 0:QPR], -1.0, float(T), ALU.mult, ALU.add))
                dve.tensor_scalar(IDX[:, cols], TOK[:, cols], float(T - 1), None, ALU.min).then_inc(R["idx_ready"], 1)

            for r in range(ROUNDS):
                step(dve.max(TK[:, 8 * r:8 * r + 8], SC))
                dve.tensor_tensor(AR[:, r % 2], TK[:, 8 * r:8 * r + 8].unsqueeze(1).to_broadcast([E1, EPT, 8]), expert_row[:],
                                  ALU.mult).then_inc(R["slots_ready"], 1)
                if r < ROUNDS - 1:
                    step(dve.match_replace(SC, TK[:, 8 * r:8 * r + 8], SC, 0.0))
                if r >= 1:
                    round_indices(r - 1)
            round_indices(ROUNDS - 1)
            for c in range(NC):
                if c == 2:
                    squares()
                dve.wait_ge(R["sh_silu"], c + 1)
                dve.tensor_tensor(SHH[:, c * CH:(c + 1) * CH], pair_bank[c % 2][0:F1, 1, :],
                                  HH[:, c % 2, :], ALU.mult).then_inc(R["sh_ready"], 1)
            for r in range(ROUNDS):
                dve.wait_ge(gathered[r], 16 * QPR)
            for q in range(QPR):
                last = dve.tensor_tensor(WSEL[:, :, q], GX[:, q:NJ:QPR, D + q * EPT:D + (q + 1) * EPT],
                                         row_expert[:].unsqueeze(1).to_broadcast([P, ROUNDS, EPT]), ALU.mult)
            last.then_inc(R["wsel_ready"], 1)
            dve.wait_ge(R["wT_psum"], 1)
            dve.tensor_copy(WT[:], bank[1][0:E1, 0:CAP]).then_inc(R["wT_ready"], 1)
            dve.wait_ge(R["ws_psum"], 1)
            step(dve.tensor_copy(WS[:], bank[1][:, CAP:CAP + NJ]))
            dve.sem_inc(R["ws_ready"], 1)
            for b in range(NJB):
                dve.wait_ge(R["y_psum"], b + 1)
                if b >= 2:
                    dve.wait_ge(y_stored[b % 2], 32 * (b // 2))
                dve.tensor_tensor(YW[:, b % 2], bank[2 + b % 2][:].rearrange("p (j n) -> p j n", n=D),
                                  WS[:, b * JB:(b + 1) * JB].unsqueeze(2).to_broadcast([P, JB, D]), ALU.mult).then_inc(R["y_weighted"], 1)
                if b == REFINE_AFTER:
                    dve.wait_ge(N1["qk_norm"], 1)
                    refine(2 * n1, 1e-8)
                if b == SCALE_AFTER:
                    scale_queries_keys()
                if b == RANKS_AFTER + 1:
                    find_slot_rows()
                if b in SPLIT_AFTER:
                    split_features(1, H, SPLIT_AFTER.index(b))
            dve.wait_ge(N1["g_psum"], 1)
            dve.tensor_copy(G32[:], bank[0][:, 0:H * VW])
            dve.tensor_scalar(GC[:], bank[1][0:1, 0:H * VW], -YAT_B, None, ALU.mult).then_inc(N1["g_ready"], 1)
            for c in range(NC):
                if c not in ACT_KEYS:
                    evacuate_kfeatures(1, H, c)
                if c + 2 < NC:
                    split_features(1, H, c + 2)
            for u in range(NU):
                dve.wait_ge(Y["distances"], u + 1)
                if u % UB == 0 and u // UB >= NPW:
                    dve.wait_ge(Y["sums"], UB * (u // UB - NPW + 1))
                dve.tensor_copy(UCOPY[:, u % 2, :], pair_bank[u % 2][:, 1, :]).then_inc(Y["copied"], 1)
                dve.wait_ge(Y["copied"], u + 1)
                dve.tensor_tensor(PW[:, (u // UB) % NPW, u % UB, :], pair_bank[u % 2][:, 0, :], UCOPY[:, u % 2, :],
                                  ALU.mult).then_inc(Y["product"], 1)
            for c in range(NC):
                ts = slice(c * TPC, (c + 1) * TPC)
                dve.wait_ge(Y["combined"], NU // MP - NC + c + 1)
                step(dve.tensor_scalar(DEN[:, ts], DEN[:, ts], 1e-6, None, ALU.add))
                step(dve.reciprocal(DEN[:, ts], DEN[:, ts]))
                dve.tensor_tensor(AO[:, ts, :].rearrange("p t (h n) -> p t h n", n=HD), NUM[:, ts],
                                  DEN[:, ts].unsqueeze(3).to_broadcast([P, TPC, H, HD]), ALU.mult).then_inc(L[1]["ao_ready"], 1)
            dve.wait_ge(R["z_silu"], 1)
            add_branches(1)

        @block.tensor
        def _(pe):
            def transpose_tiles(src, c, dst):
                for i in range(TPC):
                    last = pe.transpose(dst[:, i * P:(i + 1) * P], src[:, c * TPC + i, :], ident[:])
                return last

            def norm(l):
                for c in range(NC):
                    pe.wait_ge(L[l]["xn_ready"], c + 1)
                    if c >= 2:
                        pe.wait_ge(L[l]["xnT_ready"], c - 1)
                    transpose_tiles(XN, c, bank[c % 2]).then_inc(L[l]["xnT_psum"], 1)

            def project(l, w, b, n, tiles):
                pe.wait_ge(L[l]["xnT_ready"], NC)
                for t in tiles:
                    if t >= 2:
                        pe.wait_ge(L[l]["qkv_evac"], t - 1)
                    o = bank[t % 2] if l == 0 else pair_bank[t % 2][:, 0, :]
                    pe.matmul(o[:, 0:n], XNT[:, t * P:(t + 1) * P], w[:], start=True, stop=False)
                    pe.matmul(o[:, 0:n], first_row[:], b[:], start=False, stop=True).then_inc(L[l]["proj_psum"], 1)

            def features(l, nk, chunk):
                for t in range(chunk * TPC, (chunk + 1) * TPC):
                    pe.wait_ge(L[l]["dup_staged"], t // TPC + 2)
                    if l == 1:
                        pe.wait_ge(N1["dup_queries"], t // TPC + 1)
                    if t >= 2:
                        pe.wait_ge(L[l]["qfeat_evac"], t - 1)
                        pe.wait_ge(L[l]["kfeat_evac"], keys_by_vector(l, t - 1))
                    c = t // TPC
                    qd = pair_bank[t % 2][:, 0, :].bitcast(BF16)
                    kd = pair_bank[t % 2][:, 1, :].bitcast(BF16)
                    for a in range(H // 2):
                        pe.transpose(qd[:, a * P:(a + 1) * P], QF[:, c % 2, t % TPC, a * P:(a + 1) * P], identb[:])
                    for a in range(nk // 2):
                        last = pe.transpose(kd[:, a * P:(a + 1) * P], KF[:, c % 2, t % TPC, a * P:(a + 1) * P], identb[:])
                    last.then_inc(L[l]["featT_psum"], 1)

            pe.wait_ge(S["consts"], 1)
            norm(0)
            pe.wait_ge(weights_in[0], 16 * len(WEIGHTS[0]))
            pe.wait_ge(S["consts"], 2)
            pe.wait_ge(L[0]["xnT_ready"], NC)
            for t in range(NT):
                last = pe.matmul(bank[2][:, t * E0:(t + 1) * E0], XNT[:, t * P:(t + 1) * P], gate_w[:], start=True, stop=True)
            last.then_inc(F["gates_psum"], 1)
            project(0, wqkv0, bqkv0, D + 2 * KV0 * HD, range(NT))

            pe.wait_ge(L[0]["qkv_evac"], NT)
            pe.wait_ge(F["gates_ready"], 1)
            for c in range(NC):
                if c >= 2:
                    pe.wait_ge(F["gateT_ready"], c - 1)
                for i in range(TPC):
                    last = pe.transpose(bank[c % 2][0:E0, i * P:(i + 1) * P], gatew[:, c * TPC + i, :], ident[:])
                last.then_inc(F["gateT_psum"], 1)
            pe.wait_ge(F["gateT_ready"], NC)

            def hidden(c):
                for m in range(NM):
                    i = hidden_step(c, m)
                    if i >= 2:
                        pe.wait_ge(F["h_act"], i - 1)
                    rows = P if m < NM - 1 else F0
                    w = w1[:, m * P:(m + 1) * P] if m < NM - 1 else ws1[:]
                    pe.matmul(bank[i % 2][0:rows, :], w, XNT[:, c * CH:(c + 1) * CH], start=True, stop=True).then_inc(F["h_psum"], 1)
                    if m < NM - 1:
                        j = (NM - 1) * c + m
                        if j >= 2:
                            pe.wait_ge(F["h_gated"], j - 1)
                        pe.matmul(bank[2 + j % 2][:], gsel[:, m, :], gateT[:, c * CH:(c + 1) * CH], start=True, stop=True).then_inc(F["gsel_psum"], 1)

            def down(c):
                pe.wait_ge(F["h_gated"], (NM - 1) * (c + 1))
                pe.wait_ge(F["h_act"], hidden_step(c, NM - 1) + 1)
                s_ = down_step(c)
                pe.wait_ge(F["h_act"], s_ - 1)
                for i in range(TPC):
                    t = c * TPC + i
                    o = bank[s_ % 2][:, i * D:(i + 1) * D]
                    cols = slice(i * P, (i + 1) * P)
                    for m in range(NM - 1):
                        pe.matmul(o, HT(c, m)[:, cols], w2[:, m, :], start=m == 0, stop=False)
                    pe.matmul(o, HT(c, NM - 1)[0:F0, cols], ws2[:], start=False, stop=False)
                    pe.matmul(o, gateT[:, t * P:(t + 1) * P], b2[:], start=False, stop=False)
                    last = pe.matmul(o, first_row[:], bs2[:], start=False, stop=True)
                last.then_inc(F["h_psum"], 1)

            pe.wait_ge(weights_in[1], 16 * len(WEIGHTS[1]))
            for c in range(NC + 1):
                if c < NC:
                    hidden(c)
                if c >= 1:
                    down(c - 1)
                    features(0, KV0, c - 1)
            pe.wait_ge(F["h_act"], H_STEPS)
            pe.wait_ge(L[0]["qfeat_evac"], NT)
            pe.wait_ge(L[0]["kfeat_evac"], NT)

            pe.wait_ge(S["consts"], 3)

            def unit_scores(ks, hd):
                n, k = KSTEPS[ks]
                c, g = STEPS[n]
                u = HPG * ks + hd
                h = HPG * g + hd
                if hd == 0 and k == 0:
                    pe.wait_ge(M["m_rows_a"], n + 1)
                    pe.wait_ge(M["m_rows_b"], n + 1)
                if u >= 2:
                    pe.wait_ge(A["probs"], u - 1)
                out_ = pair_bank[u % 2][:].rearrange("p a b -> p (a b)")
                unit = causal_units(c)[k]
                for blk, at, w in unit:
                    q0 = (c + 1) * CH - w
                    diag = blk >= TPC * c
                    last = pe.matmul(out_[:, at:at + w], KFT[:, h % KV0, blk * P:(blk + 1) * P],
                                     QFT[:, h // 2, q0:q0 + w], start=True, stop=not diag)
                    if diag:
                        last = pe.matmul(out_[:, at:at + P], identb[:], mask_kq[:], start=False, stop=True)
                last.then_inc(A["scores"], 1)

            def unit_sums(ks, quarter):
                n, k = KSTEPS[ks]
                c, g = STEPS[n]
                unit = causal_units(c)[k]
                blocks = unit[0:1] if quarter < 2 else unit[1:]
                if quarter == 0:
                    pe.wait_ge(A["probs"], HPG * (ks + 1))
                    if k == 0 and n >= 1:
                        pe.wait_ge(A["sums_evac"], n)
                last_quarter = 3 if len(unit) > 1 else 1
                for blk, at, w in blocks:
                    lo, hi = (0, w // 2) if quarter % 2 == 0 else (w // 2, w)
                    for hd in range(HPG):
                        last = pe.matmul(bank[2][32 * hd:32 * hd + 32, CH - w + lo:CH - w + hi], VA[:, blk, hd * VW:hd * VW + 32],
                                         WORK[:, ks % 2, hd * 2 * CH + at + lo:hd * 2 * CH + at + hi],
                                         start=k == 0 and quarter == 0,
                                         stop=k == len(causal_units(c)) - 1 and quarter == last_quarter and blk == blocks[-1][0])
                if quarter == last_quarter:
                    last.then_inc(A["sums"], 1)

            def sums_transpose(n):
                pe.wait_ge(A["sums_evac"], n + 1)
                if n >= 1:
                    pe.wait_ge(L[0]["ao_ready"], n)
                k = min(n + 2, len(STEPS))
                pe.wait_ge(M["m_rows_a"], k)
                pe.wait_ge(M["m_rows_b"], k)
                for i in range(TPC):
                    last = pe.transpose(bank[3][:, i * P:(i + 1) * P], OT[:, n % 2, i * P:(i + 1) * P], ident[:])
                last.then_inc(A["sumsT"], 1)

            def max_scores(lo, hi):
                for u in range(lo, hi):
                    n, i = MAX_OF[u]
                    hd, qt, kc = MAXIMA[n][i]
                    c, g = STEPS[n]
                    if u >= 2:
                        pe.wait_ge(M["max_done"], u - 1)
                    h = HPG * g + hd
                    w = CH if kc < c else (qt + 1) * P
                    last = pe.matmul(bank[u % 2][:, 0:w], QFT[:, h // 2, c * CH + qt * P:c * CH + (qt + 1) * P],
                                     KFT[:, h % KV0, kc * CH:kc * CH + w], start=True, stop=kc < c)
                    if kc == c:
                        last = pe.matmul(bank[u % 2][:, w - P:w], identb[:], mask_qk[:], start=False, stop=True)
                    last.then_inc(M["max_scores"], 1)

            def max_transpose(n):
                pe.wait_ge(M["minus_max"], n + 1)
                if n >= 2:
                    pe.wait_ge(L[0]["ao_ready"], n - 1)
                dst = bank[3][:].bitcast(BF16).rearrange("p (a n) -> p a n", n=CH)
                for a in range(2):
                    for i in range(TPC):
                        last = pe.transpose(dst[:, a, i * P:(i + 1) * P], MF[:, i, a, :], identb[:])
                last.then_inc(M["mT_psum"], 1)

            max_scores(0, MAX_BASE[1])
            done = MAX_BASE[1]
            max_transpose(0)
            nsteps = len(STEPS)
            for ks, (n, k) in enumerate(KSTEPS):
                c, g = STEPS[n]
                nk = len(causal_units(c))
                more = n + 1 < nsteps
                for i, (what, part) in enumerate(PIECES):
                    if what == "logits":
                        unit_scores(ks, part)
                    elif ks >= 1:
                        unit_sums(ks - 1, part)
                    max_scores(done, MAX_PLAN[NPC * ks + i])
                    done = MAX_PLAN[NPC * ks + i]
                    if k == 1 and i == 0 and n >= 1:
                        sums_transpose(n - 1)
                    if more and k == nk - 1 and (what, part) == ("logits", 2):
                        max_transpose(n + 1)
            for quarter in range(2):
                unit_sums(len(KSTEPS) - 1, quarter)
            sums_transpose(nsteps - 1)

            def end_layer(l, w, b):
                for c in range(NC):
                    if l == 0:
                        pe.wait_ge(L[0]["ao_ready"], nsteps + 1 + c + 1)
                    else:
                        pe.wait_ge(L[1]["ao_ready"], c + 1)
                    if c >= 2:
                        pe.wait_ge(L[l]["lnT_ready"], c - 1)
                    transpose_tiles(AO, c, bank[c % 2]).then_inc(L[l]["lnT_psum"], 1)
                for t in range(NT):
                    c, i = divmod(t, TPC)
                    if i == 0:
                        pe.wait_ge(L[l]["lnT_ready"], c + 1)
                        if c >= 2:
                            pe.wait_ge(L[l]["y_used"], c - 1)
                    o = bank[2 + c % 2][:, i * D:(i + 1) * D]
                    pe.matmul(o, AOT[l][:, t * P:(t + 1) * P], w[:], start=True, stop=False)
                    last = pe.matmul(o, first_row[:], b[:], start=False, stop=True)
                    if i == TPC - 1:
                        last.then_inc(L[l]["y_psum"], 1)

            pe.wait_ge(weights_in[2], 16 * len(WEIGHTS[2]))
            end_layer(0, wo[0], bo[0])

            norm(1)
            pe.wait_ge(L[1]["xnT_ready"], NC)
            for t in range(NT):
                last = pe.matmul(bank[t // 8][:, (t % 8) * E1:(t % 8 + 1) * E1], XNT[:, t * P:(t + 1) * P], router[:], start=True, stop=True)
                if t % 8 == 7:
                    last.then_inc(R["logits_psum"], 1)
            project(1, wqkv1, bqkv1, 3 * D, range(EARLY_TILES))
            pe.wait_ge(R["logits_evac"], 2)
            pe.wait_ge(R["mask_ready"], 1)
            for c in range(NC):
                if c >= 2:
                    pe.wait_ge(R["score_ready"], c - 1)
                for i in range(TPC):
                    last = pe.transpose(bank[c % 2][0:E1, i * P:(i + 1) * P], MK[:, c * TPC + i, :], ident[:])
                last.then_inc(R["maskT_psum"], 1)
            def shared(c):
                if c < 2:
                    pe.wait_ge(L[1]["qkv_evac"], NT)
                else:
                    pe.wait_ge(R["sh_ready"], c - 1)
                for which in range(2):
                    last = pe.matmul(pair_bank[c % 2][0:F1, which, :], wsgu[:, which * F1:(which + 1) * F1],
                                     XNT[:, c * CH:(c + 1) * CH], start=True, stop=True)
                last.then_inc(R["sh_psum"], 1)

            pe.wait_ge(R["score_ready"], NC)
            for r in range(ROUNDS + 2):
                if r < ROUNDS:
                    pe.wait_ge(S["selectors"], 1)
                    pe.wait_ge(R["slots_ready"], r + 1)
                    if r >= 2:
                        pe.wait_ge(R["idx_ready"], r - 1)
                    pe.matmul(bank[r % 2][:, 0:QPR], AR[:, r % 2].rearrange("p a s -> p (a s)"), expert_tile[:],
                              start=True, stop=True).then_inc(R["slotT_psum"], 1)
                project(1, wqkv1, bqkv1, 3 * D, late_tiles(r))
                if r - LATE_ROUNDS in (0, 1):
                    shared(r - LATE_ROUNDS)
                b = r - 2
                if b >= 0:
                    pe.wait_ge(gathered[b], 16 * QPR)
                    if b >= 2:
                        pe.wait_ge(R["xbT_ready"], b - 1)
                    for i in range(JB):
                        last = pe.transpose(bank[2 + b % 2][:, i * P:(i + 1) * P], GX[:, b * JB + i, 0:D], ident[:])
                    last.then_inc(R["xbT_psum"], 1)
            shared(2)
            shared(3)
            pe.wait_ge(R["idx_ready"], ROUNDS)
            pe.wait_ge(R["wsel_ready"], 1)
            for r in range(ROUNDS):
                last = pe.matmul(bank[1][0:E1, 8 * r:8 * r + 8], WSEL[:, r].rearrange("p q a -> p (q a)"), row_slot[:], start=True, stop=True)
            last.then_inc(R["wT_psum"], 1)
            pe.wait_ge(R["wT_ready"], 1)
            for half in range(2):
                last = pe.matmul(bank[1][64 * half:64 * half + 64, CAP:CAP + NJ], WT[:], ident[0:E1, half * NJ:(half + 1) * NJ], start=True, stop=True)
            last.then_inc(R["ws_psum"], 1)

            def ranks():
                pe.wait_ge(R["ws_ready"], 1)
                pe.wait_ge(R["mask_copied"], 1)
                for half in range(2):
                    first, end = half * NT // 2, (half + 1) * NT // 2
                    pe.matmul(bank[half][:], upto[:], MKB[:, first:end].rearrange("p t e -> p (t e)"), start=True, stop=False)
                    for t in range(end - 1):
                        at = max(t + 1, first)
                        last = pe.matmul(bank[half][:, (at - first) * E1:], all_ones[:],
                                         MKB[:, t:t + 1].to_broadcast([P, end - at, E1]), start=False, stop=t == end - 2)
                    last.then_inc(R["rank_psum"], 1)

            def shared_out(c):
                pe.wait_ge(R["rows_ready"], 1)
                if c >= 2:
                    pe.wait_ge(R["shared_evac"], c - 1)
                for i in range(TPC):
                    t = c * TPC + i
                    last = pe.matmul(bank[c % 2][:, i * D:(i + 1) * D], SHH[:, t * P:(t + 1) * P], wsd[:], start=True, stop=True)
                last.then_inc(R["shared_psum"], 1)

            def linear_part():
                pe.wait_ge(N1["qk_scaled"], 2)
                pe.wait_ge(R["shared_evac"], NC)
                for t in range(NT):
                    pe.matmul(bank[0][:, 0:H * VW], K32[:, t, :], VA[:, t, 0:H * VW], start=t == 0, stop=t == NT - 1)
                for t in range(NT):
                    last = pe.matmul(bank[1][0:1, 0:H * VW], ones_col[:], VA[:, t, 0:H * VW], start=t == 0, stop=t == NT - 1)
                last.then_inc(N1["g_psum"], 1)

            xbt5 = XBT.rearrange("p (r q) (a s) -> p r q a s", r=ROUNDS, a=EPT)
            expert_rows = lambda e: xbt5[:, :, e // EPT, e % EPT, :]

            def gate_up(b):
                pe.wait_ge(R["xbT_ready"], NJB)
                pe.wait_ge(gu_in[b % len(wgu)], 64 * (b // len(wgu) + 1))
                if b >= 2:
                    pe.wait_ge(R["silu_ready"], b - 1)
                for which in range(2):
                    for i in range(JB):
                        for half in range(2):
                            last = pe.matmul(pair_bank[b % 2][0:F1, which, i * P + half * CAP:i * P + (half + 1) * CAP],
                                             wgu[b % len(wgu)][:, which, half, i, :],
                                             expert_rows(half * NJ + b * JB + i), start=True, stop=True)
                last.then_inc(R["gu_psum"], 1)

            def expert_down(b):
                pe.wait_ge(R["h_ready"], b + 1)
                pe.wait_ge(dn_in[b % len(wdn)], 32 * (b // len(wdn) + 1))
                if b >= 2:
                    pe.wait_ge(R["y_weighted"], b - 1)
                for i in range(JB):
                    for half in range(2):
                        last = pe.matmul(bank[2 + b % 2][64 * half:64 * half + 64, i * D:(i + 1) * D],
                                         HH[:, 2 + b % 2, i * P + half * CAP:i * P + (half + 1) * CAP],
                                         wdn[b % len(wdn)][:, half, i, :], start=True, stop=True)
                last.then_inc(R["y_psum"], 1)

            pe.wait_ge(R["sh_ready"], NC)
            gate_up(0)
            for b in range(NJB):
                if b + 1 < NJB:
                    gate_up(b + 1)
                expert_down(b)
                if b == RANKS_AFTER:
                    ranks()
                if b in SHARED_AFTER:
                    shared_out(2 * SHARED_AFTER.index(b))
                    shared_out(2 * SHARED_AFTER.index(b) + 1)
                if b == LINEAR_AFTER:
                    linear_part()
            for c in range(NC):
                features(1, H, c)
            pe.wait_ge(L[1]["qfeat_evac"], NT)
            pe.wait_ge(L[1]["kfeat_evac"], keys_by_vector(1, NT))

            def distances(u):
                i, m = divmod(u, MP)
                h, c = divmod(i, NC)
                r = 64 * (h % 2)
                if u >= 2:
                    pe.wait_ge(Y["product"], u - 1)
                for b in range(2):
                    blk = 2 * m + b
                    last = pe.matmul(pair_bank[u % 2][:, b, :], KFT[r:r + 64, h // 2, blk * P:(blk + 1) * P],
                                     QFT[r:r + 64, h // 2, c * CH:(c + 1) * CH], start=True, stop=True)
                last.then_inc(Y["distances"], 1)

            def pair_sums(u):
                i, m = divmod(u, MP)
                h, c = divmod(i, NC)
                if u % UB == 0:
                    pe.wait_ge(Y["inverse"], u // UB + 1)
                if m == 0:
                    pe.wait_ge(Y["matrices"], h + 1)
                    if i >= 2:
                        pe.wait_ge(Y["sums_evac"], i - 1)
                last = pe.matmul(bank[i % 2][0:V2, :], MM[:, h % 2, m, :], PW[:, (u // UB) % NPW, u % UB, :],
                                 start=m == 0, stop=m == MP - 1)
                last.then_inc(Y["sums"], 1)

            def pair_sums_transpose(i):
                pe.wait_ge(Y["sums_evac"], i + 1)
                if i >= 2:
                    pe.wait_ge(Y["sumsT_evac"], i - 1)
                for q in range(TPC):
                    last = pe.transpose(bank[2 + i % 2][:, q * V2:(q + 1) * V2], TS[:, i % 2, q * P:(q + 1) * P], ident[0:V2, 0:V2])
                last.then_inc(Y["sumsT"], 1)

            LAG = 2 * UB
            for u in range(NU + LAG):
                if u < NU:
                    distances(u)
                if u >= LAG:
                    pair_sums(u - LAG)
                    if (u - LAG) % MP == 6 and u - LAG >= MP:
                        pair_sums_transpose((u - LAG) // MP - 1)
            pair_sums_transpose(NU // MP - 1)
            end_layer(1, wo[1], bo[1])


def kernel(**inputs):
    import concourse.bacc as bacc
    from concourse.bass_utils import run_bass_kernel_spmd

    a = {k: np.asarray(v) for k, v in inputs.items()}
    row = lambda n: a[n].reshape(1, -1)
    col = lambda n: a[n].reshape(-1, 1)
    laid = {
        "x": a["L0_attn_x"].reshape(T, D),
        "Wq0": a["L0_attn_Wq"], "bq0": row("L0_attn_bq"), "Wk0": a["L0_attn_Wk"], "bk0": row("L0_attn_bk"),
        "Wv0": a["L0_attn_Wv"], "bv0": row("L0_attn_bv"), "ln_g": col("L0_attn_ln_g"), "ln_b": col("L0_attn_ln_b"),
        "Wo0": a["L0_attn_Wo"], "bo0": row("L0_attn_bo"),
        "gate_W": a["L0_ffn_gate_W"],
        "W1": a["L0_ffn_W1"].transpose(1, 0, 2).reshape(D, E0 * F0),
        "b1": a["L0_ffn_b1"].reshape(E0 // 2, P).T,
        "W2": a["L0_ffn_W2"].reshape(E0 // 2, P, D).transpose(1, 0, 2).reshape(P, E0 // 2 * D),
        "b2": a["L0_ffn_b2"],
        "Ws1": a["L0_ffn_Ws1"], "bs1": col("L0_ffn_bs1"), "Ws2": a["L0_ffn_Ws2"], "bs2": row("L0_ffn_bs2"),
        "route_scale": a["L0_ffn_route_scale"].reshape(1, 1),
        "Wq1": a["L1_attn_Wq"], "bq1": row("L1_attn_bq"), "Wk1": a["L1_attn_Wk"], "bk1": row("L1_attn_bk"),
        "Wv1": a["L1_attn_Wv"], "bv1": row("L1_attn_bv"), "Wo1": a["L1_attn_Wo"], "bo1": row("L1_attn_bo"),
        "router": a["L1_ffn_router_w"].T,
        "w_gate": a["L1_ffn_w_gate"].transpose(1, 0, 2).reshape(D, E1 * F1),
        "w_up": a["L1_ffn_w_up"].transpose(1, 0, 2).reshape(D, E1 * F1),
        "w_down": a["L1_ffn_w_down"].transpose(1, 0, 2).reshape(F1, E1 * D),
        "ws_gate_up": a["L1_ffn_ws_gate_up"], "ws_down": a["L1_ffn_ws_down"],
    }
    nc = bacc.Bacc("TRN2", target_bir_lowering=False, num_devices=1)
    arrays, ins = {}, {}
    for name, shape in IN_SHAPES.items():
        arrays[f"in_{name}"] = np.ascontiguousarray(laid[name])
        assert arrays[f"in_{name}"].shape == shape, name
        ins[name] = nc.dram_tensor(f"in_{name}", shape, FP32, kind="ExternalInput").ap()
    out = nc.dram_tensor("out", (T, D), FP32, kind="ExternalOutput").ap()
    scratch = nc.dram_tensor("token_rows", (T, D + E1), FP32, kind="Internal").ap()
    lin = nc.dram_tensor("linear_part", (H, V2), FP32, kind="Internal").ap()
    slot_out = nc.dram_tensor("slot_outputs", (1 + E1 * CAP, D), FP32, kind="Internal").ap()
    two_layers(nc, ins, out, scratch, lin, slot_out)
    r = run_bass_kernel_spmd(nc, [arrays], core_ids=[0])
    return r.results[0]["out"].reshape(1, T, D)
```
